# Optimizing a Trainium2 kernel written in Bass

```python
import numpy as np
import jax
import jax.numpy as jnp

def _softmax(x, axis=-1):
    return jax.nn.softmax(x, axis=axis)

def _gelu(x):
    return jax.nn.gelu(x, approximate=True)

def _silu(x):
    return jax.nn.silu(x)

def _sigmoid(x):
    return jax.nn.sigmoid(x)

def _layernorm(x, axis=-1, eps=1e-05):
    m = jnp.mean(x, axis=axis, keepdims=True)
    v = jnp.var(x, axis=axis, keepdims=True)
    return (x - m) / jnp.sqrt(v + eps)

def _scatter_add(tgt, idx, src, axis=0):
    return tgt.at[idx].add(src)

def _segment_sum(src, seg, n):
    return jax.ops.segment_sum(src, seg, n)
kernel_name = 'mk_xattn_ffn_d2_seqx_r4_0dec0f'

def setup_inputs(seed: int=0):
    np.random.seed(seed)
    _w = jnp.asarray

    def _rec_inputs():
        import jax
        import jax.numpy as jnp
        _rk = jax.random.key(seed)
        x = 7.22e-05 + 1 * jax.random.normal(jax.random.fold_in(_rk, 1), (4, 512, 512), jnp.float32)
        _lenS = 512 - jax.random.randint(jax.random.fold_in(_rk, 7), (4,), 0, max(1, 512 // 4) + 1, jnp.int32)
        _lenS2 = 512 - jax.random.randint(jax.random.fold_in(_rk, 8), (4,), 0, max(1, 512 // 4) + 1, jnp.int32)
        _ctx_1024P = jax.random.normal(jax.random.fold_in(_rk, 11), (4, 16, 256), jnp.float32)
        _ctx_1024c = jax.random.dirichlet(jax.random.fold_in(_rk, 511), 0.3 * jnp.ones((16,), jnp.float32), (4, 512))
        _ctx_1024t = jnp.einsum('bsk,bkd->bsd', _ctx_1024c, _ctx_1024P)
        _ctx_1024t = _ctx_1024t * jax.lax.rsqrt(jnp.mean(jnp.square(_ctx_1024t)) + 1e-12) * 0.953939
        ctx_1024 = 2.81802e-05 + 1.00001 * (_ctx_1024t + 0.3 * jax.random.normal(jax.random.fold_in(_rk, 611), (4, 512, 256), jnp.float32))
        return (x, ctx_1024)
    x, ctx_1024 = _rec_inputs()

    def _L0_xattn_setup():
        import jax, jax.numpy as jnp
        import numpy as np
        key = jax.random.key(seed)
        ks = jax.random.split(key, 6)
        B, L, N, C, D = (8, 128, 512, 256, 128)
        return {'teacher_logits': jax.random.normal(ks[0], (B, L, N), dtype=jnp.float32), 'teacher_features': jax.random.normal(ks[1], (B, N, C), dtype=jnp.float32), 'Wq': jax.random.normal(ks[2], (D, C), dtype=jnp.float32) * (1.0 / np.sqrt(C)), 'bq': jnp.zeros((D,), dtype=jnp.float32), 'Wk': jax.random.normal(ks[3], (D, C), dtype=jnp.float32) * (1.0 / np.sqrt(C)), 'bk': jnp.zeros((D,), dtype=jnp.float32)}
    _L0_xattn_all = _L0_xattn_setup()
    _L0_xattn_in = {k: v for k, v in _L0_xattn_all.items() if k in ('Wq', 'bq', 'Wk', 'bk')}
    del _L0_xattn_all

    def _L0_ffn_setup():
        import jax, jax.numpy as jnp
        import numpy as np
        B, T, D, F, E, K = (2, 256, 512, 192, 16, 2)
        key = jax.random.key(seed)
        k0, k1, k2, k3, k4 = jax.random.split(key, 5)
        scale = 0.02
        return {'x': jax.random.normal(k0, (B, T, D), dtype=jnp.float32), 'router_w': jax.random.normal(k1, (D, E), dtype=jnp.float32) * scale, 'gate_w': jax.random.normal(k2, (E, D, F), dtype=jnp.float32) * scale, 'up_w': jax.random.normal(k3, (E, D, F), dtype=jnp.float32) * scale, 'down_w': jax.random.normal(k4, (E, F, D), dtype=jnp.float32) * scale}
    _L0_ffn_all = _L0_ffn_setup()
    _L0_ffn_in = {k: v for k, v in _L0_ffn_all.items() if k in ('router_w', 'gate_w', 'up_w', 'down_w')}
    del _L0_ffn_all

    def _L1_xattn_setup():
        import jax, jax.numpy as jnp
        import numpy as np
        B_, L_, D_MODEL = (4, 512, 256)
        D_STATE, D_CONV, EXPAND = (16, 4, 2)
        D_INNER = EXPAND * D_MODEL
        DT_RANK = (D_MODEL + 15) // 16

        def silu(x):
            return x * jax.nn.sigmoid(x)
        key = jax.random.key(seed)
        ks = jax.random.split(key, 10)
        f32 = jnp.float32
        hidden_states = jax.random.normal(ks[0], (B_, L_, D_MODEL), dtype=f32)
        z = jax.random.normal(ks[1], (B_, D_INNER, L_), dtype=f32)
        in_proj_w = jax.random.normal(ks[2], (D_INNER, D_MODEL), dtype=f32) * 0.02
        conv_w = jax.random.normal(ks[3], (D_INNER, 1, D_CONV), dtype=f32) * 0.1
        conv_b = jax.random.normal(ks[4], (D_INNER,), dtype=f32) * 0.02
        x_proj_w = jax.random.normal(ks[5], (DT_RANK + 2 * D_STATE, D_INNER), dtype=f32) * 0.02
        dt_proj_w = jax.random.uniform(ks[6], (D_INNER, DT_RANK), dtype=f32, minval=-DT_RANK ** (-0.5), maxval=DT_RANK ** (-0.5))
        dt = jnp.exp(jax.random.uniform(ks[7], (D_INNER,), dtype=f32, minval=np.log(0.001), maxval=np.log(0.1)))
        dt_proj_b = jnp.log(jnp.expm1(dt))
        A_log = jnp.log(jnp.broadcast_to(jnp.arange(1, D_STATE + 1, dtype=f32), (D_INNER, D_STATE)))
        D = jnp.ones((D_INNER,), f32)
        return {'hidden_states': hidden_states, 'z': z, 'in_proj_w': in_proj_w, 'conv_w': conv_w, 'conv_b': conv_b, 'x_proj_w': x_proj_w, 'dt_proj_w': dt_proj_w, 'dt_proj_b': dt_proj_b, 'A_log': A_log, 'D': D}
    _L1_xattn_all = _L1_xattn_setup()
    _L1_xattn_in = {k: v for k, v in _L1_xattn_all.items() if k in ('in_proj_w', 'conv_w', 'conv_b', 'x_proj_w', 'dt_proj_w', 'dt_proj_b', 'A_log', 'D')}
    del _L1_xattn_all

    def _L1_ffn_setup():
        import jax, jax.numpy as jnp
        import numpy as np
        B, S, D = (2, 1024, 512)
        E, DFF = (8, 2048)
        TOP_K = 2
        key = jax.random.key(seed)
        ks = jax.random.split(key, 4)
        scale_in = 1.0 / np.sqrt(D)
        scale_ff = 1.0 / np.sqrt(DFF)
        return {'hidden_states': jax.random.normal(ks[0], (B, S, D), dtype=jnp.float32), 'gate_w': jax.random.normal(ks[1], (E, D), dtype=jnp.float32) * scale_in, 'w1': jax.random.normal(ks[2], (E, D, DFF), dtype=jnp.float32) * scale_in, 'b1': jnp.zeros((E, DFF), dtype=jnp.float32), 'w2': jax.random.normal(ks[3], (E, DFF, D), dtype=jnp.float32) * scale_ff, 'b2': jnp.zeros((E, D), dtype=jnp.float32)}
    _L1_ffn_all = _L1_ffn_setup()
    _L1_ffn_in = {k: v for k, v in _L1_ffn_all.items() if k in ('gate_w', 'w1', 'b1', 'w2', 'b2')}
    del _L1_ffn_all
    return {'x': x, 'ctx_1024': ctx_1024, 'L0_xattn_Wq': _L0_xattn_in['Wq'], 'L0_xattn_bq': _L0_xattn_in['bq'], 'L0_xattn_Wk': _L0_xattn_in['Wk'], 'L0_xattn_bk': _L0_xattn_in['bk'], 'L0_ffn_router_w': _L0_ffn_in['router_w'], 'L0_ffn_gate_w': _L0_ffn_in['gate_w'], 'L0_ffn_up_w': _L0_ffn_in['up_w'], 'L0_ffn_down_w': _L0_ffn_in['down_w'], 'L1_xattn_in_proj_w': _L1_xattn_in['in_proj_w'], 'L1_xattn_conv_w': _L1_xattn_in['conv_w'], 'L1_xattn_conv_b': _L1_xattn_in['conv_b'], 'L1_xattn_x_proj_w': _L1_xattn_in['x_proj_w'], 'L1_xattn_dt_proj_w': _L1_xattn_in['dt_proj_w'], 'L1_xattn_dt_proj_b': _L1_xattn_in['dt_proj_b'], 'L1_xattn_A_log': _L1_xattn_in['A_log'], 'L1_xattn_D': _L1_xattn_in['D'], 'L1_ffn_gate_w': _L1_ffn_in['gate_w'], 'L1_ffn_w1': _L1_ffn_in['w1'], 'L1_ffn_b1': _L1_ffn_in['b1'], 'L1_ffn_w2': _L1_ffn_in['w2'], 'L1_ffn_b2': _L1_ffn_in['b2']}

def reference(x, ctx_1024, L0_xattn_Wq, L0_xattn_bq, L0_xattn_Wk, L0_xattn_bk, L0_ffn_router_w, L0_ffn_gate_w, L0_ffn_up_w, L0_ffn_down_w, L1_xattn_in_proj_w, L1_xattn_conv_w, L1_xattn_conv_b, L1_xattn_x_proj_w, L1_xattn_dt_proj_w, L1_xattn_dt_proj_b, L1_xattn_A_log, L1_xattn_D, L1_ffn_gate_w, L1_ffn_w1, L1_ffn_b1, L1_ffn_w2, L1_ffn_b2):
    import jax
    import jax.numpy as jnp

    def _L0_xattn_ref(teacher_logits, teacher_features, Wq, bq, Wk, bk):
        import jax, jax.numpy as jnp
        import numpy as np
        query = jnp.einsum('bnc,dc->bnd', teacher_features, Wq) + bq
        key = jnp.einsum('bnc,dc->bnd', teacher_features, Wk) + bk
        energy = jnp.einsum('bnd,bmd->bnm', query, key)
        attention = jax.nn.softmax(energy, axis=-1)
        x_m = jnp.einsum('bln,bmn->blm', teacher_logits, attention)
        return x_m

    def _L0_ffn_ref(x, router_w, gate_w, up_w, down_w):
        import jax, jax.numpy as jnp
        import numpy as np
        B, T, D, F, E, K = (2, 256, 512, 192, 16, 2)
        scores = jnp.einsum('btd,de->bte', x, router_w).astype(jnp.float32)
        probs = jax.nn.softmax(scores, axis=-1)
        routing_weights, routing_idx = jax.lax.top_k(probs, K)
        routing_weights = routing_weights / jnp.sum(routing_weights, axis=-1, keepdims=True)
        routing_weights = routing_weights.astype(x.dtype)
        one_hot = jax.nn.one_hot(routing_idx, E, dtype=x.dtype)
        combine = jnp.einsum('btk,btke->bte', routing_weights, one_hot)
        g = jnp.einsum('btd,edf->ebtf', x, gate_w)
        u = jnp.einsum('btd,edf->ebtf', x, up_w)
        h = jax.nn.silu(g) * u
        expert_out = jnp.einsum('ebtf,efd->ebtd', h, down_w)
        out = jnp.einsum('ebtd,bte->btd', expert_out, combine)
        return out

    def _L1_xattn_ref(hidden_states, z, in_proj_w, conv_w, conv_b, x_proj_w, dt_proj_w, dt_proj_b, A_log, D):
        import jax, jax.numpy as jnp
        import numpy as np
        B_, L_, D_MODEL = (4, 512, 256)
        D_STATE, D_CONV, EXPAND = (16, 4, 2)
        D_INNER = EXPAND * D_MODEL
        DT_RANK = (D_MODEL + 15) // 16

        def silu(x):
            return x * jax.nn.sigmoid(x)
        Bsz, L, _ = hidden_states.shape
        d_inner, _, d_conv = conv_w.shape
        dt_rank = dt_proj_w.shape[1]
        d_state = A_log.shape[1]
        x = jnp.einsum('bld,ed->bel', hidden_states, in_proj_w)
        xc = jax.lax.conv_general_dilated(x, conv_w, window_strides=(1,), padding=[(d_conv - 1, 0)], feature_group_count=d_inner, dimension_numbers=('NCH', 'OIH', 'NCH'))
        x = silu(xc + conv_b[None, :, None])
        x_dbl = jnp.einsum('bdl,ed->bel', x, x_proj_w)
        dt_low, Bm, Cm = jnp.split(x_dbl, [dt_rank, dt_rank + d_state], axis=1)
        dt = jnp.einsum('brl,dr->bdl', dt_low, dt_proj_w)
        dt = jax.nn.softplus(dt + dt_proj_b[None, :, None])
        A = -jnp.exp(A_log)
        dt_t = jnp.moveaxis(dt, -1, 0)
        B_t = jnp.moveaxis(Bm, -1, 0)
        C_t = jnp.moveaxis(Cm, -1, 0)
        u_t = jnp.moveaxis(x, -1, 0)

        def step(state, inp):
            d, b, c, u = inp
            dA = jnp.exp(d[..., None] * A)
            state = state * dA + (d * u)[..., None] * b[:, None, :]
            y = jnp.einsum('bdn,bn->bd', state, c)
            return (state, y)
        state0 = jnp.zeros((Bsz, d_inner, d_state), x.dtype)
        _, ys = jax.lax.scan(step, state0, (dt_t, B_t, C_t, u_t))
        y = jnp.moveaxis(ys, 0, 2)
        y = y + D[None, :, None] * x
        y = y * silu(z)
        return jnp.swapaxes(y, 1, 2)

    def _L1_ffn_ref(hidden_states, gate_w, w1, b1, w2, b2):
        import jax, jax.numpy as jnp
        import numpy as np
        B, S, D = (2, 1024, 512)
        E, DFF = (8, 2048)
        TOP_K = 2
        b, s, d = hidden_states.shape
        x = hidden_states.reshape(-1, d)
        router_logits = x @ gate_w.T
        _, sel = jax.lax.top_k(router_logits.sum(axis=0), TOP_K)
        rw = jax.nn.softmax(router_logits[:, sel].astype(jnp.float32), axis=1)
        rw = rw.astype(x.dtype)
        w1s, b1s = (w1[sel], b1[sel])
        w2s, b2s = (w2[sel], b2[sel])
        h = jax.nn.gelu(jnp.einsum('nd,kdf->knf', x, w1s) + b1s[:, None, :])
        y = jnp.einsum('knf,kfd->knd', h, w2s) + b2s[:, None, :]
        out = jnp.einsum('nk,knd->nd', rw, y)
        return out.reshape(b, s, -1)
    x = x + _L0_xattn_ref(_layernorm(x, axis=-1), ctx_1024, L0_xattn_Wq, L0_xattn_bq, L0_xattn_Wk, L0_xattn_bk)
    x = x + _L0_ffn_ref(_layernorm(x, axis=-1), L0_ffn_router_w, L0_ffn_gate_w, L0_ffn_up_w, L0_ffn_down_w)
    x = x + _L1_xattn_ref(ctx_1024, _layernorm(x, axis=-1), L1_xattn_in_proj_w, L1_xattn_conv_w, L1_xattn_conv_b, L1_xattn_x_proj_w, L1_xattn_dt_proj_w, L1_xattn_dt_proj_b, L1_xattn_A_log, L1_xattn_D)
    x = x + _L1_ffn_ref(_layernorm(x, axis=-1), L1_ffn_gate_w, L1_ffn_w1, L1_ffn_b1, L1_ffn_w2, L1_ffn_b2)
    return x

_drawn_inputs = setup_inputs


def setup_inputs(seed=0):
    import zlib

    import numpy as np

    out = dict(_drawn_inputs(seed))
    spreads = {'L0_xattn_bq': (0.0, 0.1),
     'L0_xattn_bk': (0.0, 2.0),
     'L1_xattn_D': (1.0, 0.6),
     'L1_ffn_b1': (0.0, 0.408),
     'L1_ffn_b2': (0.0, 0.279)}
    factors = {'L0_ffn_router_w': 3.497,
     'L0_ffn_gate_w': 3.325,
     'L0_ffn_up_w': 3.277,
     'L0_ffn_down_w': 3.269,
     'L1_xattn_in_proj_w': 3.667,
     'L1_xattn_conv_w': 3.742,
     'L1_xattn_conv_b': 8.0,
     'L1_xattn_x_proj_w': 8.0,
     'L1_xattn_dt_proj_w': 8.0,
     'L1_xattn_dt_proj_b': 8.0,
     'L1_xattn_A_log': 8.0}
    for name, (base, spread) in spreads.items():
        noise = np.random.default_rng([zlib.crc32(name.encode()), seed]).standard_normal(out[name].shape)
        drawn = base * np.exp(spread * noise) if base else spread * noise
        out[name] = jnp.asarray(drawn.astype(out[name].dtype))
    for name, factor in factors.items():
        out[name] = (out[name] * factor).astype(out[name].dtype)
    return out
```

```python
from contextlib import ExitStack, contextmanager

import concourse.bass as bass
from concourse import mybir

ALU = mybir.AluOpType
ACT = mybir.ActivationFunctionType
AX = mybir.AxisListType.X
F32 = mybir.dt.float32
F32R = mybir.dt.float32r
I32 = mybir.dt.int32
U32 = mybir.dt.uint32
ds = bass.ds

P = 128
EPS = 1e-5
TOP = 2
DMA = 16
A_RING = 2
S_RING = 4
BC_RING = 4
GROUP = 4
AHEAD = 2
WQ = 4


class Steps:

    def __init__(self, eng, sem):
        self.eng, self.sem, self.n, self.base = eng, sem, 0, 0

    def mark(self, ins):
        ins.then_inc(self.sem, 1)
        self.n += 1

    def wait(self, apart=None):
        if apart:
            apart(self.eng, self.sem, self.base + self.n)
        else:
            self.eng.wait_ge(self.sem, self.base + self.n)

    @contextmanager
    def loop(self, trips, per):
        before = self.n
        with self.eng.Fori(0, trips) as i:
            self.base = i * per
            yield i
        assert self.n - before == per, f"{self.n - before} steps in the body, not {per}"
        self.base, self.n = 0, before + trips * per


def build_program(nc, x, ctx, Wq, bq, Wk, bk, router_w, gate_w, up_w, down_w, in_w, conv_w, conv_b,
                  xp_w, dtp_w, dtp_b, A_log, D_skip, gate2_w, w1, b1, w2, b2, out):
    B, L, DM = x.shape
    C = ctx.shape[2]
    CK = C // P
    T = L // P
    NT = B * T
    K = DM // P
    E, _, F = gate_w.shape
    FH = F // 2
    NS = A_log.shape[1]
    DI = in_w.shape[0]
    DC = DI // P
    R = dtp_w.shape[1]
    TAPS = conv_w.shape[2]
    XD = R + 2 * NS
    E2, _, FF = w1.shape
    FT = FF // P
    SLOT_TILES = B * L * TOP // P + E
    SLOTS = SLOT_TILES * P
    assert DI == DM == L and SLOT_TILES == (B - 1) * NS and F == 2 * FH and TAPS == 4 and E == NS

    def dram(name, shape):
        return nc.dram_tensor(name, shape, F32, kind="Internal").ap()

    u_dram = dram("u_spill", [B, P, DC * L])
    bc_dram = dram("bc_rows", [B, 2 * NS, L])
    x1_dram = dram("x1_spill", [NT, P, DM])
    xn_dram = dram("xn_rows", [B * L, DM])
    y_dram = dram("expert_rows", [SLOTS, DM])
    slot_dram = dram("slot_tokens", [SLOTS, 1])
    x3_dram = dram("x3_spill", [NT, P, DM])
    xt_dram = dram("xt_spill", [B, P, K * L])

    top = ExitStack()
    with top:
        def sem(name):
            return top.enter_context(nc.semaphore(name))

        def sb(stack, name, shape, dt=F32):
            return stack.enter_context(nc.sbuf_tensor(name, shape, dt))

        PS = [top.enter_context(nc.psum_tensor(f"bank{i}", [P, 512], F32)) for i in range(8)]


        ident = sb(top, "ident", [P, P])
        ones = sb(top, "ones", [P, P])
        gate2T = sb(top, "gate2T", [P, K, E2])
        minus_half = sb(top, "minus_half", [P, T])
        stats = sb(top, "stats", [P, T, 6])
        mv = sb(top, "mv", [P, T, 2])
        vare = sb(top, "vare", [P, T])
        rstd = sb(top, "rstd", [P, T])
        iota_e = sb(top, "iota_e", [P, E])
        logits = sb(top, "logits", [P, NT, E2])
        rwf = sb(top, "rwf", [P, TOP, NT])
        lidx = sb(top, "lidx", [P, 8], U32)

        a = ExitStack()
        DT = sb(a, "DT", [P, B, DC, L])
        DTU = sb(a, "DTU", [P, B, DC, L])
        ctxT = sb(a, "ctxT", [P, CK, B * L])
        U = sb(a, "U", [P, DC, L])
        wqkT = sb(a, "wqkT", [P, 2, CK, P])
        routerW = sb(a, "routerW", [P, K, E])
        qkb = sb(a, "qkb", [P, 2])
        convW = sb(a, "convW", [P, DC, TAPS])
        convB = sb(a, "convB", [P, DC])
        halfW = sb(a, "halfW", [P, DC, TAPS])
        halfB = sb(a, "halfB", [P, DC])
        dtB = sb(a, "dtB", [P, DC])
        skip = sb(a, "skip", [P, DC])
        negA = sb(a, "negA", [P, DC, NS])
        SC = sb(a, "SC", [P, NT, E])
        rwt = sb(a, "rwt", [P, TOP, NT])
        pos = sb(a, "pos", [P, TOP, NT], I32)
        slot_tok = sb(a, "slot_tok", [P, SLOT_TILES], I32)
        tile_exp = sb(a, "tile_exp", [P, SLOT_TILES], I32)
        pcol = [sb(a, f"pcol{i}", [P, 1], I32) for i in range(2 * TOP)]

        s = ExitStack()
        nat_qk = sb(s, "nat_qk", [P, 2, C])
        nat_in = sb(s, "nat_in", [P, DC, C])
        nat_xp = sb(s, "nat_xp", [XD, DI])
        nat_dtp = sb(s, "nat_dtp", [P, DC, R])
        nat_g2 = sb(s, "nat_g2", [E2, DM])
        nat_A = sb(s, "nat_A", [P, DC, NS])
        nat_ctx = sb(s, "nat_ctx", [P, NT, C])
        zslots = sb(s, "zslots", [SLOT_TILES, P])
        XP = sb(s, "XP", [P, DC, L + TAPS - 1])
        XH = sb(s, "XH", [P, DC, L])
        TH = sb(s, "TH", [P, DC, L])
        ZZ = sb(s, "ZZ", [P, DC, L])
        WW = sb(s, "WW", [P, DC, L])
        ND = sb(s, "ND", [P, DC, L])
        RL = sb(s, "RL", [P, DC, L])
        xdb = sb(s, "xdb", [XD, L])
        inT = sb(s, "inT", [P, CK, DI])
        xpT = sb(s, "xpT", [P, DC, XD])
        dtpT = sb(s, "dtpT", [R, DI])
        s.close()

        m = ExitStack()
        dA = [sb(m, f"dA{i}", [P, DC, L]) for i in range(A_RING)]
        S = [sb(m, f"S{i}", [P, DC, L]) for i in range(S_RING)]
        Bb = [sb(m, f"Bb{i}", [P, L]) for i in range(BC_RING)]
        Cb = [sb(m, f"Cb{i}", [P, L]) for i in range(BC_RING)]

        q = ExitStack()
        XB = sb(q, "XB", [P, T, DM])
        XN = sb(q, "XN", [P, T, DM])
        XNT = sb(q, "XNT", [P, K, L])
        ATT = sb(q, "ATT", [P, K, L])
        PR = sb(q, "PR", [P, T, L])
        QKT = sb(q, "QKT", [P, 2, L])
        nmax = sb(q, "nmax", [P, T])
        nneg = sb(q, "nneg", [P, T])
        rsum = sb(q, "rsum", [P, T])
        rinv = sb(q, "rinv", [P, T])
        q.close()

        r = ExitStack()
        tri = sb(r, "tri", [P, P])
        M8 = sb(r, "M8", [P, NT, 8])
        I8 = sb(r, "I8", [P, NT, 8], U32)
        IF = sb(r, "IF", [P, TOP, NT])
        OH = sb(r, "OH", [P, TOP, NT, E])
        MM = sb(r, "MM", [P, NT, E])
        PX = sb(r, "PX", [P, NT + 1, E])
        PO = sb(r, "PO", [P, NT, E])
        PSEL = sb(r, "PSEL", [P, TOP, NT, E])
        posf = sb(r, "posf", [P, TOP, NT])
        cnt = sb(r, "cnt", [P, E])
        cnti = sb(r, "cnti", [P, E], I32)
        tiles = sb(r, "tiles", [P, E])
        incl = sb(r, "incl", [P, E])
        off = sb(r, "off", [P, E])
        iota_j = sb(r, "iota_j", [P, SLOT_TILES])
        cmpj = sb(r, "cmpj", [P, SLOT_TILES, E])
        texf = sb(r, "texf", [P, SLOT_TILES])
        tokid = sb(r, "tokid", [P, NT])
        diff = sb(r, "diff", [P, NT])
        ex = sb(r, "ex", [P, NT])
        den = sb(r, "den", [P, NT])
        slotf = sb(r, "slotf", [SLOT_TILES, P])
        r.close()

        f = ExitStack()
        WGU = [sb(f, f"WGU{i}", [P, K, 2, F]) for i in range(2)]
        WD = [sb(f, f"WD{i}", [FH, 2, DM]) for i in range(2)]
        XG = [sb(f, f"XG{i}", [P, DM]) for i in range(2)]
        XGT = [sb(f, f"XGT{i}", [P, K, P]) for i in range(2)]
        gcol = [sb(f, f"gcol{i}", [P, 1], I32) for i in range(2)]
        TG = [sb(f, f"TG{i}", [P, F]) for i in range(2)]
        GG = [sb(f, f"GG{i}", [P, F]) for i in range(2)]
        HH = [sb(f, f"HH{i}", [P, F]) for i in range(2)]
        HT = [sb(f, f"HT{i}", [FH, 2, P]) for i in range(2)]
        YT = [sb(f, f"YT{i}", [P, DM]) for i in range(2)]
        f.close()
        m.close()

        g = ExitStack()
        X2 = sb(g, "X2", [P, T, DM])
        Y1 = [sb(g, f"Y1_{i}", [P, DM]) for i in range(2)]
        Y2 = [sb(g, f"Y2_{i}", [P, DM]) for i in range(2)]
        ZN = sb(g, "ZN", [P, T, DM])
        ZT = sb(g, "ZT", [P, T, DM])
        XT3 = sb(g, "XT3", [P, K, L])
        lsum = sb(g, "lsum", [P, E2])
        lmax = sb(g, "lmax", [P, 8])
        lidf = sb(g, "lidf", [P, TOP])
        lsel = sb(g, "lsel", [P, TOP, NT])
        loh = sb(g, "loh", [P, TOP, E2])
        ltmp = sb(g, "ltmp", [P, TOP, NT, E2])
        lme = sb(g, "lme", [P, NT])
        lden = sb(g, "lden", [P, NT])
        g.close()
        a.close()

        h = ExitStack()
        W1R = sb(h, "W1R", [P, TOP, K, FF])
        W2R = sb(h, "W2R", [P, TOP, FT, DM])
        W1H = [sb(h, f"W1H{i}", [P, K, P], F32R) for i in range(2)]
        W1L = [sb(h, f"W1L{i}", [P, K, P], F32R) for i in range(2)]
        W2H = [sb(h, f"W2H{i}", [P, DM], F32R) for i in range(2)]
        W2L = [sb(h, f"W2L{i}", [P, DM], F32R) for i in range(2)]
        XS = sb(h, "XS", [P, K, L])
        XSH = sb(h, "XSH", [P, K, L], F32R)
        XSL = sb(h, "XSL", [P, K, L], F32R)
        HF = [sb(h, f"HF{i}", [P, L]) for i in range(2)]
        HFH = [sb(h, f"HFH{i}", [P, L], F32R) for i in range(2)]
        HFL = [sb(h, f"HFL{i}", [P, L], F32R) for i in range(2)]
        O = sb(h, "O", [P, T, DM])
        b1n = sb(h, "b1n", [FT, TOP, P])
        b1T = sb(h, "b1T", [P, TOP, FT])
        b2b = sb(h, "b2b", [P, TOP, DM])
        h.close()

        nat_loaded = sem("nat_loaded")
        ctx_loaded = sem("ctx_loaded")
        slots_zeroed = sem("slots_zeroed")
        const_ready = sem("const_ready")
        pool_step = sem("pool_step")
        act_step = sem("act_step")
        dve_step = sem("dve_step")
        small_ready = sem("small_ready")
        set_t = sem("set_t")
        set_c = sem("set_c")
        xin_ready = sem("xin_ready")
        xp_ready = sem("xp_ready")
        xh_ready = sem("xh_ready")
        th_ready = sem("th_ready")
        u_ready = sem("u_ready")
        u_spilled = sem("u_spilled")
        xd_ready = sem("xd_ready")
        xd_copied = sem("xd_copied")
        bc_stored = sem("bc_stored")
        dtp_ready = sem("dtp_ready")
        z_ready = sem("z_ready")
        r_ready = sem("r_ready")
        w_ready = sem("w_ready")
        ln_ready = sem("ln_ready")
        dt_ready = sem("dt_ready")

        xb_loaded = sem("xb_loaded")
        var_ready = sem("var_ready")
        rstd_ready = sem("rstd_ready")
        xn_ready = sem("xn_ready")
        qk_ready = sem("qk_ready")
        qk_copied = sem("qk_copied")
        t_ready = sem("t_ready")
        t_copied = sem("t_copied")
        e_ready = sem("e_ready")
        nneg_ready = sem("nneg_ready")
        exp_ready = sem("exp_ready")
        p_ready = sem("p_ready")
        o_ready = sem("o_ready")
        x1_ready = sem("x1_ready")
        x1_stored = sem("x1_stored")
        xn1_ready = sem("xn1_ready")
        xn1_stored = sem("xn1_stored")
        score_ready = sem("score_ready")
        score_copied = sem("score_copied")

        mask_ready = sem("mask_ready")
        rank_ready = sem("rank_ready")
        diff_ready = sem("diff_ready")
        ex_ready = sem("ex_ready")
        pos_ready = sem("pos_ready")
        tex_ready = sem("tex_ready")
        slots_set = sem("slots_set")
        slots_loaded = sem("slots_loaded")
        slots_t = sem("slots_t")
        slots_ready = sem("slots_ready")

        bb_loaded = [sem(f"bb_loaded{i}") for i in range(BC_RING)]
        cb_loaded = [sem(f"cb_loaded{i}") for i in range(BC_RING)]
        ul_loaded = sem("ul_loaded")
        da_ready = sem("da_ready")
        dbu_ready = sem("dbu_ready")
        scan_done = sem("scan_done")
        hc_ready = sem("hc_ready")
        added = sem("added")
        s_summed = sem("s_summed")
        y_ready = sem("y_ready")

        gu_loaded = [sem(f"gu_loaded{i}") for i in range(2)]
        wd_loaded = [sem(f"wd_loaded{i}") for i in range(2)]
        gcol_ready = sem("gcol_ready")
        xg_loaded = [sem(f"xg_loaded{i}") for i in range(2)]
        xgt_ready = sem("xgt_ready")
        xgt_copied = sem("xgt_copied")
        up_ready = sem("up_ready")
        tg_ready = sem("tg_ready")
        gg_ready = sem("gg_ready")
        hh_ready = sem("hh_ready")
        ht_ready = sem("ht_ready")
        ht_copied = sem("ht_copied")
        down_ready = sem("down_ready")
        yt_ready = sem("yt_ready")
        yt_stored = sem("yt_stored")

        x1_loaded = sem("x1_loaded")
        pcol_ready = sem("pcol_ready")
        y12_loaded = [sem(f"y12_loaded{i}") for i in range(2)]
        y12_used = sem("y12_used")
        var2_ready = sem("var2_ready")
        rstd2_ready = sem("rstd2_ready")
        zn_ready = sem("zn_ready")
        zt_ready = sem("zt_ready")
        gate_ready = sem("gate_ready")
        gt_ready = sem("gt_ready")
        x3_ready = sem("x3_ready")
        x3_stored = sem("x3_stored")
        xn3_ready = sem("xn3_ready")
        t3_ready = sem("t3_ready")
        t3_copied = sem("t3_copied")
        xt3_stored = sem("xt3_stored")
        lg_ready = sem("lg_ready")
        lg_copied = sem("lg_copied")
        lsum_ready = sem("lsum_ready")
        lidx_ready = sem("lidx_ready")
        lme_ready = sem("lme_ready")
        lexp_ready = sem("lexp_ready")
        rwf_ready = sem("rwf_ready")

        wq_loaded = [sem(f"wq_loaded{i}") for i in range(WQ)]
        b1_loaded = sem("b1_loaded")
        b1_t = sem("b1_t")
        b1_ready = sem("b1_ready")
        xs_loaded = sem("xs_loaded")
        xs_split = sem("xs_split")
        w1h_ready = sem("w1h_ready")
        w1l_ready = sem("w1l_ready")
        w2h_ready = sem("w2h_ready")
        w2l_ready = sem("w2l_ready")
        xsh_ready = sem("xsh_ready")
        hfh_ready = sem("hfh_ready")
        ob_ready = sem("ob_ready")
        up2_ready = sem("up2_ready")
        hf_ready = sem("hf_ready")
        hfl_ready = sem("hfl_ready")
        down2_done = sem("down2_done")
        y2_added = sem("y2_added")
        o_loaded = sem("o_loaded")
        o_final = sem("o_final")
        out_stored = sem("out_stored")

        wait_regs = {}

        def wait_apart(eng, sem_, value):
            if not isinstance(value, int):
                reg = wait_regs.setdefault(eng.engine, None) or eng.alloc_register(f"wait_value_{len(wait_regs)}")
                wait_regs[eng.engine] = reg
                eng.reg_mov(reg, value)
                eng.wait_ge(const_ready, 2)
                value = reg
            eng.wait_ge(sem_, value)

        def bank(i, parts, cols):
            return PS[i][0:parts, 0:cols]

        setup = [
            ([nat_qk[:, w, k * P:(k + 1) * P] for w in range(2) for k in range(CK)], P,
             P, wqkT[:].rearrange("p w k c -> p (w k c)")),
            *[([nat_in[:, c, k * P:(k + 1) * P] for c in range(DC)], P, P, inT[:, k, :]) for k in range(CK)],
            ([nat_xp[:, c * P:(c + 1) * P] for c in range(DC)], XD, P, xpT[:].rearrange("p c x -> p (c x)")),
            ([nat_dtp[:, c, :] for c in range(DC)], P, R, dtpT[:]),
            ([nat_g2[:, k * P:(k + 1) * P] for k in range(K)], E2, P, gate2T[:].rearrange("p k e -> p (k e)")),
            *[([nat_ctx[:, b * T + t, k * P:(k + 1) * P] for t in range(T)], P, P,
               ctxT[:, k, b * L:(b + 1) * L]) for b in range(B) for k in range(CK)],
        ]
        NAT_LOADS = 14

        block = top.enter_context(nc.Block())

        @block.sync
        def _(sp):
            with nc.allow_non_contiguous_dma(reason="a few hundred words of weights"):
                sp.dma_start(nat_qk[:, 0, :], Wq).then_inc(nat_loaded, DMA)
                sp.dma_start(nat_qk[:, 1, :], Wk).then_inc(nat_loaded, DMA)
                sp.dma_start(nat_in[:], in_w.rearrange("(c p) k -> p c k", p=P)).then_inc(nat_loaded, DMA)
                sp.dma_start(nat_ctx[:], ctx.rearrange("b (t p) c -> p (b t) c", p=P)).then_inc(ctx_loaded, DMA)
                sp.dma_start(nat_xp[:], xp_w).then_inc(nat_loaded, DMA)
                sp.dma_start(nat_dtp[:], dtp_w.rearrange("(c p) r -> p c r", p=P)).then_inc(nat_loaded, DMA)
                sp.dma_start(nat_g2[:], gate2_w).then_inc(nat_loaded, DMA)
                sp.dma_start(nat_A[:], A_log.rearrange("(c p) n -> p c n", p=P)).then_inc(nat_loaded, DMA)
                sp.dma_start(convW[:], conv_w.rearrange("(c p) o t -> p c (o t)", p=P)).then_inc(nat_loaded, DMA)
                sp.dma_start(convB[:], conv_b.rearrange("(c p) -> p c", p=P)).then_inc(nat_loaded, DMA)
                sp.dma_start(dtB[:], dtp_b.rearrange("(c p) -> p c", p=P)).then_inc(nat_loaded, DMA)
                sp.dma_start(skip[:], D_skip.rearrange("(c p) -> p c", p=P)).then_inc(nat_loaded, DMA)
                sp.dma_start(qkb[:, 0:1], bq.rearrange("(p o) -> p o", o=1)).then_inc(nat_loaded, DMA)
                sp.dma_start(qkb[:, 1:2], bk.rearrange("(p o) -> p o", o=1)).then_inc(nat_loaded, DMA)
                sp.dma_start(routerW[:], router_w.rearrange("(k p) e -> p k e", p=P)).then_inc(nat_loaded, DMA)
                sp.wait_ge(const_ready, 1)
                sp.dma_start(slot_dram.rearrange("(j p) o -> j (p o)", p=P), zslots[:]).then_inc(slots_zeroed, DMA)

            with sp.Fori(0, B) as b:
                sp.wait_ge(u_ready, b + 1)
                sp.dma_start(u_dram[ds(b, 1)].rearrange("b p f -> (b p) f"),
                             U[:].rearrange("p c l -> p (c l)")).then_inc(u_spilled, DMA)
                sp.wait_ge(xd_copied, b + 1)
                sp.dma_start(bc_dram[ds(b, 1)].rearrange("b n l -> (b n) l"), xdb[R:XD, :]).then_inc(bc_stored, DMA)

            with sp.Fori(0, B) as b:
                sp.wait_ge(dt_ready, B)
                sp.dma_start(XB[:], x[ds(b, 1)].rearrange("b (t p) d -> p (b t) d", p=P)).then_inc(xb_loaded, DMA)
                sp.wait_ge(x1_ready, (b + 1) * T)
                sp.dma_start(x1_dram[ds(b * T, T)].rearrange("t p d -> p t d"), XB[:]).then_inc(x1_stored, DMA)
                sp.wait_ge(xn1_ready, b + 1)
                sp.dma_start(xn_dram[ds(b * L, L), :].rearrange("(t p) d -> p t d", p=P),
                             XN[:]).then_inc(xn1_stored, DMA)
                wait_apart(sp, x1_stored, b * DMA + DMA)

            def load_bc(b, n):
                sp.wait_ge(dbu_ready, b * NS + (n + 1))
                sp.dma_start(Bb[n % BC_RING][:], bc_dram[ds(b, 1), n, :].to_broadcast([P, L])).then_inc(bb_loaded[n % BC_RING], DMA)
                sp.wait_ge(hc_ready, b * NS + (n + 1))
                sp.dma_start(Cb[n % BC_RING][:], bc_dram[ds(b, 1), NS + n, :].to_broadcast([P, L])).then_inc(cb_loaded[n % BC_RING], DMA)

            def load_u(b):
                sp.dma_start(U[:].rearrange("p c l -> p (c l)"),
                             u_dram[ds(b, 1)].rearrange("b p f -> (b p) f")).then_inc(ul_loaded, DMA)

            def load_expert(j0, n):
                j = j0 + n
                e = sp.value_load(tile_exp[0:1, ds(j, 1)], min_val=0, max_val=E - 1)
                sp.wait_ge(up_ready, j + 1)
                w = WGU[n % 2]
                sp.dma_start(w[:, :, 0, :], gate_w[ds(e, 1)].rearrange("e (p k) f -> (e p) k f", p=P)).then_inc(gu_loaded[n % 2], DMA)
                sp.dma_start(w[:, :, 1, :], up_w[ds(e, 1)].rearrange("e (p k) f -> (e p) k f", p=P)).then_inc(gu_loaded[n % 2], DMA)
                sp.wait_ge(down_ready, j + 1)
                sp.dma_start(WD[n % 2][:], down_w[ds(e, 1)].rearrange("e (p k) d -> (e p) k d", p=FH)).then_inc(wd_loaded[n % 2], DMA)

            sp.wait_ge(bc_stored, B * DMA)
            sp.wait_ge(u_spilled, B * DMA)
            load_u(0)
            for n in range(NS):
                load_bc(0, n)
                if n == NS // 2:
                    sp.wait_ge(slots_set, TOP * NT * DMA)
                    sp.dma_start(slotf[:], slot_dram.rearrange("(j p) o -> j (p o)", p=P)).then_inc(slots_loaded, DMA)
            sp.wait_ge(tex_ready, 1)
            sp.wait_ge(slots_ready, 1)
            with sp.Fori(1, B) as b:
                for n in range(NS):
                    load_bc(b, n)
                    if n == NS // 2:
                        sp.wait_ge(y_ready, b * DC)
                        load_u(b)
                    load_expert(b * NS - NS, n)

            with sp.Fori(0, B) as b:
                sp.wait_ge(yt_stored, SLOT_TILES * DMA + DMA)
                sp.wait_ge(y_ready, B * DC)
                sp.dma_start(X2[:], x1_dram[ds(b * T, T)].rearrange("t p d -> p t d")).then_inc(x1_loaded, DMA)
                sp.wait_ge(x3_ready, (b + 1) * T)
                sp.dma_start(x3_dram[ds(b * T, T)].rearrange("t p d -> p t d"), X2[:]).then_inc(x3_stored, DMA)
                sp.wait_ge(t3_copied, (b + 1) * T)
                sp.dma_start(xt_dram[ds(b, 1)].rearrange("b p f -> (b p) f"),
                             XT3[:].rearrange("p k l -> p (k l)")).then_inc(xt3_stored, DMA)
                wait_apart(sp, x3_stored, b * DMA + DMA)

            sp.wait_ge(rwf_ready, 1)
            sp.wait_ge(x3_stored, B * DMA)
            sp.wait_ge(xt3_stored, B * DMA)
            ev = [sp.value_load(lidx[0:1, k:k + 1], min_val=0, max_val=E2 - 1) for k in range(TOP)]
            sp.dma_start(XS[:].rearrange("p k l -> p (k l)"), xt_dram[0]).then_inc(xs_loaded, DMA)
            for k in range(TOP):
                sp.dma_start(b1n[:, k, :], b1[ds(ev[k], 1)].rearrange("e (c p) -> (e c) p", p=P)).then_inc(b1_loaded, DMA)
                sp.dma_start(b2b[:, k, :], b2[ds(ev[k], 1), :].to_broadcast([P, DM])).then_inc(b1_loaded, DMA)
            FQ = FF // WQ
            for k in range(TOP):
                for i in range(WQ):
                    cols = slice(i * FQ, (i + 1) * FQ)
                    if k:
                        sp.wait_ge(wq_loaded[i], k * 2 * DMA)
                    sp.dma_start(W1R[:, k, :, cols], w1[ds(ev[k], 1), :, cols].rearrange(
                        "e (k p) f -> p (e k) f", p=P)).then_inc(wq_loaded[i], DMA)
                    sp.dma_start(W2R[:, k, i * FT // WQ:(i + 1) * FT // WQ, :], w2[ds(ev[k], 1), cols, :].rearrange(
                        "e (f p) d -> p (e f) d", p=P)).then_inc(wq_loaded[i], DMA)
            for tb in range(B):
                if tb:
                    sp.wait_ge(out_stored, tb * DMA)
                sp.dma_start(O[:], x3_dram[tb * T:(tb + 1) * T].rearrange("t p d -> p t d")).then_inc(o_loaded, DMA)
                if tb + 1 < B:
                    sp.wait_ge(xs_split, tb + 1)
                    sp.dma_start(XS[:].rearrange("p k l -> p (k l)"), xt_dram[tb + 1]).then_inc(xs_loaded, DMA)
                sp.wait_ge(y2_added, (tb + 1) * TOP + 1)
                sp.dma_start(out[tb].rearrange("(t p) d -> p t d", p=P), O[:]).then_inc(out_stored, DMA)
            sp.wait_ge(out_stored, B * DMA)

        @block.gpsimd
        def _(pool):
            step = Steps(pool, pool_step)
            pool.memset(zslots[:], 0.0).then_inc(const_ready, 1)
            step.mark(pool.memset(ident[:], 0.0))
            step.mark(pool.memset(ones[:], 1.0))
            step.wait()
            pool.affine_select(out=ident[:], in_=ident[:], compare_op=ALU.not_equal, fill=1.0, base=0,
                               pattern=[[-1, P]], channel_multiplier=1).then_inc(const_ready, 1)
            pool.memset(minus_half[:], -0.5).then_inc(const_ready, 1)
            pool.iota(iota_e[:], pattern=[[1, E]], base=0, channel_multiplier=0,
                      allow_small_or_imprecise_dtypes=True).then_inc(const_ready, 1)
            pool.memset(XP[:], 0.0).then_inc(const_ready, 1)

            def rstd_of(count, ready, done):
                pool.wait_ge(ready, count)
                pool.tensor_tensor(rstd[:], vare[:], minus_half[:], ALU.pow).then_inc(done, 1)

            with pool.Fori(0, B) as b:
                rstd_of(b * 2 + 1, var_ready, rstd_ready)
                rstd_of(b * 2 + 2, var_ready, rstd_ready)

            pool.wait_ge(score_copied, B)
            pool.wait_ge(x1_stored, B * DMA)
            pool.wait_ge(xn1_stored, B * DMA)
            pool.affine_select(out=tri[:], in_=ones[:], compare_op=ALU.is_gt, fill=0.0, base=0,
                               pattern=[[1, P]], channel_multiplier=-1).then_inc(const_ready, 1)
            pool.iota(iota_j[:], pattern=[[1, SLOT_TILES]], base=0, channel_multiplier=0,
                      allow_small_or_imprecise_dtypes=True).then_inc(const_ready, 1)
            pool.iota(tokid[:], pattern=[[P, NT]], base=0, channel_multiplier=1,
                      allow_small_or_imprecise_dtypes=True).then_inc(const_ready, 1)
            pool.wait_ge(const_ready, 8)
            pool.wait_ge(slots_zeroed, DMA)
            pool.wait_ge(pos_ready, 1)
            def scatter(k, t):
                pool.indirect_dma_start(
                    out=slot_dram, out_offset=bass.IndirectOffsetOnAxis(ap=pos[:, k, t:t + 1], axis=0),
                    in_=tokid[:, t:t + 1], in_offset=None).then_inc(slots_set, DMA)

            pool.sem_inc(dbu_ready, BC_RING)

            def dbu(b, n):
                group = b * (NS // GROUP) + n // GROUP
                pool.wait_ge(bb_loaded[n % BC_RING], b * (NS // BC_RING * DMA) + (n // BC_RING + 1) * DMA)
                if n % GROUP < GROUP - 1:
                    wait_apart(pool, added, group * (GROUP - 1) + (n % GROUP + 1))
                else:
                    wait_apart(pool, s_summed, group + 1)
                pool.tensor_tensor(S[n % S_RING][:], DTU[:, ds(b, 1), :, :].rearrange("p b c l -> p (b c) l"),
                                   Bb[n % BC_RING][:].rearrange("p (o l) -> p o l", o=1).to_broadcast([P, DC, L]),
                                   ALU.mult).then_inc(dbu_ready, 1)

            def gather(j0, n):
                j = j0 + n
                pool.wait_ge(xgt_ready, j + 1)
                pool.tensor_copy(gcol[n % 2][:], slot_tok[:, ds(j, 1)]).then_inc(gcol_ready, 1)
                wait_apart(pool, gcol_ready, j + 1)
                pool.indirect_dma_start(out=XG[n % 2][:], out_offset=None, in_=xn_dram,
                                        in_offset=bass.IndirectOffsetOnAxis(ap=gcol[n % 2][:, 0:1], axis=0)
                                        ).then_inc(xg_loaded[n % 2], DMA)

            pool.wait_ge(dt_ready, B)
            per = TOP * NT // (NS // 2)
            for n in range(NS):
                if n < NS // 2:
                    for i in range(n * per, (n + 1) * per):
                        scatter(i // NT, i % NT)
                dbu(0, n)
            pool.wait_ge(slots_ready, 1)

            def mixture_steps(b, last):
                for n in range(NS):
                    dbu(b, n)
                    if n + 2 < NS:
                        gather(b * NS - NS, n + 2)
                    elif not last:
                        gather(b * NS, n + 2 - NS)

            gather(0, 0)
            gather(0, 1)
            with pool.Fori(1, B - 1) as b:
                mixture_steps(b, False)
            mixture_steps(B - 1, True)

            pool.wait_ge(yt_stored, SLOT_TILES * DMA + DMA)
            pool.wait_ge(y_ready, B * DC)
            with pool.Fori(0, B) as b:
                for c in range(T):
                    t = b * T + c
                    pool.wait_ge(y12_used, t + 1)
                    for k in range(TOP):
                        pool.tensor_copy(pcol[(c % 2) * TOP + k][:], pos[:, k, ds(t, 1)]).then_inc(pcol_ready, 1)
                    wait_apart(pool, pcol_ready, t * TOP + TOP)
                    for k, y in enumerate((Y1, Y2)):
                        pool.indirect_dma_start(
                            out=y[c % 2][:], out_offset=None, in_=y_dram,
                            in_offset=bass.IndirectOffsetOnAxis(ap=pcol[(c % 2) * TOP + k][:, 0:1], axis=0)
                        ).then_inc(y12_loaded[c % 2], DMA)
                rstd_of(b * 2 + 1, var2_ready, rstd2_ready)
                rstd_of(b * 2 + 2, var2_ready, rstd2_ready)

            for e in range(TOP):
                pool.wait_ge(rwf_ready, 1)
            with pool.Fori(0, B) as tb:
                with pool.Fori(0, TOP) as e:
                    it = pool.snap(tb * (TOP * FT) + e * FT)
                    for f in range(FT):
                        pool.wait_ge(w1h_ready, it + (f + 1))
                        pool.tensor_tensor(W1L[f % 2][:],
                                           W1R[:, ds(e, 1), :, f * P:(f + 1) * P].rearrange("p e k f -> p (e k) f"),
                                           W1H[f % 2][:].bitcast(F32), ALU.subtract).then_inc(w1l_ready, 1)
                        pool.wait_ge(w2h_ready, it + (f + 1))
                        pool.tensor_tensor(W2L[f % 2][:], W2R[:, ds(e, 1), f, :].rearrange("p e d -> p (e d)"),
                                           W2H[f % 2][:].bitcast(F32), ALU.subtract).then_inc(w2l_ready, 1)

        @block.scalar
        def _(act):
            step = Steps(act, act_step)
            act.wait_ge(nat_loaded, NAT_LOADS * DMA)
            step.mark(act.activation(negA[:], nat_A[:], ACT.Exp))
            step.wait()
            act.mul(negA[:], negA[:], -1.0).then_inc(small_ready, 1)
            for i, (_, _, parts, dst) in enumerate(setup):
                act.wait_ge(set_t, i + 1)
                act.copy(dst, bank(4 + i % 2, parts, dst.shape[1])).then_inc(set_c, 1)

            act.wait_ge(const_ready, 5)
            with act.Fori(0, B) as b:
                for c in range(DC):
                    act.wait_ge(xin_ready, b * DC + (c + 1))
                    act.copy(XP[:, c, TAPS - 1:], PS[c][:]).then_inc(xp_ready, 1)
                act.wait_ge(xh_ready, b + 1)
                act.activation(TH[:], XH[:], ACT.Tanh).then_inc(th_ready, 1)
                act.wait_ge(xd_ready, b + 1)
                act.copy(xdb[:], PS[4][0:XD, :]).then_inc(xd_copied, 1)
                first = step.n
                for c in range(DC):
                    act.wait_ge(r_ready, b * DC + (c + 1))
                    act.activation(ZZ[:, c, :], PS[c][:], ACT.Abs, bias=dtB[:, c:c + 1]).then_inc(act_step, 1)
                act.wait_ge(act_step, b * DC + (first + DC))
                act.activation(ZZ[:], ZZ[:], ACT.Exp, scale=-1.0).then_inc(z_ready, 1)
                act.wait_ge(w_ready, b * 2 + 2)
                act.activation(TH[:], WW[:], ACT.Ln).then_inc(ln_ready, 1)
                act.wait_ge(bc_stored, b * DMA + DMA)
            step.n += B * DC

            def copy_t(count, dst, i):
                act.wait_ge(t_ready, count)
                act.copy(dst, PS[4 + i % 2][:].rearrange("p (k c) -> p k c", k=K)).then_inc(t_copied, 1)

            with act.Fori(0, B) as b:
                act.wait_ge(qk_ready, b + 1)
                for w in range(2):
                    act.activation(QKT[:, w, :], PS[6 + w][:], ACT.Identity, bias=qkb[:, w:w + 1]).then_inc(qk_copied, 1)
                for t in range(T):
                    copy_t(b * 12 + (t + 1), XNT[:, :, t * P:(t + 1) * P], t)
                for t in range(T):
                    act.wait_ge(nneg_ready, b * T + (t + 1))
                    act.activation(PR[:, t, :], PS[6 + t % 2][:], ACT.Exp, bias=nneg[:, t:t + 1],
                                   accum_out=rsum[:, t:t + 1]).then_inc(exp_ready, 1)
                for t in range(T):
                    copy_t(b * 12 + (T + t + 1), ATT[:, :, t * P:(t + 1) * P], t)
                for t in range(T):
                    copy_t(b * 12 + (2 * T + t + 1), XNT[:, :, t * P:(t + 1) * P], t)

            act.wait_ge(diff_ready, 1)
            act.activation(ex[:], diff[:], ACT.Exp).then_inc(ex_ready, 1)

            def decay(b, n):
                u = b * NS + n
                wait_apart(act, scan_done, u + 1)
                for c in range(DC):
                    ins = act.activation(
                        dA[n % A_RING][:, c, 1:], DT[:, ds(b, 1), c, 1:].rearrange("p b l -> p (b l)"),
                        ACT.Exp, scale=negA[:, c, n:n + 1])
                ins.then_inc(da_ready, 1)

            def copy_xg(j0, n):
                j = j0 + n
                act.wait_ge(xgt_ready, j + 3)
                act.copy(XGT[n % 2][:], PS[4][:].rearrange("p (k t) -> p k t", k=K)).then_inc(xgt_copied, 1)

            def tanh_g(j0, n):
                act.wait_ge(up_ready, j0 + (n + 3))
                act.activation(TG[n % 2][:], PS[5][:, 0:F], ACT.Tanh, scale=0.5).then_inc(tg_ready, 1)

            def copy_ht(j0, n):
                act.wait_ge(ht_ready, j0 + (n + 1))
                act.copy(HT[n % 2][:], PS[6][0:FH, 0:2 * P].rearrange("p (k t) -> p k t", k=2)).then_inc(ht_copied, 1)

            def copy_y(j0, n):
                j = j0 + n
                act.wait_ge(down_ready, j + 3)
                act.wait_ge(yt_stored, j * DMA + DMA)
                act.copy(YT[n % 2][:], PS[7][:]).then_inc(yt_ready, 1)

            def store_y(j0, n):
                j = j0 + n
                act.wait_ge(yt_ready, j + 2)
                act.dma_start(y_dram[ds(j * P, P), :], YT[n % 2][:]).then_inc(yt_stored, DMA)

            act.wait_ge(dt_ready, B)
            act.wait_ge(scan_done, A_RING)
            for n in range(NS):
                decay(0, n)
            act.wait_ge(slots_ready, 1)
            act.sem_inc(yt_ready, 1)
            act.sem_inc(yt_stored, DMA)

            def mixture_steps(b, last):
                j0 = b * NS - NS
                for n in range(NS):
                    if n + AHEAD < NS:
                        decay(b, n + AHEAD)
                    elif not last:
                        decay(b + 1, n + AHEAD - NS)
                    copy_ht(j0, n)
                    if n + 2 < NS:
                        copy_xg(j0, n + 2)
                    elif not last:
                        copy_xg(j0 + NS, n + 2 - NS)
                    if n + 1 < NS:
                        tanh_g(j0, n + 1)
                    elif not last:
                        tanh_g(j0 + NS, 0)
                    copy_y(j0, n)
                    store_y(j0, n)

            copy_xg(0, 0)
            tanh_g(0, 0)
            copy_xg(0, 1)
            for n in range(AHEAD):
                decay(1, n)
            with act.Fori(1, B - 1) as b:
                mixture_steps(b, False)
            mixture_steps(B - 1, True)

            with act.Fori(0, B) as b:
                act.wait_ge(zn_ready, b + 1)
                act.activation(ZT[:], ZN[:], ACT.Tanh, scale=0.5).then_inc(zt_ready, 1)
                for t in range(T):
                    act.wait_ge(t3_ready, b * T + (t + 1))
                    act.copy(XT3[:, :, t * P:(t + 1) * P],
                             PS[4 + t % 2][:].rearrange("p (k c) -> p k c", k=K)).then_inc(t3_copied, 1)
                act.wait_ge(xt3_stored, b * DMA + DMA)
            act.wait_ge(lme_ready, 1)
            act.activation(lsel[:], lsel[:], ACT.Exp).then_inc(lexp_ready, 1)

            act.wait_ge(b1_t, 1)
            act.copy(b1T[:], PS[6][:, 0:TOP * FT].rearrange("p (k f) -> p k f", k=TOP)).then_inc(b1_ready, 1)
            act.wait_ge(b1_ready, 1)
            with act.Fori(0, B) as tb:
                with act.Fori(0, TOP) as e:
                    it = act.snap(tb * (TOP * FT) + e * FT)

                    def split(f):
                        if f % (FT // WQ) == 0:
                            act.wait_ge(wq_loaded[f // (FT // WQ)], e * (2 * DMA) + 2 * DMA)
                        act.wait_ge(up2_ready, it + (f + 1))
                        act.copy(W1H[f % 2][:], W1R[:, ds(e, 1), :, f * P:(f + 1) * P].rearrange(
                            "p e k f -> p (e k) f")).then_inc(w1h_ready, 1)
                        act.wait_ge(down2_done, it + (f + 1))
                        act.copy(W2H[f % 2][:], W2R[:, ds(e, 1), f, :].rearrange("p e d -> p (e d)")
                                 ).then_inc(w2h_ready, 1)

                    def gelu(f):
                        wait_apart(act, up2_ready, it + (f + 3))
                        act.activation(HF[f % 2][:], PS[4 + f % 2][:], ACT.Gelu_apprx_tanh,
                                       bias=b1T[:, ds(e, 1), f:f + 1].rearrange("p e f -> p (e f)")).then_inc(hf_ready, 1)

                    split(0)
                    for f in range(FT):
                        if f + 1 < FT:
                            split(f + 1)
                        gelu(f)

        @block.vector
        def _(dve):
            step = Steps(dve, dve_step)
            dve.wait_ge(nat_loaded, NAT_LOADS * DMA)
            dve.tensor_scalar(halfW[:], convW[:], 0.5, None, ALU.mult).then_inc(small_ready, 1)
            dve.tensor_scalar(halfB[:], convB[:], 0.5, None, ALU.mult).then_inc(small_ready, 1)
            dve.wait_ge(small_ready, 3)

            with step.loop(B, 3 * DC + 2) as b:
                for c in range(DC):
                    dve.wait_ge(xp_ready, b * DC + (c + 1))
                    step.mark(dve.tensor_scalar(XH[:, c, :], XP[:, c, TAPS - 1:], halfW[:, c, TAPS - 1:TAPS],
                                                halfB[:, c:c + 1], ALU.mult, ALU.add))
                for j in range(TAPS - 1):
                    for c in range(DC):
                        if c == 0:
                            step.wait()
                        ins = dve.scalar_tensor_tensor(XH[:, c, :], XP[:, c, j:j + L], halfW[:, c, j:j + 1],
                                                       XH[:, c, :], ALU.mult, ALU.add)
                        if j < TAPS - 2:
                            step.mark(ins)
                ins.then_inc(xh_ready, 1)
                dve.wait_ge(th_ready, b + 1)
                dve.scalar_tensor_tensor(U[:], TH[:], 1.0, XH[:], ALU.add, ALU.mult).then_inc(u_ready, 1)
                for c in range(DC):
                    dve.wait_ge(dtp_ready, b * DC + (c + 1))
                    dve.tensor_scalar(RL[:, c, :], PS[c][:], dtB[:, c:c + 1], 0.0, ALU.add, ALU.max).then_inc(r_ready, 1)
                dve.wait_ge(z_ready, b + 1)
                dve.tensor_scalar(WW[:], ZZ[:], 1.0, None, ALU.add).then_inc(w_ready, 1)
                dve.wait_ge(w_ready, b * 2 + 1)
                dve.scalar_tensor_tensor(ND[:], WW[:], 1.0, ZZ[:], ALU.subtract, ALU.subtract).then_inc(w_ready, 1)
                dve.wait_ge(w_ready, b * 2 + 2)
                step.mark(dve.tensor_tensor(RL[:], RL[:], ND[:], ALU.subtract))
                dve.wait_ge(ln_ready, b + 1)
                step.wait()
                step.mark(dve.tensor_tensor(DT[:, ds(b, 1)].rearrange("p b c l -> p (b c) l"), RL[:], TH[:], ALU.add))
                step.wait()
                (dve.tensor_tensor(DTU[:, ds(b, 1)].rearrange("p b c l -> p (b c) l"),
                                            DT[:, ds(b, 1)].rearrange("p b c l -> p (b c) l"), U[:], ALU.mult)).then_inc(dt_ready, 1)
                dve.wait_ge(u_spilled, b * DMA + DMA)

            def layernorm(src, dst, count, ready, got, done):
                for t in range(T):
                    ins = dve.bn_stats(stats[:, t, :], src[:, t, :])
                step.mark(ins)
                step.wait(apart=wait_apart)
                for t in range(T):
                    ins = dve.bn_aggr(mv[:, t, :], stats[:, t, :])
                step.mark(ins)
                step.wait()
                dve.tensor_scalar(vare[:].rearrange("p (t o) -> p t o", o=1), mv[:, :, 1:2], EPS, None,
                                  ALU.add).then_inc(ready, 1)
                dve.wait_ge(got, count)
                for t in range(T):
                    ins = dve.tensor_scalar(dst[:, t, :], src[:, t, :], mv[:, t, 0:1], rstd[:, t:t + 1],
                                            ALU.subtract, ALU.mult)
                ins.then_inc(done, 1)

            with step.loop(B, 4 + 2 * T) as b:
                dve.wait_ge(xb_loaded, b * DMA + DMA)
                layernorm(XB, XN, b * 2 + 1, var_ready, rstd_ready, xn_ready)

                def row_max(t):
                    dve.wait_ge(e_ready, b * T + (t + 1))
                    step.mark(dve.tensor_reduce(nmax[:, t:t + 1], PS[6 + t % 2][:], AX, ALU.max))
                    step.wait()
                    dve.tensor_scalar(nneg[:, t:t + 1], nmax[:, t:t + 1], -1.0, None, ALU.mult).then_inc(nneg_ready, 1)

                def normalize(t):
                    dve.wait_ge(exp_ready, b * T + (t + 1))
                    step.mark(dve.reciprocal(rinv[:, t:t + 1], rsum[:, t:t + 1]))
                    step.wait()
                    dve.tensor_scalar(PR[:, t, :], PR[:, t, :], rinv[:, t:t + 1], None, ALU.mult).then_inc(p_ready, 1)

                row_max(0)
                row_max(1)
                for t in range(T):
                    normalize(t)
                    if t + 2 < T:
                        row_max(t + 2)
                for t in range(T):
                    dve.wait_ge(o_ready, b * T + (t + 1))
                    dve.tensor_tensor(XB[:, t, :], PS[6 + t % 2][:], XB[:, t, :], ALU.add).then_inc(x1_ready, 1)
                dve.wait_ge(x1_ready, b * T + T)
                layernorm(XB, XN, b * 2 + 2, var_ready, rstd_ready, xn1_ready)
                dve.wait_ge(score_ready, b + 1)
                dve.tensor_copy(SC[:, ds(b * T, T), :], PS[6][:, 0:T * E].rearrange("p (t e) -> p t e", t=T)
                                ).then_inc(score_copied, 1)
                dve.wait_ge(xn1_stored, b * DMA + DMA)

            def do(ins):
                step.mark(ins)
                step.wait()

            dve.wait_ge(score_copied, B)
            dve.wait_ge(x1_stored, B * DMA)
            dve.wait_ge(xn1_stored, B * DMA)
            for t in range(NT):
                ins = dve.max(M8[:, t, :], SC[:, t, :])
            do(ins)
            for t in range(NT):
                ins = dve.max_index(I8[:, t, :], M8[:, t, :], SC[:, t, :])
            dve.tensor_tensor(diff[:].rearrange("p (t o) -> p t o", o=1), M8[:, :, 1:2], M8[:, :, 0:1],
                              ALU.subtract).then_inc(diff_ready, 1)
            do(ins)
            for k in range(TOP):
                ins = dve.tensor_copy(IF[:, k, :].rearrange("p (t o) -> p t o", o=1), I8[:, :, k:k + 1])
            do(ins)
            dve.wait_ge(const_ready, 4)
            for k in range(TOP):
                ins = dve.tensor_tensor(OH[:, k], iota_e[:].rearrange("p (o e) -> p o e", o=1).to_broadcast([P, NT, E]),
                                        IF[:, k, :].rearrange("p (t o) -> p t o", o=1).to_broadcast([P, NT, E]),
                                        ALU.is_equal)
            do(ins)
            dve.tensor_tensor(MM[:], OH[:, 0], OH[:, 1], ALU.add).then_inc(mask_ready, 1)
            dve.wait_ge(ex_ready, 1)
            do(dve.tensor_scalar(den[:], ex[:], 1.0, None, ALU.add))
            do(dve.reciprocal(rwt[:, 0, :], den[:]))
            do(dve.tensor_tensor(rwt[:, 1, :], ex[:], rwt[:, 0, :], ALU.mult))
            dve.wait_ge(rank_ready, 1)
            do(dve.memset(PX[:, 0, :], 0.0))
            totals = PS[5][:, 0:NT * E].rearrange("p (t e) -> p t e", t=NT)
            for t in range(NT):
                do(dve.tensor_tensor(PX[:, t + 1, :], PX[:, t, :], totals[:, t, :], ALU.add))
            do(dve.tensor_tensor(PO[:], PX[:, 0:NT, :], PS[4][:, 0:NT * E].rearrange("p (t e) -> p t e", t=NT), ALU.add))
            do(dve.tensor_scalar(cnt[:], PX[:, NT, :], (P - 1) / 2, 1 / P, ALU.add, ALU.mult))
            do(dve.tensor_copy(cnti[:], cnt[:]))
            do(dve.tensor_copy(tiles[:], cnti[:]))
            do(dve.tensor_tensor_scan(incl[:], ones[:, 0:E], tiles[:], 0.0, ALU.mult, ALU.add))
            do(dve.tensor_tensor(off[:], incl[:], tiles[:], ALU.subtract))
            do(dve.tensor_scalar(off[:], off[:], float(P), None, ALU.mult))
            do(dve.tensor_tensor(PO[:], PO[:], off[:].rearrange("p (o e) -> p o e", o=1).to_broadcast([P, NT, E]), ALU.add))
            for k in range(TOP):
                ins = dve.tensor_tensor(PSEL[:, k], OH[:, k], PO[:], ALU.mult)
            do(ins)
            for k in range(TOP):
                ins = dve.tensor_reduce(posf[:, k, :].rearrange("p (t o) -> p t o", o=1), PSEL[:, k], AX, ALU.add)
            do(ins)
            dve.tensor_copy(pos[:], posf[:]).then_inc(pos_ready, 1)
            dve.wait_ge(const_ready, 8)
            do(dve.tensor_tensor(cmpj[:], incl[:].rearrange("p (o e) -> p o e", o=1).to_broadcast([P, SLOT_TILES, E]),
                                 iota_j[:].rearrange("p (j o) -> p j o", o=1).to_broadcast([P, SLOT_TILES, E]),
                                 ALU.is_le))
            do(dve.tensor_reduce(texf[:].rearrange("p (j o) -> p j o", o=1), cmpj[:], AX, ALU.add))
            do(dve.tensor_scalar(texf[:], texf[:], float(E - 1), None, ALU.min))
            dve.tensor_copy(tile_exp[:], texf[:]).then_inc(tex_ready, 1)
            for i in range(A_RING):
                ins = dve.memset(dA[i][:, :, 0:1], 0.0)
                ins.then_inc(scan_done, 1)
            dve.sem_inc(hc_ready, BC_RING)
            dve.sem_inc(added, GROUP - 1)

            def scan(b, n):
                u = b * NS + n
                dve.wait_ge(da_ready, u + 1)
                dve.wait_ge(dbu_ready, u + (BC_RING + 1))
                s_ = S[n % S_RING]
                flat = s_[:].rearrange("p c l -> p (c l)")
                dve.tensor_tensor_scan(flat, dA[n % A_RING][:].rearrange("p c l -> p (c l)"), flat, 0.0,
                                       ALU.mult, ALU.add).then_inc(scan_done, 1)
                dve.wait_ge(cb_loaded[n % BC_RING], b * (NS // BC_RING * DMA) + (n // BC_RING + 1) * DMA)
                dve.wait_ge(scan_done, u + (A_RING + 1))
                dve.tensor_tensor(s_[:], s_[:], Cb[n % BC_RING][:].rearrange("p (o l) -> p o l", o=1).to_broadcast([P, DC, L]),
                                  ALU.mult).then_inc(hc_ready, 1)
                if n % GROUP:
                    dve.wait_ge(hc_ready, u + (BC_RING + 1))
                    if n % GROUP > 1:
                        dve.wait_ge(added, (b * (NS // GROUP) + n // GROUP) * (GROUP - 1) + (GROUP - 2 + n % GROUP))
                    dve.tensor_tensor(s_[:], s_[:], S[n % S_RING - 1][:], ALU.add).then_inc(added, 1)

            def take_y(b):
                dve.wait_ge(s_summed, b * (NS // GROUP) + (NS // GROUP + 1))
                dve.wait_ge(ul_loaded, b * DMA + DMA)
                for c in range(DC):
                    dve.scalar_tensor_tensor(DTU[:, ds(b, 1), c, :].rearrange("p b l -> p (b l)"), U[:, c, :],
                                             skip[:, c:c + 1], PS[c][:], ALU.mult, ALU.add).then_inc(y_ready, 1)

            def silu_h(j0, n):
                dve.wait_ge(tg_ready, j0 + (n + 1))
                dve.scalar_tensor_tensor(GG[n % 2][:], TG[n % 2][:], 1.0, PS[5][:, 0:F], ALU.add,
                                         ALU.mult).then_inc(gg_ready, 1)
                dve.wait_ge(gg_ready, j0 + (n + 1))
                dve.scalar_tensor_tensor(HH[n % 2][:], GG[n % 2][:], 0.5, PS[5][:, F:2 * F], ALU.mult,
                                         ALU.mult).then_inc(hh_ready, 1)

            for n in range(NS):
                scan(0, n)
                if n == NS - 4:
                    dve.wait_ge(slots_t, 1)
                    dve.tensor_copy(slot_tok[:], PS[6][:, 0:SLOT_TILES]).then_inc(slots_ready, 1)
            take_y(0)

            def mixture_steps(b, last):
                j0 = b * NS - NS
                for n in range(NS):
                    if n + 1 < NS:
                        scan(b, n + 1)
                        silu_h(j0, n + 1)
                    elif not last:
                        take_y(b)
                        scan(b + 1, 0)
                        silu_h(j0 + NS, 0)
                    else:
                        take_y(b)

            scan(1, 0)
            silu_h(0, 0)
            with dve.Fori(1, B - 1) as b:
                mixture_steps(b, False)
            mixture_steps(B - 1, True)

            dve.sem_inc(y12_used, 2)
            with step.loop(B, 4 + T + 1) as b:
                dve.wait_ge(x1_loaded, b * DMA + DMA)
                for c in range(T):
                    t = b * T + c
                    dve.wait_ge(y12_loaded[c % 2], b * (T // 2 * TOP * DMA) + (c // 2 + 1) * TOP * DMA)
                    step.mark(dve.scalar_tensor_tensor(X2[:, c, :], Y1[c % 2][:], rwt[:, 0, ds(t, 1)], X2[:, c, :],
                                                       ALU.mult, ALU.add))
                    step.wait()
                    dve.scalar_tensor_tensor(X2[:, c, :], Y2[c % 2][:], rwt[:, 1, ds(t, 1)], X2[:, c, :],
                                             ALU.mult, ALU.add).then_inc(y12_used, 1)
                dve.wait_ge(y12_used, b * T + (T + 2))
                layernorm(X2, ZN, b * 2 + 1, var2_ready, rstd2_ready, zn_ready)
                dve.wait_ge(zt_ready, b + 1)
                step.mark(dve.scalar_tensor_tensor(ZT[:], ZT[:], 1.0, ZN[:], ALU.add, ALU.mult))
                step.wait()
                dve.scalar_tensor_tensor(ZT[:], ZT[:], 0.5, DTU[:, ds(b, 1)].rearrange("p b c l -> p (b c) l"),
                                         ALU.mult, ALU.mult).then_inc(gate_ready, 1)
                for t in range(T):
                    dve.wait_ge(gt_ready, b * T + (t + 1))
                    dve.tensor_tensor(X2[:, t, :], PS[t][:], X2[:, t, :], ALU.add).then_inc(x3_ready, 1)
                dve.wait_ge(x3_ready, b * T + T)
                layernorm(X2, ZN, b * 2 + 2, var2_ready, rstd2_ready, xn3_ready)
                dve.wait_ge(lg_ready, b + 1)
                dve.tensor_copy(logits[:, ds(b * T, T), :],
                                PS[6][:, 0:T * E2].rearrange("p (t e) -> p t e", t=T)).then_inc(lg_copied, 1)
            dve.wait_ge(lg_copied, B)

            dve.wait_ge(lsum_ready, 1)
            do(dve.tensor_copy(lsum[:], PS[7][:, 0:E2]))
            do(dve.max(lmax[:], lsum[:]))
            dve.max_index(lidx[:], lmax[:], lsum[:]).then_inc(lidx_ready, 1)
            dve.wait_ge(lidx_ready, 1)
            do(dve.tensor_copy(lidf[:], lidx[:, 0:TOP]))
            for k in range(TOP):
                ins = dve.tensor_scalar(loh[:, k, :], iota_e[:, 0:E2], lidf[:, k:k + 1], None, ALU.is_equal)
            do(ins)
            for k in range(TOP):
                ins = dve.tensor_tensor(ltmp[:, k], logits[:], loh[:, k:k + 1, :].to_broadcast([P, NT, E2]), ALU.mult)
            do(ins)
            for k in range(TOP):
                ins = dve.tensor_reduce(lsel[:, k, :].rearrange("p (t o) -> p t o", o=1), ltmp[:, k], AX, ALU.add)
            do(ins)
            do(dve.tensor_tensor(lme[:], lsel[:, 0, :], lsel[:, 1, :], ALU.max))
            dve.tensor_tensor(lsel[:], lsel[:], lme[:].rearrange("p (o t) -> p o t", o=1).to_broadcast([P, TOP, NT]),
                              ALU.subtract).then_inc(lme_ready, 1)
            dve.wait_ge(lexp_ready, 1)
            do(dve.tensor_tensor(lden[:], lsel[:, 0, :], lsel[:, 1, :], ALU.add))
            do(dve.reciprocal(lme[:], lden[:]))
            dve.tensor_tensor(rwf[:], lsel[:], lme[:].rearrange("p (o t) -> p o t", o=1).to_broadcast([P, TOP, NT]),
                              ALU.mult).then_inc(rwf_ready, 1)

            dve.sem_inc(y2_added, 1)
            with dve.Fori(0, B) as tb:
                dve.wait_ge(xs_loaded, tb * DMA + DMA)
                dve.wait_ge(up2_ready, tb * (TOP * FT) + 2)
                dve.tensor_copy(XSH[:], XS[:]).then_inc(xsh_ready, 1)
                dve.wait_ge(xsh_ready, tb + 1)
                dve.tensor_tensor(XSL[:], XS[:], XSH[:].bitcast(F32), ALU.subtract).then_inc(xs_split, 1)
                with dve.Fori(0, TOP) as e:
                    it = dve.snap(tb * (TOP * FT) + e * FT)
                    for f in range(FT):
                        dve.wait_ge(hf_ready, it + (f + 1))
                        dve.tensor_copy(HFH[f % 2][:], HF[f % 2][:]).then_inc(hfh_ready, 1)
                        dve.wait_ge(hfh_ready, it + (f + 1))
                        dve.tensor_tensor(HFL[f % 2][:], HF[f % 2][:], HFH[f % 2][:].bitcast(F32),
                                          ALU.subtract).then_inc(hfl_ready, 1)
                    dve.wait_ge(o_loaded, tb * DMA + DMA)
                    dve.wait_ge(b1_loaded, 2 * TOP * DMA)
                    for t in range(T):
                        w = rwf[:, ds(e, 1), ds(tb * T + t, 1)].rearrange("p e t -> p (e t)")
                        dve.scalar_tensor_tensor(O[:, t, :], b2b[:, ds(e, 1), :].rearrange("p e d -> p (e d)"), w,
                                                 O[:, t, :], ALU.mult, ALU.add).then_inc(ob_ready, 1)
                    dve.wait_ge(down2_done, it + (FT + 2))
                    for t in range(T):
                        w = rwf[:, ds(e, 1), ds(tb * T + t, 1)].rearrange("p e t -> p (e t)")
                        dve.wait_ge(ob_ready, tb * (TOP * T) + e * T + (t + 1))
                        ins = dve.scalar_tensor_tensor(O[:, t, :], PS[t][:], w, O[:, t, :], ALU.mult, ALU.add)
                    ins.then_inc(y2_added, 1)
                    dve.wait_ge(y2_added, tb * TOP + e + 2)

        @block.tensor
        def _(pe):
            pe.wait_ge(nat_loaded, NAT_LOADS * DMA)
            pe.wait_ge(const_ready, 2)
            for i, (srcs, parts_in, parts, dst) in enumerate(setup):
                if i >= 2:
                    pe.wait_ge(set_c, i - 1)
                if i == len(setup) - 2 * B:
                    pe.wait_ge(ctx_loaded, DMA)
                w = dst.shape[1] // len(srcs)
                for k, src in enumerate(srcs):
                    ins = pe.transpose(PS[4 + i % 2][0:parts, k * w:(k + 1) * w], src, ident[0:parts_in, 0:parts_in])
                ins.then_inc(set_t, 1)

            pe.wait_ge(set_c, len(setup))
            with pe.Fori(0, B) as b:
                for c in range(DC):
                    for k in range(CK):
                        ins = pe.matmul(PS[c][:], inT[:, k, c * P:(c + 1) * P], ctxT[:, k, ds(b * L, L)],
                                        start=(k == 0), stop=(k == CK - 1))
                    ins.then_inc(xin_ready, 1)
                pe.wait_ge(u_ready, b + 1)
                for c in range(DC):
                    ins = pe.matmul(PS[4][0:XD, :], xpT[:, c, :], U[:, c, :], start=(c == 0), stop=(c == DC - 1))
                ins.then_inc(xd_ready, 1)
                pe.wait_ge(xd_copied, b + 1)
                for c in range(DC):
                    pe.matmul(PS[c][:], dtpT[:, c * P:(c + 1) * P], xdb[0:R, :],
                              start=True, stop=True).then_inc(dtp_ready, 1)
                pe.wait_ge(z_ready, b + 1)
                pe.wait_ge(r_ready, b * DC + DC)

            def four_transposes(src, i, count):
                for k in range(K):
                    ins = pe.transpose(PS[4 + i % 2][:, k * P:(k + 1) * P], src[:, k * P:(k + 1) * P], ident[:])
                ins.then_inc(count, 1)

            with pe.Fori(0, B) as b:
                for w in range(2):
                    for k in range(CK):
                        ins = pe.matmul(PS[6 + w][:], wqkT[:, w, k, :], ctxT[:, k, ds(b * L, L)],
                                        start=(k == 0), stop=(k == CK - 1))
                ins.then_inc(qk_ready, 1)
                pe.wait_ge(xn_ready, b + 1)
                for t in range(T):
                    if t >= 2:
                        pe.wait_ge(t_copied, b * 12 + (t - 1))
                    four_transposes(XN[:, t, :], t, t_ready)
                pe.wait_ge(qk_copied, b * 2 + 2)
                for t in range(T):
                    if t >= 2:
                        pe.wait_ge(exp_ready, b * T + (t - 1))
                    pe.matmul(PS[6 + t % 2][:], QKT[:, 0, t * P:(t + 1) * P], QKT[:, 1, :],
                              start=True, stop=True).then_inc(e_ready, 1)
                for t in range(T):
                    pe.wait_ge(p_ready, b * T + (t + 1))
                    pe.wait_ge(t_copied, b * 12 + (T + t - 1))
                    four_transposes(PR[:, t, :], t, t_ready)
                pe.wait_ge(t_copied, b * 12 + 2 * T)
                for t in range(T):
                    if t >= 2:
                        pe.wait_ge(x1_ready, b * T + (t - 1))
                    for k in range(K):
                        ins = pe.matmul(PS[6 + t % 2][:], XNT[:, k, t * P:(t + 1) * P], ATT[:, k, :],
                                        start=(k == 0), stop=(k == K - 1))
                    ins.then_inc(o_ready, 1)
                pe.wait_ge(xn1_ready, b + 1)
                for t in range(T):
                    pe.wait_ge(t_copied, b * 12 + (2 * T + t - 1))
                    four_transposes(XN[:, t, :], t, t_ready)
                pe.wait_ge(t_copied, b * 12 + 3 * T)
                for t in range(T):
                    for k in range(K):
                        ins = pe.matmul(PS[6][:, t * E:(t + 1) * E], XNT[:, k, t * P:(t + 1) * P], routerW[:, k, :],
                                        start=(k == 0), stop=(k == K - 1))
                ins.then_inc(score_ready, 1)
                pe.wait_ge(score_copied, b + 1)

            pe.wait_ge(mask_ready, 1)
            pe.wait_ge(const_ready, 6)
            pe.matmul(PS[4][:, 0:NT * E], tri[:], MM[:].rearrange("p t e -> p (t e)"), start=True, stop=True)
            pe.matmul(PS[5][:, 0:NT * E], ones[:], MM[:].rearrange("p t e -> p (t e)"), start=True,
                      stop=True).then_inc(rank_ready, 1)

            pe.sem_inc(s_summed, 1)
            pe.sem_inc(xgt_ready, 2)
            pe.sem_inc(up_ready, 2)
            pe.sem_inc(down_ready, 2)

            def add_group(b, n):
                pe.wait_ge(added, (b * (NS // GROUP) + n // GROUP) * (GROUP - 1) + 2 * (GROUP - 1))
                if n == GROUP - 1 and not isinstance(b, int):
                    pe.wait_ge(y_ready, b * DC)
                for c in range(DC):
                    ins = pe.matmul(PS[c][:], ident[:], S[n % S_RING][:, c, :], start=(n == GROUP - 1), stop=(n == NS - 1))
                ins.then_inc(s_summed, 1)

            def turn_x(j0, n):
                xg = XG[n % 2][:].rearrange("p (q k) -> p k q", k=K)
                pe.wait_ge(xg_loaded[n % 2], block_of(j0, DMA) + (n // 2 + 1) * DMA)
                if not (isinstance(j0, int) and j0 + n == 0):
                    pe.wait_ge(xgt_copied, j0 + n)
                for k in range(K):
                    ins = pe.transpose(PS[4][:, k * P:(k + 1) * P], xg[:, k, :], ident[:])
                ins.then_inc(xgt_ready, 1)

            def up(j0, n):
                pe.wait_ge(xgt_copied, j0 + (n + 1))
                pe.wait_ge(gu_loaded[n % 2], block_of(j0, 2 * DMA) + (n // 2 + 1) * 2 * DMA)
                for k in range(K):
                    ins = pe.matmul(PS[5][:, 0:2 * F], XGT[n % 2][:, k, :],
                                    WGU[n % 2][:, k].rearrange("p g f -> p (g f)"), start=(k == 0), stop=(k == K - 1))
                ins.then_inc(up_ready, 1)

            def turn_h(j0, n):
                hh = HH[n % 2][:].rearrange("p (q k) -> p k q", k=2)
                pe.wait_ge(hh_ready, j0 + (n + 1))
                for k in range(2):
                    ins = pe.transpose(PS[6][0:FH, k * P:(k + 1) * P], hh[:, k, :], ident[:])
                ins.then_inc(ht_ready, 1)

            def down(j0, n):
                pe.wait_ge(ht_copied, j0 + (n + 1))
                pe.wait_ge(wd_loaded[n % 2], block_of(j0, DMA) + (n // 2 + 1) * DMA)
                pe.wait_ge(yt_ready, j0 + (n + 1))
                for k in range(2):
                    ins = pe.matmul(PS[7][:], HT[n % 2][:, k, :], WD[n % 2][:, k, :], start=(k == 0), stop=(k == 1))
                ins.then_inc(down_ready, 1)

            def block_of(j0, per):
                return j0 * (per // 2)

            def mixture_steps(b, last):
                j0 = b * NS - NS
                for n in range(NS):
                    turn_h(j0, n)
                    if n + 2 < NS:
                        turn_x(j0, n + 2)
                    elif not last:
                        turn_x(j0 + NS, n + 2 - NS)
                    if n + 1 < NS:
                        up(j0, n + 1)
                    elif not last:
                        up(j0 + NS, 0)
                    down(j0, n)
                    if n % GROUP == GROUP - 1:
                        add_group(b, n)

            for n in range(NS):
                if n % GROUP == GROUP - 1:
                    add_group(0, n)
                if n == NS - 5:
                    pe.wait_ge(slots_loaded, DMA)
                    pe.transpose(PS[6][:, 0:SLOT_TILES], slotf[:], ident[0:SLOT_TILES, 0:SLOT_TILES]).then_inc(slots_t, 1)
            pe.wait_ge(slots_ready, 1)
            turn_x(0, 0)
            up(0, 0)
            turn_x(0, 1)
            with pe.Fori(1, B - 1) as b:
                mixture_steps(b, False)
            mixture_steps(B - 1, True)

            with pe.Fori(0, B) as b:
                pe.wait_ge(gate_ready, b + 1)
                for t in range(T):
                    for c in range(DC):
                        ins = pe.transpose(PS[t][:, c * P:(c + 1) * P], ZT[:, c, t * P:(t + 1) * P], ident[:])
                    ins.then_inc(gt_ready, 1)
                pe.wait_ge(xn3_ready, b + 1)
                for t in range(T):
                    if t >= 2:
                        pe.wait_ge(t3_copied, b * T + (t - 1))
                    four_transposes(ZN[:, t, :], t, t3_ready)
                pe.wait_ge(t3_copied, b * T + T)
                for t in range(T):
                    for k in range(K):
                        ins = pe.matmul(PS[6][:, t * E2:(t + 1) * E2], XT3[:, k, t * P:(t + 1) * P], gate2T[:, k, :],
                                        start=(k == 0), stop=(k == K - 1))
                ins.then_inc(lg_ready, 1)
                pe.wait_ge(lg_copied, b + 1)
            pe.wait_ge(lg_copied, B)
            for t in range(NT):
                ins = pe.matmul(PS[7][:, 0:E2], ones[:], logits[:, t, :], start=(t == 0), stop=(t == NT - 1))
            ins.then_inc(lsum_ready, 1)

            pe.wait_ge(b1_loaded, 2 * TOP * DMA)
            for k in range(TOP):
                ins = pe.transpose(PS[6][:, k * FT:(k + 1) * FT], b1n[:, k, :], ident[0:FT, 0:FT])
            ins.then_inc(b1_t, 1)
            pe.sem_inc(up2_ready, 2)
            pe.sem_inc(down2_done, 2)
            with pe.Fori(0, B) as tb:
                wait_apart(pe, xs_split, tb + 1)
                with pe.Fori(0, TOP) as e:
                    it = pe.snap(tb * (TOP * FT) + e * FT)

                    def up(f):
                        pe.wait_ge(w1l_ready, it + (f + 1))
                        for k in range(K):
                            for i, (w, v) in enumerate(((W1H, XSH), (W1H, XSL), (W1L, XSH))):
                                ins = pe.matmul(PS[4 + f % 2][:], w[f % 2][:, k, :], v[:, k, :],
                                                start=(k == 0 and i == 0), stop=(k == K - 1 and i == 2))
                        ins.then_inc(up2_ready, 1)

                    def down(f):
                        pe.wait_ge(hfl_ready, it + (f + 1))
                        pe.wait_ge(w2l_ready, it + (f + 1))
                        if f == 0:
                            pe.wait_ge(y2_added, tb * TOP + e + 1)
                        for t in range(T):
                            for i, (u_, w) in enumerate(((HFH, W2H), (HFH, W2L), (HFL, W2H))):
                                ins = pe.matmul(PS[t][:], u_[f % 2][:, t * P:(t + 1) * P], w[f % 2][:],
                                                start=(f == 0 and i == 0), stop=(f == FT - 1 and i == 2))
                        ins.then_inc(down2_done, 1)

                    up(0)
                    for f in range(FT):
                        if f + 1 < FT:
                            up(f + 1)
                        down(f)


_INS = ['x', 'ctx_1024', 'L0_xattn_Wq', 'L0_xattn_bq', 'L0_xattn_Wk', 'L0_xattn_bk', 'L0_ffn_router_w',
        'L0_ffn_gate_w', 'L0_ffn_up_w', 'L0_ffn_down_w', 'L1_xattn_in_proj_w', 'L1_xattn_conv_w',
        'L1_xattn_conv_b', 'L1_xattn_x_proj_w', 'L1_xattn_dt_proj_w', 'L1_xattn_dt_proj_b', 'L1_xattn_A_log',
        'L1_xattn_D', 'L1_ffn_gate_w', 'L1_ffn_w1', 'L1_ffn_b1', 'L1_ffn_w2', 'L1_ffn_b2']


def kernel(**inputs):
    import numpy as _np
    import concourse.bacc as _bacc
    from concourse import mybir as _mybir
    from concourse.bass_utils import run_bass_kernel_spmd as _run

    nc = _bacc.Bacc("TRN2", target_bir_lowering=False, num_devices=1)
    arrays, args = {}, []
    for name in _INS:
        a = _np.ascontiguousarray(inputs[name])
        arrays[f"in_{name}"] = a
        args.append(nc.dram_tensor(f"in_{name}", a.shape, _mybir.dt.from_np(a.dtype), kind="ExternalInput").ap())
    args.append(nc.dram_tensor("out_x", inputs["x"].shape, _mybir.dt.float32, kind="ExternalOutput").ap())
    build_program(nc, *args)
    r = _run(nc, [arrays], core_ids=[0])
    return r.results[0]["out_x"]
```

```python
from contextlib import ExitStack, contextmanager

import concourse.bass as bass
from concourse import mybir

ALU = mybir.AluOpType
ACT = mybir.ActivationFunctionType
AX = mybir.AxisListType.X
F32 = mybir.dt.float32
F32R = mybir.dt.float32r
I32 = mybir.dt.int32
U32 = mybir.dt.uint32
ds = bass.ds

P = 128
EPS = 1e-5
TOP = 2
DMA = 16
A_RING = 2
S_RING = 4
BC_RING = 4
GROUP = 4
AHEAD = 2
WQ = 4


class Steps:

    def __init__(self, eng, sem):
        self.eng, self.sem, self.n, self.base = eng, sem, 0, 0

    def mark(self, ins):
        ins.then_inc(self.sem, 1)
        self.n += 1

    def wait(self, apart=None):
        if apart:
            apart(self.eng, self.sem, self.base + self.n)
        else:
            self.eng.wait_ge(self.sem, self.base + self.n)

    @contextmanager
    def loop(self, trips, per):
        before = self.n
        with self.eng.Fori(0, trips) as i:
            self.base = i * per
            yield i
        assert self.n - before == per, f"{self.n - before} steps in the body, not {per}"
        self.base, self.n = 0, before + trips * per


def build_program(nc, x, ctx, Wq, bq, Wk, bk, router_w, gate_w, up_w, down_w, in_w, conv_w, conv_b,
                  xp_w, dtp_w, dtp_b, A_log, D_skip, gate2_w, w1, b1, w2, b2, out):
    B, L, DM = x.shape
    C = ctx.shape[2]
    CK = C // P
    T = L // P
    NT = B * T
    K = DM // P
    E, _, F = gate_w.shape
    FH = F // 2
    NS = A_log.shape[1]
    DI = in_w.shape[0]
    DC = DI // P
    R = dtp_w.shape[1]
    TAPS = conv_w.shape[2]
    XD = R + 2 * NS
    E2, _, FF = w1.shape
    FT = FF // P
    SLOT_TILES = B * L * TOP // P + E
    SLOTS = SLOT_TILES * P
    assert DI == DM == L and SLOT_TILES == (B - 1) * NS and F == 2 * FH and TAPS == 4 and E == NS

    def dram(name, shape):
        return nc.dram_tensor(name, shape, F32, kind="Internal").ap()

    u_dram = dram("u_spill", [B, P, DC * L])
    bc_dram = dram("bc_rows", [B, 2 * NS, L])
    x1_dram = dram("x1_spill", [NT, P, DM])
    xn_dram = dram("xn_rows", [B * L, DM])
    y_dram = dram("expert_rows", [SLOTS, DM])
    slot_dram = dram("slot_tokens", [SLOTS, 1])
    x3_dram = dram("x3_spill", [NT, P, DM])
    xt_dram = dram("xt_spill", [B, P, K * L])

    top = ExitStack()
    with top:
        def sem(name):
            return top.enter_context(nc.semaphore(name))

        def sb(stack, name, shape, dt=F32):
            return stack.enter_context(nc.sbuf_tensor(name, shape, dt))

        PS = [top.enter_context(nc.psum_tensor(f"bank{i}", [P, 512], F32)) for i in range(8)]


        ident = sb(top, "ident", [P, P])
        ones = sb(top, "ones", [P, P])
        gate2T = sb(top, "gate2T", [P, K, E2])
        minus_half = sb(top, "minus_half", [P, T])
        stats = sb(top, "stats", [P, T, 6])
        mv = sb(top, "mv", [P, T, 2])
        vare = sb(top, "vare", [P, T])
        rstd = sb(top, "rstd", [P, T])
        norm = (stats, mv, vare, rstd)
        iota_e = sb(top, "iota_e", [P, E])
        logits = sb(top, "logits", [P, NT, E2])
        rwf = sb(top, "rwf", [P, TOP, NT])
        lidx = sb(top, "lidx", [P, 8], U32)

        a = ExitStack()
        DT = sb(a, "DT", [P, B, DC, L])
        DTU = sb(a, "DTU", [P, B, DC, L])
        ctxT = sb(a, "ctxT", [P, CK, B * L])
        U = sb(a, "U", [P, DC, L])
        wqkT = sb(a, "wqkT", [P, 2, CK, P])
        routerW = sb(a, "routerW", [P, K, E])
        qkb = sb(a, "qkb", [P, 2])
        convW = sb(a, "convW", [P, DC, TAPS])
        convB = sb(a, "convB", [P, DC])
        dtB = sb(a, "dtB", [P, DC])
        skip = sb(a, "skip", [P, DC])
        negA = sb(a, "negA", [P, DC, NS])
        SC = sb(a, "SC", [P, NT, E])
        rwt = sb(a, "rwt", [P, TOP, NT])
        pos = sb(a, "pos", [P, TOP, NT], I32)
        slot_tok = sb(a, "slot_tok", [P, SLOT_TILES], I32)
        tile_exp = sb(a, "tile_exp", [P, SLOT_TILES], I32)
        pcol = [sb(a, f"pcol{k}", [P, T], I32) for k in range(TOP)]

        s = ExitStack()
        zslots = sb(s, "zslots", [SLOT_TILES, P])
        XP = sb(s, "XP", [P, DC, L + TAPS - 1])
        XH = sb(s, "XH", [P, DC, L])
        ZZ = sb(s, "ZZ", [P, DC, L])
        ND = sb(s, "ND", [P, DC, L])
        RL = sb(s, "RL", [P, DC, L])
        xdb = sb(s, "xdb", [XD, L])
        inT = sb(s, "inT", [P, CK, DI])
        xpT = sb(s, "xpT", [P, DC, XD])
        dtpT = sb(s, "dtpT", [R, DI])

        w = ExitStack()
        nat_qk = sb(w, "nat_qk", [P, 2, C])
        nat_in = sb(w, "nat_in", [P, DC, C])
        nat_xp = sb(w, "nat_xp", [XD, DI])
        nat_dtp = sb(w, "nat_dtp", [P, DC, R])
        nat_g2 = sb(w, "nat_g2", [E2, DM])
        nat_A = sb(w, "nat_A", [P, DC, NS])
        nat_ctx = sb(w, "nat_ctx", [P, NT, C])
        w.close()

        q = ExitStack()
        QKT = sb(q, "QKT", [P, 2, L])
        XNT = sb(q, "XNT", [P, K, L])
        ATT = sb(q, "ATT", [P, K, L])
        PR = sb(q, "PR", [P, T, L])
        X1A = sb(q, "X1A", [P, T, DM])
        XN1 = sb(q, "XN1", [P, T, DM])
        XN = sb(q, "XN", [P, T, DM])
        XB = sb(q, "XB", [P, T, DM])
        nmax = sb(q, "nmax", [P, T])
        nneg = sb(q, "nneg", [P, T])
        rsum = sb(q, "rsum", [P, T])
        rinv = sb(q, "rinv", [P, T])
        q.close()
        s.close()

        m = ExitStack()
        dA = [sb(m, f"dA{i}", [P, DC, L]) for i in range(A_RING)]
        S = [sb(m, f"S{i}", [P, DC, L]) for i in range(S_RING)]
        Bb = [sb(m, f"Bb{i}", [P, L]) for i in range(BC_RING)]
        Cb = [sb(m, f"Cb{i}", [P, L]) for i in range(BC_RING)]

        r = ExitStack()
        tri = sb(r, "tri", [P, P])
        M8 = sb(r, "M8", [P, NT, 8])
        I8 = sb(r, "I8", [P, NT, 8], U32)
        IF = sb(r, "IF", [P, TOP, NT])
        OH = sb(r, "OH", [P, TOP, NT, E])
        MM = sb(r, "MM", [P, NT, E])
        PX = sb(r, "PX", [P, NT + 1, E])
        PO = sb(r, "PO", [P, NT, E])
        PSEL = sb(r, "PSEL", [P, TOP, NT, E])
        posf = sb(r, "posf", [P, TOP, NT])
        cnt = sb(r, "cnt", [P, E])
        cnti = sb(r, "cnti", [P, E], I32)
        tiles = sb(r, "tiles", [P, E])
        incl = sb(r, "incl", [P, E])
        off = sb(r, "off", [P, E])
        iota_j = sb(r, "iota_j", [P, SLOT_TILES])
        cmpj = sb(r, "cmpj", [P, SLOT_TILES, E])
        texf = sb(r, "texf", [P, SLOT_TILES])
        tokid = sb(r, "tokid", [P, NT])
        diff = sb(r, "diff", [P, NT])
        ex = sb(r, "ex", [P, NT])
        den = sb(r, "den", [P, NT])
        slotf = sb(r, "slotf", [SLOT_TILES, P])
        r.close()

        f = ExitStack()
        WGU = [sb(f, f"WGU{i}", [P, K, 2, F]) for i in range(2)]
        WD = [sb(f, f"WD{i}", [FH, 2, DM]) for i in range(2)]
        XG = [sb(f, f"XG{i}", [P, DM]) for i in range(2)]
        XGT = [sb(f, f"XGT{i}", [P, K, P]) for i in range(2)]
        gcol = [sb(f, f"gcol{i}", [P, 1], I32) for i in range(2)]
        TG = [sb(f, f"TG{i}", [P, F]) for i in range(2)]
        GG = [sb(f, f"GG{i}", [P, F]) for i in range(2)]
        HH = [sb(f, f"HH{i}", [P, F]) for i in range(2)]
        HT = [sb(f, f"HT{i}", [FH, 2, P]) for i in range(2)]
        YT = [sb(f, f"YT{i}", [P, DM]) for i in range(2)]
        f.close()
        m.close()

        g = ExitStack()
        X1 = sb(g, "X1", [P, T, DM])
        X2 = sb(g, "X2", [P, T, DM])
        X3 = sb(g, "X3", [P, T, DM])
        Y1 = sb(g, "Y1", [P, T, DM])
        Y2 = sb(g, "Y2", [P, T, DM])
        ZN = sb(g, "ZN", [P, T, DM])
        ZT = sb(g, "ZT", [P, T, DM])
        ZN3 = sb(g, "ZN3", [P, T, DM])
        XT3 = sb(g, "XT3", [P, K, L])
        norm3 = (sb(g, "stats3", [P, T, 6]), sb(g, "mv3", [P, T, 2]), sb(g, "vare3", [P, T]), sb(g, "rstd3", [P, T]))
        lsum = sb(g, "lsum", [P, E2])
        lmax = sb(g, "lmax", [P, 8])
        lidf = sb(g, "lidf", [P, TOP])
        lsel = sb(g, "lsel", [P, TOP, NT])
        loh = sb(g, "loh", [P, TOP, E2])
        ltmp = sb(g, "ltmp", [P, TOP, NT, E2])
        lme = sb(g, "lme", [P, NT])
        lden = sb(g, "lden", [P, NT])
        g.close()
        a.close()

        h = ExitStack()
        W1R = sb(h, "W1R", [P, TOP, K, FF])
        W2R = sb(h, "W2R", [P, TOP, FT, DM])
        W1H = [sb(h, f"W1H{i}", [P, K, P], F32R) for i in range(2)]
        W1L = [sb(h, f"W1L{i}", [P, K, P], F32R) for i in range(2)]
        W2H = [sb(h, f"W2H{i}", [P, DM], F32R) for i in range(2)]
        W2L = [sb(h, f"W2L{i}", [P, DM], F32R) for i in range(2)]
        XS = sb(h, "XS", [P, K, L])
        XSH = sb(h, "XSH", [P, K, L], F32R)
        XSL = sb(h, "XSL", [P, K, L], F32R)
        HF = [sb(h, f"HF{i}", [P, L]) for i in range(2)]
        HFH = [sb(h, f"HFH{i}", [P, L], F32R) for i in range(2)]
        HFL = [sb(h, f"HFL{i}", [P, L], F32R) for i in range(2)]
        O = sb(h, "O", [P, T, DM])
        b1n = sb(h, "b1n", [FT, TOP, P])
        b1T = sb(h, "b1T", [P, TOP, FT])
        b2b = sb(h, "b2b", [P, TOP, DM])
        h.close()

        nat_loaded = sem("nat_loaded")
        ctx_loaded = sem("ctx_loaded")
        slots_zeroed = sem("slots_zeroed")
        const_ready = sem("const_ready")
        pool_step = sem("pool_step")
        dve_step = sem("dve_step")
        small_ready = sem("small_ready")
        set_t = sem("set_t")
        set_c = sem("set_c")
        xin_ready = sem("xin_ready")
        xp_ready = sem("xp_ready")
        xh_ready = sem("xh_ready")
        u_ready = sem("u_ready")
        u_spilled = sem("u_spilled")
        xd_ready = sem("xd_ready")
        xd_copied = sem("xd_copied")
        bc_stored = sem("bc_stored")
        dtp_ready = sem("dtp_ready")
        abs_ready = sem("abs_ready")
        z_ready = sem("z_ready")
        r_ready = sem("r_ready")
        w_ready = sem("w_ready")
        ln_ready = sem("ln_ready")
        dt_ready = sem("dt_ready")

        xb_loaded = sem("xb_loaded")
        var_ready = sem("var_ready")
        rstd_ready = sem("rstd_ready")
        xn_ready = sem("xn_ready")
        qk_ready = sem("qk_ready")
        qk_copied = sem("qk_copied")
        t_ready = sem("t_ready")
        t_copied = sem("t_copied")
        e_ready = sem("e_ready")
        nneg_ready = sem("nneg_ready")
        exp_ready = sem("exp_ready")
        p_ready = sem("p_ready")
        o_ready = sem("o_ready")
        x1_ready = sem("x1_ready")
        x1_stored = sem("x1_stored")
        xn1_ready = sem("xn1_ready")
        xn1_stored = sem("xn1_stored")
        score_ready = sem("score_ready")
        score_copied = sem("score_copied")

        mask_ready = sem("mask_ready")
        rank_ready = sem("rank_ready")
        diff_ready = sem("diff_ready")
        ex_ready = sem("ex_ready")
        pos_ready = sem("pos_ready")
        tex_ready = sem("tex_ready")
        slots_set = sem("slots_set")
        slots_loaded = sem("slots_loaded")
        slots_t = sem("slots_t")
        slots_ready = sem("slots_ready")

        bb_loaded = [sem(f"bb_loaded{i}") for i in range(BC_RING)]
        cb_loaded = [sem(f"cb_loaded{i}") for i in range(BC_RING)]
        ul_loaded = sem("ul_loaded")
        da_ready = sem("da_ready")
        dbu_ready = sem("dbu_ready")
        scan_done = sem("scan_done")
        hc_ready = sem("hc_ready")
        added = sem("added")
        s_summed = sem("s_summed")
        y_ready = sem("y_ready")

        gu_loaded = [sem(f"gu_loaded{i}") for i in range(2)]
        wd_loaded = [sem(f"wd_loaded{i}") for i in range(2)]
        gcol_ready = sem("gcol_ready")
        xg_loaded = [sem(f"xg_loaded{i}") for i in range(2)]
        xgt_ready = sem("xgt_ready")
        xgt_copied = sem("xgt_copied")
        up_ready = sem("up_ready")
        tg_ready = sem("tg_ready")
        gg_ready = sem("gg_ready")
        hh_ready = sem("hh_ready")
        ht_ready = sem("ht_ready")
        ht_copied = sem("ht_copied")
        down_ready = sem("down_ready")
        yt_ready = sem("yt_ready")
        yt_stored = sem("yt_stored")

        x1_loaded = sem("x1_loaded")
        pcol_ready = sem("pcol_ready")
        y_loaded = [sem(f"y{k}_loaded") for k in range(TOP)]
        part_ready = sem("part_ready")
        x2_ready = sem("x2_ready")
        var2_ready = sem("var2_ready")
        rstd2_ready = sem("rstd2_ready")
        var3_ready = sem("var3_ready")
        rstd3_ready = sem("rstd3_ready")
        zn_ready = sem("zn_ready")
        zt_ready = sem("zt_ready")
        gate_ready = sem("gate_ready")
        gt_ready = sem("gt_ready")
        x3_ready = sem("x3_ready")
        x3_stored = sem("x3_stored")
        xn3_ready = sem("xn3_ready")
        t3_ready = sem("t3_ready")
        t3_copied = sem("t3_copied")
        xt3_stored = sem("xt3_stored")
        lg_ready = sem("lg_ready")
        lg_copied = sem("lg_copied")
        lsum_ready = sem("lsum_ready")
        lidx_ready = sem("lidx_ready")
        lme_ready = sem("lme_ready")
        lexp_ready = sem("lexp_ready")
        rwf_ready = sem("rwf_ready")

        wq_loaded = [sem(f"wq_loaded{i}") for i in range(WQ)]
        b1_loaded = sem("b1_loaded")
        b1_t = sem("b1_t")
        b1_ready = sem("b1_ready")
        xs_loaded = sem("xs_loaded")
        xs_split = sem("xs_split")
        w1h_ready = sem("w1h_ready")
        w1l_ready = sem("w1l_ready")
        w2h_ready = sem("w2h_ready")
        w2l_ready = sem("w2l_ready")
        xsh_ready = sem("xsh_ready")
        hfh_ready = sem("hfh_ready")
        ob_ready = sem("ob_ready")
        up2_ready = sem("up2_ready")
        hf_ready = sem("hf_ready")
        hfl_ready = sem("hfl_ready")
        down2_done = sem("down2_done")
        y2_added = sem("y2_added")
        o_loaded = sem("o_loaded")
        o_final = sem("o_final")
        out_stored = sem("out_stored")

        wait_regs = {}

        def wait_apart(eng, sem_, value):
            if not isinstance(value, int):
                reg = wait_regs.setdefault(eng.engine, None) or eng.alloc_register(f"wait_value_{len(wait_regs)}")
                wait_regs[eng.engine] = reg
                eng.reg_mov(reg, value)
                eng.wait_ge(const_ready, 2)
                value = reg
            eng.wait_ge(sem_, value)

        def bank(i, parts, cols):
            return PS[i][0:parts, 0:cols]

        setup = [
            ([nat_qk[:, w, k * P:(k + 1) * P] for w in range(2) for k in range(CK)], P,
             P, wqkT[:].rearrange("p w k c -> p (w k c)")),
            *[([nat_in[:, c, k * P:(k + 1) * P] for c in range(DC)], P, P, inT[:, k, :]) for k in range(CK)],
            ([nat_xp[:, c * P:(c + 1) * P] for c in range(DC)], XD, P, xpT[:].rearrange("p c x -> p (c x)")),
            ([nat_dtp[:, c, :] for c in range(DC)], P, R, dtpT[:]),
            ([nat_g2[:, k * P:(k + 1) * P] for k in range(K)], E2, P, gate2T[:].rearrange("p k e -> p (k e)")),
            *[([nat_ctx[:, b * T + t, k * P:(k + 1) * P] for t in range(T)], P, P,
               ctxT[:, k, b * L:(b + 1) * L]) for b in range(B) for k in range(CK)],
        ]
        NAT_LOADS = 14

        block = top.enter_context(nc.Block())

        @block.sync
        def _(sp):
            with nc.allow_non_contiguous_dma(reason="a few hundred words of weights"):
                sp.dma_start(nat_qk[:, 0, :], Wq).then_inc(nat_loaded, DMA)
                sp.dma_start(nat_qk[:, 1, :], Wk).then_inc(nat_loaded, DMA)
                sp.dma_start(nat_in[:], in_w.rearrange("(c p) k -> p c k", p=P)).then_inc(nat_loaded, DMA)
                sp.dma_start(nat_ctx[:], ctx.rearrange("b (t p) c -> p (b t) c", p=P)).then_inc(ctx_loaded, DMA)
                sp.dma_start(nat_xp[:], xp_w).then_inc(nat_loaded, DMA)
                sp.dma_start(nat_dtp[:], dtp_w.rearrange("(c p) r -> p c r", p=P)).then_inc(nat_loaded, DMA)
                sp.dma_start(nat_g2[:], gate2_w).then_inc(nat_loaded, DMA)
                sp.dma_start(nat_A[:], A_log.rearrange("(c p) n -> p c n", p=P)).then_inc(nat_loaded, DMA)
                sp.dma_start(convW[:], conv_w.rearrange("(c p) o t -> p c (o t)", p=P)).then_inc(nat_loaded, DMA)
                sp.dma_start(convB[:], conv_b.rearrange("(c p) -> p c", p=P)).then_inc(nat_loaded, DMA)
                sp.dma_start(dtB[:], dtp_b.rearrange("(c p) -> p c", p=P)).then_inc(nat_loaded, DMA)
                sp.dma_start(skip[:], D_skip.rearrange("(c p) -> p c", p=P)).then_inc(nat_loaded, DMA)
                sp.dma_start(qkb[:, 0:1], bq.rearrange("(p o) -> p o", o=1)).then_inc(nat_loaded, DMA)
                sp.dma_start(qkb[:, 1:2], bk.rearrange("(p o) -> p o", o=1)).then_inc(nat_loaded, DMA)
                sp.dma_start(routerW[:], router_w.rearrange("(k p) e -> p k e", p=P)).then_inc(nat_loaded, DMA)
                sp.wait_ge(const_ready, 1)
                sp.dma_start(slot_dram.rearrange("(j p) o -> j (p o)", p=P), zslots[:]).then_inc(slots_zeroed, DMA)

            def load_x(b):
                sp.dma_start(XB[:], x[ds(b, 1)].rearrange("b (t p) d -> p (b t) d", p=P)).then_inc(xb_loaded, DMA)

            def sequence_transfers(b, last):
                sp.wait_ge(u_ready, b + 1)
                sp.dma_start(u_dram[ds(b, 1)].rearrange("b p f -> (b p) f"),
                             U[:].rearrange("p c l -> p (c l)")).then_inc(u_spilled, DMA)
                sp.wait_ge(x1_ready, (b + 1) * T)
                if not last:
                    load_x(b + 1)
                sp.dma_start(x1_dram[ds(b * T, T)].rearrange("t p d -> p t d"), X1A[:]).then_inc(x1_stored, DMA)
                sp.wait_ge(xd_copied, b + 1)
                sp.dma_start(bc_dram[ds(b, 1)].rearrange("b n l -> (b n) l"), xdb[R:XD, :]).then_inc(bc_stored, DMA)
                sp.wait_ge(xn1_ready, b + 1)
                sp.dma_start(xn_dram[ds(b * L, L), :].rearrange("(t p) d -> p t d", p=P),
                             XN1[:]).then_inc(xn1_stored, DMA)

            load_x(0)
            for stored in (u_spilled, bc_stored, x1_stored, xn1_stored):
                sp.sem_inc(stored, DMA)
            with sp.Fori(0, B - 1) as b:
                sequence_transfers(b, False)
            sequence_transfers(B - 1, True)

            def load_bc(b, n):
                sp.wait_ge(dbu_ready, b * NS + (n + 1))
                sp.dma_start(Bb[n % BC_RING][:], bc_dram[ds(b, 1), n, :].to_broadcast([P, L])).then_inc(bb_loaded[n % BC_RING], DMA)
                sp.wait_ge(hc_ready, b * NS + (n + 1))
                sp.dma_start(Cb[n % BC_RING][:], bc_dram[ds(b, 1), NS + n, :].to_broadcast([P, L])).then_inc(cb_loaded[n % BC_RING], DMA)

            def load_u(b):
                sp.dma_start(U[:].rearrange("p c l -> p (c l)"),
                             u_dram[ds(b, 1)].rearrange("b p f -> (b p) f")).then_inc(ul_loaded, DMA)

            def load_expert(j0, n):
                j = j0 + n
                e = sp.value_load(tile_exp[0:1, ds(j, 1)], min_val=0, max_val=E - 1)
                sp.wait_ge(up_ready, j + 1)
                w = WGU[n % 2]
                sp.dma_start(w[:, :, 0, :], gate_w[ds(e, 1)].rearrange("e (p k) f -> (e p) k f", p=P)).then_inc(gu_loaded[n % 2], DMA)
                sp.dma_start(w[:, :, 1, :], up_w[ds(e, 1)].rearrange("e (p k) f -> (e p) k f", p=P)).then_inc(gu_loaded[n % 2], DMA)
                sp.wait_ge(down_ready, j + 1)
                sp.dma_start(WD[n % 2][:], down_w[ds(e, 1)].rearrange("e (p k) d -> (e p) k d", p=FH)).then_inc(wd_loaded[n % 2], DMA)

            sp.wait_ge(bc_stored, B * DMA + DMA)
            sp.wait_ge(u_spilled, B * DMA + DMA)
            sp.wait_ge(x1_stored, B * DMA + DMA)
            sp.wait_ge(xn1_stored, B * DMA + DMA)
            sp.wait_ge(dt_ready, B)
            sp.wait_ge(score_copied, B)
            load_u(0)
            for n in range(NS):
                load_bc(0, n)
                if n == NS // 2:
                    sp.wait_ge(slots_set, TOP * NT * DMA)
                    sp.dma_start(slotf[:], slot_dram.rearrange("(j p) o -> j (p o)", p=P)).then_inc(slots_loaded, DMA)
            sp.wait_ge(tex_ready, 1)
            sp.wait_ge(slots_ready, 1)
            with sp.Fori(1, B) as b:
                for n in range(NS):
                    load_bc(b, n)
                    if n == NS // 2:
                        sp.wait_ge(y_ready, b * DC)
                        load_u(b)
                    load_expert(b * NS - NS, n)

            def load_x1(b):
                sp.dma_start(X1[:], x1_dram[ds(b * T, T)].rearrange("t p d -> p t d")).then_inc(x1_loaded, DMA)

            def combine_transfers(b, ahead):
                sp.wait_ge(x3_ready, (b + 1) * T)
                sp.dma_start(x3_dram[ds(b * T, T)].rearrange("t p d -> p t d"), X3[:]).then_inc(x3_stored, DMA)
                if ahead > 1:
                    sp.wait_ge(x2_ready, (b + 2) * T)
                    load_x1(b + 2)
                sp.wait_ge(t3_copied, (b + 1) * T)
                sp.dma_start(xt_dram[ds(b, 1)].rearrange("b p f -> (b p) f"),
                             XT3[:].rearrange("p k l -> p (k l)")).then_inc(xt3_stored, DMA)

            sp.wait_ge(yt_stored, SLOT_TILES * DMA + DMA)
            sp.wait_ge(y_ready, B * DC)
            sp.sem_inc(x3_stored, DMA)
            sp.sem_inc(xt3_stored, DMA)
            load_x1(0)
            sp.wait_ge(x2_ready, T)
            load_x1(1)
            with sp.Fori(0, B - 2) as b:
                combine_transfers(b, 2)
            combine_transfers(B - 2, 1)
            combine_transfers(B - 1, 0)

            sp.wait_ge(rwf_ready, 1)
            sp.wait_ge(x3_stored, B * DMA + DMA)
            sp.wait_ge(xt3_stored, B * DMA + DMA)
            ev = [sp.value_load(lidx[0:1, k:k + 1], min_val=0, max_val=E2 - 1) for k in range(TOP)]
            sp.dma_start(XS[:].rearrange("p k l -> p (k l)"), xt_dram[0]).then_inc(xs_loaded, DMA)
            for k in range(TOP):
                sp.dma_start(b1n[:, k, :], b1[ds(ev[k], 1)].rearrange("e (c p) -> (e c) p", p=P)).then_inc(b1_loaded, DMA)
                sp.dma_start(b2b[:, k, :], b2[ds(ev[k], 1), :].to_broadcast([P, DM])).then_inc(b1_loaded, DMA)
            FQ = FF // WQ
            for k in range(TOP):
                for i in range(WQ):
                    cols = slice(i * FQ, (i + 1) * FQ)
                    if k:
                        sp.wait_ge(wq_loaded[i], k * 2 * DMA)
                    sp.dma_start(W1R[:, k, :, cols], w1[ds(ev[k], 1), :, cols].rearrange(
                        "e (k p) f -> p (e k) f", p=P)).then_inc(wq_loaded[i], DMA)
                    sp.dma_start(W2R[:, k, i * FT // WQ:(i + 1) * FT // WQ, :], w2[ds(ev[k], 1), cols, :].rearrange(
                        "e (f p) d -> p (e f) d", p=P)).then_inc(wq_loaded[i], DMA)
            for tb in range(B):
                if tb:
                    sp.wait_ge(out_stored, tb * DMA)
                sp.dma_start(O[:], x3_dram[tb * T:(tb + 1) * T].rearrange("t p d -> p t d")).then_inc(o_loaded, DMA)
                if tb + 1 < B:
                    sp.wait_ge(xs_split, tb + 1)
                    sp.dma_start(XS[:].rearrange("p k l -> p (k l)"), xt_dram[tb + 1]).then_inc(xs_loaded, DMA)
                sp.wait_ge(y2_added, (tb + 1) * TOP + 1)
                sp.dma_start(out[tb].rearrange("(t p) d -> p t d", p=P), O[:]).then_inc(out_stored, DMA)
            sp.wait_ge(out_stored, B * DMA)

        @block.gpsimd
        def _(pool):
            step = Steps(pool, pool_step)
            pool.memset(zslots[:], 0.0).then_inc(const_ready, 1)
            step.mark(pool.memset(ident[:], 0.0))
            step.mark(pool.memset(ones[:], 1.0))
            step.wait()
            pool.affine_select(out=ident[:], in_=ident[:], compare_op=ALU.not_equal, fill=1.0, base=0,
                               pattern=[[-1, P]], channel_multiplier=1).then_inc(const_ready, 1)
            pool.memset(minus_half[:], -0.5).then_inc(const_ready, 1)
            pool.iota(iota_e[:], pattern=[[1, E]], base=0, channel_multiplier=0,
                      allow_small_or_imprecise_dtypes=True).then_inc(const_ready, 1)
            pool.memset(XP[:], 0.0).then_inc(const_ready, 1)

            def rstd_of(count, ready, done):
                pool.wait_ge(ready, count)
                pool.tensor_tensor(rstd[:], vare[:], minus_half[:], ALU.pow).then_inc(done, 1)

            pool.wait_ge(const_ready, 5)
            rstd_of(1, var_ready, rstd_ready)
            with pool.Fori(0, B - 1) as b:
                rstd_of(b * 2 + 2, var_ready, rstd_ready)
                rstd_of(b * 2 + 3, var_ready, rstd_ready)
            rstd_of(2 * B, var_ready, rstd_ready)

            pool.wait_ge(score_copied, B)
            pool.wait_ge(x1_stored, B * DMA + DMA)
            pool.wait_ge(xn1_stored, B * DMA + DMA)
            pool.wait_ge(bc_stored, B * DMA + DMA)
            pool.wait_ge(dt_ready, B)
            pool.affine_select(out=tri[:], in_=ones[:], compare_op=ALU.is_gt, fill=0.0, base=0,
                               pattern=[[1, P]], channel_multiplier=-1).then_inc(const_ready, 1)
            pool.iota(iota_j[:], pattern=[[1, SLOT_TILES]], base=0, channel_multiplier=0,
                      allow_small_or_imprecise_dtypes=True).then_inc(const_ready, 1)
            pool.iota(tokid[:], pattern=[[P, NT]], base=0, channel_multiplier=1,
                      allow_small_or_imprecise_dtypes=True).then_inc(const_ready, 1)
            pool.wait_ge(const_ready, 8)
            pool.wait_ge(slots_zeroed, DMA)
            pool.wait_ge(pos_ready, 1)
            def scatter(k, t):
                pool.indirect_dma_start(
                    out=slot_dram, out_offset=bass.IndirectOffsetOnAxis(ap=pos[:, k, t:t + 1], axis=0),
                    in_=tokid[:, t:t + 1], in_offset=None).then_inc(slots_set, DMA)

            pool.sem_inc(dbu_ready, BC_RING)

            def dbu(b, n):
                group = b * (NS // GROUP) + n // GROUP
                pool.wait_ge(bb_loaded[n % BC_RING], b * (NS // BC_RING * DMA) + (n // BC_RING + 1) * DMA)
                if n % GROUP < GROUP - 1:
                    wait_apart(pool, added, group * (GROUP - 1) + (n % GROUP + 1))
                else:
                    wait_apart(pool, s_summed, group + 1)
                pool.tensor_tensor(S[n % S_RING][:], DTU[:, ds(b, 1), :, :].rearrange("p b c l -> p (b c) l"),
                                   Bb[n % BC_RING][:].rearrange("p (o l) -> p o l", o=1).to_broadcast([P, DC, L]),
                                   ALU.mult).then_inc(dbu_ready, 1)

            def gather(j0, n):
                j = j0 + n
                pool.wait_ge(xgt_ready, j + 1)
                pool.tensor_copy(gcol[n % 2][:], slot_tok[:, ds(j, 1)]).then_inc(gcol_ready, 1)
                wait_apart(pool, gcol_ready, j + 1)
                pool.indirect_dma_start(out=XG[n % 2][:], out_offset=None, in_=xn_dram,
                                        in_offset=bass.IndirectOffsetOnAxis(ap=gcol[n % 2][:, 0:1], axis=0)
                                        ).then_inc(xg_loaded[n % 2], DMA)

            pool.wait_ge(dt_ready, B)
            per = TOP * NT // (NS // 2)
            for n in range(NS):
                if n < NS // 2:
                    for i in range(n * per, (n + 1) * per):
                        scatter(i // NT, i % NT)
                dbu(0, n)
            pool.wait_ge(slots_ready, 1)

            def mixture_steps(b, last):
                for n in range(NS):
                    dbu(b, n)
                    if n + 2 < NS:
                        gather(b * NS - NS, n + 2)
                    elif not last:
                        gather(b * NS, n + 2 - NS)

            gather(0, 0)
            gather(0, 1)
            with pool.Fori(1, B - 1) as b:
                mixture_steps(b, False)
            mixture_steps(B - 1, True)

            def gather_y(b, k, y):
                pool.tensor_copy(pcol[k][:], pos[:, k, ds(b * T, T)]).then_inc(pcol_ready, 1)
                wait_apart(pool, pcol_ready, b * TOP + (k + 1))
                for t in range(T):
                    pool.indirect_dma_start(
                        out=y[:, t, :], out_offset=None, in_=y_dram,
                        in_offset=bass.IndirectOffsetOnAxis(ap=pcol[k][:, t:t + 1], axis=0)).then_inc(y_loaded[k], DMA)

            def rstd_and_gate(b):
                pool.wait_ge(var2_ready, b + 1)
                pool.tensor_tensor(rstd[:], vare[:], minus_half[:], ALU.pow).then_inc(rstd2_ready, 1)
                for c in range(DC):
                    wait_apart(pool, zt_ready, b * DC + (c + 1))
                    pool.tensor_tensor(ZT[:, c, :], ZT[:, c, :], DTU[:, ds(b, 1), c, :].rearrange("p b l -> p (b l)"),
                                       ALU.mult).then_inc(gate_ready, 1)

            def combine_pool(b, ahead):
                if ahead > 1:
                    pool.wait_ge(part_ready, (b + 2) * T)
                    gather_y(b + 2, 0, Y1)
                pool.wait_ge(var3_ready, b + 1)
                pool.tensor_tensor(norm3[3][:], norm3[2][:], minus_half[:], ALU.pow).then_inc(rstd3_ready, 1)
                if ahead > 0:
                    rstd_and_gate(b + 1)
                if ahead > 1:
                    pool.wait_ge(x2_ready, (b + 2) * T)
                    gather_y(b + 2, 1, Y2)

            pool.wait_ge(yt_stored, SLOT_TILES * DMA + DMA)
            pool.wait_ge(y_ready, B * DC)
            gather_y(0, 0, Y1)
            gather_y(0, 1, Y2)
            rstd_and_gate(0)
            pool.wait_ge(part_ready, T)
            gather_y(1, 0, Y1)
            pool.wait_ge(x2_ready, T)
            gather_y(1, 1, Y2)
            with pool.Fori(0, B - 2) as b:
                combine_pool(b, 2)
            combine_pool(B - 2, 1)
            combine_pool(B - 1, 0)

            pool.wait_ge(rwf_ready, 1)
            with pool.Fori(0, B) as tb:
                with pool.Fori(0, TOP) as e:
                    it = pool.snap(tb * (TOP * FT) + e * FT)
                    for f in range(FT):
                        pool.wait_ge(w1h_ready, it + (f + 1))
                        pool.tensor_tensor(W1L[f % 2][:],
                                           W1R[:, ds(e, 1), :, f * P:(f + 1) * P].rearrange("p e k f -> p (e k) f"),
                                           W1H[f % 2][:].bitcast(F32), ALU.subtract).then_inc(w1l_ready, 1)
                        pool.wait_ge(w2h_ready, it + (f + 1))
                        pool.tensor_tensor(W2L[f % 2][:], W2R[:, ds(e, 1), f, :].rearrange("p e d -> p (e d)"),
                                           W2H[f % 2][:].bitcast(F32), ALU.subtract).then_inc(w2l_ready, 1)

        @block.scalar
        def _(act):
            act.wait_ge(nat_loaded, NAT_LOADS * DMA)
            act.activation(negA[:], nat_A[:], ACT.Exp).then_inc(small_ready, 1)
            act.wait_ge(small_ready, 1)
            act.mul(negA[:], negA[:], -1.0).then_inc(small_ready, 1)
            for i, (_, _, parts, dst) in enumerate(setup):
                act.wait_ge(set_t, i + 1)
                act.copy(dst, bank(4 + i % 2, parts, dst.shape[1])).then_inc(set_c, 1)

            def copy_xin(b):
                for c in range(DC):
                    act.wait_ge(xin_ready, b * DC + (c + 1))
                    act.copy(XP[:, c, TAPS - 1:], PS[c][:]).then_inc(xp_ready, 1)

            def copy_t(count, dst, i):
                act.wait_ge(t_ready, count)
                act.copy(dst, PS[4 + i % 2][:].rearrange("p (k c) -> p k c", k=K)).then_inc(t_copied, 1)

            def sequence_act(b, last):
                act.wait_ge(qk_ready, b + 1)
                for w in range(2):
                    act.activation(QKT[:, w, :], PS[6 + w][:], ACT.Identity, bias=qkb[:, w:w + 1]).then_inc(qk_copied, 1)
                for t in range(T):
                    act.wait_ge(nneg_ready, b * T + (t + 1))
                    act.activation(PR[:, t, :], PS[6 + t % 2][:], ACT.Exp, bias=nneg[:, t:t + 1],
                                   accum_out=rsum[:, t:t + 1]).then_inc(exp_ready, 1)
                for t in range(T):
                    copy_t(b * 12 + (t + 1), XNT[:, :, t * P:(t + 1) * P], t)
                for t in range(T):
                    copy_t(b * 12 + (T + t + 1), ATT[:, :, t * P:(t + 1) * P], t)
                act.wait_ge(xh_ready, b + 1)
                act.wait_ge(u_spilled, b * DMA + DMA)
                act.activation(U[:], XH[:], ACT.Silu).then_inc(u_ready, 1)
                act.wait_ge(xd_ready, b + 1)
                act.wait_ge(bc_stored, b * DMA + DMA)
                act.copy(xdb[:], PS[0][0:XD, :]).then_inc(xd_copied, 1)
                for t in range(T):
                    copy_t(b * 12 + (2 * T + t + 1), XNT[:, :, t * P:(t + 1) * P], t)
                for c in range(DC):
                    act.wait_ge(r_ready, b * DC + (c + 1))
                    act.activation(ZZ[:, c, :], PS[c][:], ACT.Abs, bias=dtB[:, c:c + 1]).then_inc(abs_ready, 1)
                act.wait_ge(abs_ready, b * DC + DC)
                act.activation(ZZ[:], ZZ[:], ACT.Exp, scale=-1.0).then_inc(z_ready, 1)
                wait_apart(act, score_ready, b + 1)
                act.copy(SC[:, ds(b * T, T), :], PS[6][:, 0:T * E].rearrange("p (t e) -> p t e", t=T)
                         ).then_inc(score_copied, 1)
                if not last:
                    copy_xin(b + 1)
                act.wait_ge(w_ready, b * 2 + 2)
                act.activation(ZZ[:], XH[:], ACT.Ln).then_inc(ln_ready, 1)

            act.wait_ge(const_ready, 5)
            copy_xin(0)
            with act.Fori(0, B - 1) as b:
                sequence_act(b, False)
            sequence_act(B - 1, True)

            act.wait_ge(diff_ready, 1)
            act.activation(ex[:], diff[:], ACT.Exp).then_inc(ex_ready, 1)

            def decay(b, n):
                u = b * NS + n
                wait_apart(act, scan_done, u + 1)
                for c in range(DC):
                    ins = act.activation(
                        dA[n % A_RING][:, c, 1:], DT[:, ds(b, 1), c, 1:].rearrange("p b l -> p (b l)"),
                        ACT.Exp, scale=negA[:, c, n:n + 1])
                ins.then_inc(da_ready, 1)

            def copy_xg(j0, n):
                j = j0 + n
                act.wait_ge(xgt_ready, j + 3)
                act.copy(XGT[n % 2][:], PS[4][:].rearrange("p (k t) -> p k t", k=K)).then_inc(xgt_copied, 1)

            def tanh_g(j0, n):
                act.wait_ge(up_ready, j0 + (n + 3))
                act.activation(TG[n % 2][:], PS[5][:, 0:F], ACT.Tanh, scale=0.5).then_inc(tg_ready, 1)

            def copy_ht(j0, n):
                act.wait_ge(ht_ready, j0 + (n + 1))
                act.copy(HT[n % 2][:], PS[6][0:FH, 0:2 * P].rearrange("p (k t) -> p k t", k=2)).then_inc(ht_copied, 1)

            def copy_y(j0, n):
                j = j0 + n
                act.wait_ge(down_ready, j + 3)
                act.wait_ge(yt_stored, j * DMA + DMA)
                act.copy(YT[n % 2][:], PS[7][:]).then_inc(yt_ready, 1)

            def store_y(j0, n):
                j = j0 + n
                act.wait_ge(yt_ready, j + 2)
                act.dma_start(y_dram[ds(j * P, P), :], YT[n % 2][:]).then_inc(yt_stored, DMA)

            act.wait_ge(dt_ready, B)
            act.wait_ge(scan_done, A_RING)
            for n in range(NS):
                decay(0, n)
            act.wait_ge(slots_ready, 1)
            act.sem_inc(yt_ready, 1)
            act.sem_inc(yt_stored, DMA)

            def mixture_steps(b, last):
                j0 = b * NS - NS
                for n in range(NS):
                    if n + AHEAD < NS:
                        decay(b, n + AHEAD)
                    elif not last:
                        decay(b + 1, n + AHEAD - NS)
                    copy_ht(j0, n)
                    if n + 2 < NS:
                        copy_xg(j0, n + 2)
                    elif not last:
                        copy_xg(j0 + NS, n + 2 - NS)
                    if n + 1 < NS:
                        tanh_g(j0, n + 1)
                    elif not last:
                        tanh_g(j0 + NS, 0)
                    copy_y(j0, n)
                    store_y(j0, n)

            copy_xg(0, 0)
            tanh_g(0, 0)
            copy_xg(0, 1)
            for n in range(AHEAD):
                decay(1, n)
            with act.Fori(1, B - 1) as b:
                mixture_steps(b, False)
            mixture_steps(B - 1, True)

            def silu_z(b):
                for c in range(DC):
                    act.wait_ge(zn_ready, b * DC + (c + 1))
                    act.activation(ZT[:, c, :], ZN[:, c, :], ACT.Silu).then_inc(zt_ready, 1)

            def combine_act(b, ahead):
                if ahead:
                    silu_z(b + 1)
                act.wait_ge(xt3_stored, b * DMA + DMA)
                for t in range(T):
                    act.wait_ge(t3_ready, b * T + (T + t + 1))
                    act.copy(XT3[:, :, t * P:(t + 1) * P],
                             PS[4 + t % 2][:].rearrange("p (k c) -> p k c", k=K)).then_inc(t3_copied, 1)
                wait_apart(act, lg_ready, b + 1)
                act.copy(logits[:, ds(b * T, T), :],
                         PS[6][:, 0:T * E2].rearrange("p (t e) -> p t e", t=T)).then_inc(lg_copied, 1)

            silu_z(0)
            with act.Fori(0, B - 1) as b:
                combine_act(b, 1)
            combine_act(B - 1, 0)
            act.wait_ge(lme_ready, 1)
            act.activation(lsel[:], lsel[:], ACT.Exp).then_inc(lexp_ready, 1)

            act.wait_ge(b1_t, 1)
            act.copy(b1T[:], PS[6][:, 0:TOP * FT].rearrange("p (k f) -> p k f", k=TOP)).then_inc(b1_ready, 1)
            act.wait_ge(b1_ready, 1)
            with act.Fori(0, B) as tb:
                with act.Fori(0, TOP) as e:
                    it = act.snap(tb * (TOP * FT) + e * FT)

                    def split(f):
                        if f % (FT // WQ) == 0:
                            act.wait_ge(wq_loaded[f // (FT // WQ)], e * (2 * DMA) + 2 * DMA)
                        act.wait_ge(up2_ready, it + (f + 1))
                        act.copy(W1H[f % 2][:], W1R[:, ds(e, 1), :, f * P:(f + 1) * P].rearrange(
                            "p e k f -> p (e k) f")).then_inc(w1h_ready, 1)
                        act.wait_ge(down2_done, it + (f + 1))
                        act.copy(W2H[f % 2][:], W2R[:, ds(e, 1), f, :].rearrange("p e d -> p (e d)")
                                 ).then_inc(w2h_ready, 1)

                    def gelu(f):
                        wait_apart(act, up2_ready, it + (f + 3))
                        act.activation(HF[f % 2][:], PS[4 + f % 2][:], ACT.Gelu_apprx_tanh,
                                       bias=b1T[:, ds(e, 1), f:f + 1].rearrange("p e f -> p (e f)")).then_inc(hf_ready, 1)

                    split(0)
                    for f in range(FT):
                        if f + 1 < FT:
                            split(f + 1)
                        gelu(f)

        @block.vector
        def _(dve):
            step = Steps(dve, dve_step)
            dve.wait_ge(nat_loaded, NAT_LOADS * DMA)
            def layernorm(src, dst, count, ready, got, done):
                for t in range(T):
                    ins = dve.bn_stats(stats[:, t, :], src[:, t, :])
                step.mark(ins)
                step.wait(apart=wait_apart)
                for t in range(T):
                    ins = dve.bn_aggr(mv[:, t, :], stats[:, t, :])
                step.mark(ins)
                step.wait()
                dve.tensor_scalar(vare[:].rearrange("p (t o) -> p t o", o=1), mv[:, :, 1:2], EPS, None,
                                  ALU.add).then_inc(ready, 1)
                dve.wait_ge(got, count)
                for t in range(T):
                    ins = dve.tensor_scalar(dst[:, t, :], src[:, t, :], mv[:, t, 0:1], rstd[:, t:t + 1],
                                            ALU.subtract, ALU.mult)
                ins.then_inc(done, 1)

            def layernorm_x(b):
                dve.wait_ge(xb_loaded, b * DMA + DMA)
                layernorm(XB, XN, b * 2 + 1, var_ready, rstd_ready, xn_ready)

            def softmax(b):
                def row_max(t):
                    dve.wait_ge(e_ready, b * T + (t + 1))
                    step.mark(dve.tensor_reduce(nmax[:, t:t + 1], PS[6 + t % 2][:], AX, ALU.max))
                    step.wait()
                    dve.tensor_scalar(nneg[:, t:t + 1], nmax[:, t:t + 1], -1.0, None, ALU.mult).then_inc(nneg_ready, 1)

                def normalize(t):
                    dve.wait_ge(exp_ready, b * T + (t + 1))
                    step.mark(dve.reciprocal(rinv[:, t:t + 1], rsum[:, t:t + 1]))
                    step.wait()
                    dve.tensor_scalar(PR[:, t, :], PR[:, t, :], rinv[:, t:t + 1], None, ALU.mult).then_inc(p_ready, 1)

                row_max(0)
                row_max(1)
                for t in range(T):
                    normalize(t)
                    if t + 2 < T:
                        row_max(t + 2)

            def convolve(b):
                for c in range(DC):
                    dve.wait_ge(xp_ready, b * DC + (c + 1))
                    step.mark(dve.tensor_scalar(XH[:, c, :], XP[:, c, TAPS - 1:], convW[:, c, TAPS - 1:TAPS],
                                                convB[:, c:c + 1], ALU.mult, ALU.add))
                for j in range(TAPS - 1):
                    for c in range(DC):
                        if c == 0:
                            step.wait()
                        ins = dve.scalar_tensor_tensor(XH[:, c, :], XP[:, c, j:j + L], convW[:, c, j:j + 1],
                                                       XH[:, c, :], ALU.mult, ALU.add)
                        if j < TAPS - 2:
                            step.mark(ins)
                ins.then_inc(xh_ready, 1)

            def positive_part(b):
                for c in range(DC):
                    dve.wait_ge(dtp_ready, b * DC + (c + 1))
                    dve.tensor_scalar(RL[:, c, :], PS[c][:], dtB[:, c:c + 1], 0.0, ALU.add, ALU.max).then_inc(r_ready, 1)

            def softplus(b):
                dt, dtu = (a_[:, ds(b, 1)].rearrange("p b c l -> p (b c) l") for a_ in (DT, DTU))
                dve.wait_ge(z_ready, b + 1)
                dve.tensor_scalar(XH[:], ZZ[:], 1.0, None, ALU.add).then_inc(w_ready, 1)
                dve.wait_ge(w_ready, b * 2 + 1)
                dve.scalar_tensor_tensor(ND[:], XH[:], 1.0, ZZ[:], ALU.subtract, ALU.subtract).then_inc(w_ready, 1)
                dve.wait_ge(w_ready, b * 2 + 2)
                step.mark(dve.tensor_tensor(RL[:], RL[:], ND[:], ALU.subtract))
                dve.wait_ge(ln_ready, b + 1)
                step.wait()
                step.mark(dve.tensor_tensor(dt, RL[:], ZZ[:], ALU.add))
                step.wait()
                dve.tensor_tensor(dtu, dt, U[:], ALU.mult).then_inc(dt_ready, 1)

            def sequence_dve(b, last):
                softmax(b)
                convolve(b)
                dve.wait_ge(x1_stored, b * DMA + DMA)
                for t in range(T):
                    dve.wait_ge(o_ready, b * T + (t + 1))
                    dve.tensor_tensor(X1A[:, t, :], PS[6 + t % 2][:], XB[:, t, :], ALU.add).then_inc(x1_ready, 1)
                dve.wait_ge(x1_ready, b * T + T)
                dve.wait_ge(xn1_stored, b * DMA + DMA)
                layernorm(X1A, XN1, b * 2 + 2, var_ready, rstd_ready, xn1_ready)
                positive_part(b)
                if not last:
                    layernorm_x(b + 1)
                softplus(b)

            layernorm_x(0)
            with step.loop(B - 1, 3 * DC + 2 + 4 + 2 * T) as b:
                sequence_dve(b, False)
            sequence_dve(B - 1, True)

            def do(ins):
                step.mark(ins)
                step.wait()

            dve.wait_ge(score_copied, B)
            dve.wait_ge(x1_stored, B * DMA + DMA)
            dve.wait_ge(xn1_stored, B * DMA + DMA)
            dve.wait_ge(bc_stored, B * DMA + DMA)
            dve.wait_ge(slots_zeroed, DMA)
            for t in range(NT):
                ins = dve.max(M8[:, t, :], SC[:, t, :])
            do(ins)
            for t in range(NT):
                ins = dve.max_index(I8[:, t, :], M8[:, t, :], SC[:, t, :])
            dve.tensor_tensor(diff[:].rearrange("p (t o) -> p t o", o=1), M8[:, :, 1:2], M8[:, :, 0:1],
                              ALU.subtract).then_inc(diff_ready, 1)
            do(ins)
            for k in range(TOP):
                ins = dve.tensor_copy(IF[:, k, :].rearrange("p (t o) -> p t o", o=1), I8[:, :, k:k + 1])
            do(ins)
            dve.wait_ge(const_ready, 4)
            for k in range(TOP):
                ins = dve.tensor_tensor(OH[:, k], iota_e[:].rearrange("p (o e) -> p o e", o=1).to_broadcast([P, NT, E]),
                                        IF[:, k, :].rearrange("p (t o) -> p t o", o=1).to_broadcast([P, NT, E]),
                                        ALU.is_equal)
            do(ins)
            dve.tensor_tensor(MM[:], OH[:, 0], OH[:, 1], ALU.add).then_inc(mask_ready, 1)
            dve.wait_ge(ex_ready, 1)
            do(dve.tensor_scalar(den[:], ex[:], 1.0, None, ALU.add))
            do(dve.reciprocal(rwt[:, 0, :], den[:]))
            do(dve.tensor_tensor(rwt[:, 1, :], ex[:], rwt[:, 0, :], ALU.mult))
            dve.wait_ge(rank_ready, 1)
            do(dve.memset(PX[:, 0, :], 0.0))
            totals = PS[5][:, 0:NT * E].rearrange("p (t e) -> p t e", t=NT)
            for t in range(NT):
                do(dve.tensor_tensor(PX[:, t + 1, :], PX[:, t, :], totals[:, t, :], ALU.add))
            do(dve.tensor_tensor(PO[:], PX[:, 0:NT, :], PS[4][:, 0:NT * E].rearrange("p (t e) -> p t e", t=NT), ALU.add))
            do(dve.tensor_scalar(cnt[:], PX[:, NT, :], (P - 1) / 2, 1 / P, ALU.add, ALU.mult))
            do(dve.tensor_copy(cnti[:], cnt[:]))
            do(dve.tensor_copy(tiles[:], cnti[:]))
            do(dve.tensor_tensor_scan(incl[:], ones[:, 0:E], tiles[:], 0.0, ALU.mult, ALU.add))
            do(dve.tensor_tensor(off[:], incl[:], tiles[:], ALU.subtract))
            do(dve.tensor_scalar(off[:], off[:], float(P), None, ALU.mult))
            do(dve.tensor_tensor(PO[:], PO[:], off[:].rearrange("p (o e) -> p o e", o=1).to_broadcast([P, NT, E]), ALU.add))
            for k in range(TOP):
                ins = dve.tensor_tensor(PSEL[:, k], OH[:, k], PO[:], ALU.mult)
            do(ins)
            for k in range(TOP):
                ins = dve.tensor_reduce(posf[:, k, :].rearrange("p (t o) -> p t o", o=1), PSEL[:, k], AX, ALU.add)
            do(ins)
            dve.tensor_copy(pos[:], posf[:]).then_inc(pos_ready, 1)
            dve.wait_ge(const_ready, 8)
            do(dve.tensor_tensor(cmpj[:], incl[:].rearrange("p (o e) -> p o e", o=1).to_broadcast([P, SLOT_TILES, E]),
                                 iota_j[:].rearrange("p (j o) -> p j o", o=1).to_broadcast([P, SLOT_TILES, E]),
                                 ALU.is_le))
            do(dve.tensor_reduce(texf[:].rearrange("p (j o) -> p j o", o=1), cmpj[:], AX, ALU.add))
            do(dve.tensor_scalar(texf[:], texf[:], float(E - 1), None, ALU.min))
            dve.tensor_copy(tile_exp[:], texf[:]).then_inc(tex_ready, 1)
            for i in range(A_RING):
                ins = dve.memset(dA[i][:, :, 0:1], 0.0)
                ins.then_inc(scan_done, 1)
            dve.sem_inc(hc_ready, BC_RING)
            dve.sem_inc(added, GROUP - 1)

            def scan(b, n):
                u = b * NS + n
                dve.wait_ge(da_ready, u + 1)
                dve.wait_ge(dbu_ready, u + (BC_RING + 1))
                s_ = S[n % S_RING]
                flat = s_[:].rearrange("p c l -> p (c l)")
                dve.tensor_tensor_scan(flat, dA[n % A_RING][:].rearrange("p c l -> p (c l)"), flat, 0.0,
                                       ALU.mult, ALU.add).then_inc(scan_done, 1)
                dve.wait_ge(cb_loaded[n % BC_RING], b * (NS // BC_RING * DMA) + (n // BC_RING + 1) * DMA)
                dve.wait_ge(scan_done, u + (A_RING + 1))
                dve.tensor_tensor(s_[:], s_[:], Cb[n % BC_RING][:].rearrange("p (o l) -> p o l", o=1).to_broadcast([P, DC, L]),
                                  ALU.mult).then_inc(hc_ready, 1)
                if n % GROUP:
                    dve.wait_ge(hc_ready, u + (BC_RING + 1))
                    if n % GROUP > 1:
                        dve.wait_ge(added, (b * (NS // GROUP) + n // GROUP) * (GROUP - 1) + (GROUP - 2 + n % GROUP))
                    dve.tensor_tensor(s_[:], s_[:], S[n % S_RING - 1][:], ALU.add).then_inc(added, 1)

            def take_y(b):
                dve.wait_ge(s_summed, b * (NS // GROUP) + (NS // GROUP + 1))
                dve.wait_ge(ul_loaded, b * DMA + DMA)
                for c in range(DC):
                    dve.scalar_tensor_tensor(DTU[:, ds(b, 1), c, :].rearrange("p b l -> p (b l)"), U[:, c, :],
                                             skip[:, c:c + 1], PS[c][:], ALU.mult, ALU.add).then_inc(y_ready, 1)

            def silu_h(j0, n):
                dve.wait_ge(tg_ready, j0 + (n + 1))
                dve.scalar_tensor_tensor(GG[n % 2][:], TG[n % 2][:], 1.0, PS[5][:, 0:F], ALU.add,
                                         ALU.mult).then_inc(gg_ready, 1)
                dve.wait_ge(gg_ready, j0 + (n + 1))
                dve.scalar_tensor_tensor(HH[n % 2][:], GG[n % 2][:], 0.5, PS[5][:, F:2 * F], ALU.mult,
                                         ALU.mult).then_inc(hh_ready, 1)

            for n in range(NS):
                scan(0, n)
                if n == NS - 4:
                    dve.wait_ge(slots_t, 1)
                    dve.tensor_copy(slot_tok[:], PS[6][:, 0:SLOT_TILES]).then_inc(slots_ready, 1)
            take_y(0)

            def mixture_steps(b, last):
                j0 = b * NS - NS
                for n in range(NS):
                    if n + 1 < NS:
                        scan(b, n + 1)
                        silu_h(j0, n + 1)
                    elif not last:
                        take_y(b)
                        scan(b + 1, 0)
                        silu_h(j0 + NS, 0)
                    else:
                        take_y(b)

            scan(1, 0)
            silu_h(0, 0)
            with dve.Fori(1, B - 1) as b:
                mixture_steps(b, False)
            mixture_steps(B - 1, True)

            def statistics(src, norm, ready):
                stats, mv, vare, _ = norm
                for t in range(T):
                    ins = dve.bn_stats(stats[:, t, :], src[:, t, :])
                step.mark(ins)
                step.wait(apart=wait_apart)
                for t in range(T):
                    ins = dve.bn_aggr(mv[:, t, :], stats[:, t, :])
                step.mark(ins)
                step.wait()
                dve.tensor_scalar(vare[:].rearrange("p (t o) -> p t o", o=1), mv[:, :, 1:2], EPS, None,
                                  ALU.add).then_inc(ready, 1)

            def normalized(dst, src, norm, got, count, done):
                _, mv, _, rstd = norm
                dve.wait_ge(got, count)
                for t in range(T):
                    dve.tensor_scalar(dst[:, t, :], src[:, t, :], mv[:, t, 0:1], rstd[:, t:t + 1],
                                      ALU.subtract, ALU.mult).then_inc(done, 1)

            def add_first(b):
                dve.wait_ge(x1_loaded, b * DMA + DMA)
                dve.wait_ge(y_loaded[0], b * (T * DMA) + T * DMA)
                for t in range(T):
                    dve.scalar_tensor_tensor(X1[:, t, :], Y1[:, t, :], rwt[:, 0, ds(b * T + t, 1)], X1[:, t, :],
                                             ALU.mult, ALU.add).then_inc(part_ready, 1)

            def add_second(b):
                dve.wait_ge(y_loaded[1], b * (T * DMA) + T * DMA)
                for t in range(T):
                    dve.wait_ge(part_ready, b * T + (t + 1))
                    dve.scalar_tensor_tensor(X2[:, t, :], Y2[:, t, :], rwt[:, 1, ds(b * T + t, 1)], X1[:, t, :],
                                             ALU.mult, ALU.add).then_inc(x2_ready, 1)
                dve.wait_ge(x2_ready, b * T + T)
                statistics(X2, norm, var2_ready)

            def combine(b, ahead):
                dve.wait_ge(x3_stored, b * DMA + DMA)
                for t in range(T):
                    dve.wait_ge(gt_ready, b * T + (t + 1))
                    dve.tensor_tensor(X3[:, t, :], PS[t][:], X2[:, t, :], ALU.add).then_inc(x3_ready, 1)
                dve.wait_ge(x3_ready, b * T + T)
                statistics(X3, norm3, var3_ready)
                if ahead > 0:
                    add_second(b + 1)
                    normalized(ZN, X2, norm, rstd2_ready, b + 2, zn_ready)
                dve.wait_ge(t3_ready, b * T + T)
                normalized(ZN3, X3, norm3, rstd3_ready, b + 1, xn3_ready)
                if ahead > 1:
                    add_first(b + 2)
                dve.wait_ge(xn3_ready, b * T + T)

            add_first(0)
            add_second(0)
            normalized(ZN, X2, norm, rstd2_ready, 1, zn_ready)
            add_first(1)
            with step.loop(B - 2, 4) as b:
                combine(b, 2)
            combine(B - 2, 1)
            combine(B - 1, 0)
            dve.wait_ge(lg_copied, B)

            dve.wait_ge(lsum_ready, 1)
            do(dve.tensor_copy(lsum[:], PS[7][:, 0:E2]))
            do(dve.max(lmax[:], lsum[:]))
            dve.max_index(lidx[:], lmax[:], lsum[:]).then_inc(lidx_ready, 1)
            dve.wait_ge(lidx_ready, 1)
            do(dve.tensor_copy(lidf[:], lidx[:, 0:TOP]))
            for k in range(TOP):
                ins = dve.tensor_scalar(loh[:, k, :], iota_e[:, 0:E2], lidf[:, k:k + 1], None, ALU.is_equal)
            do(ins)
            for k in range(TOP):
                ins = dve.tensor_tensor(ltmp[:, k], logits[:], loh[:, k:k + 1, :].to_broadcast([P, NT, E2]), ALU.mult)
            do(ins)
            for k in range(TOP):
                ins = dve.tensor_reduce(lsel[:, k, :].rearrange("p (t o) -> p t o", o=1), ltmp[:, k], AX, ALU.add)
            do(ins)
            do(dve.tensor_tensor(lme[:], lsel[:, 0, :], lsel[:, 1, :], ALU.max))
            dve.tensor_tensor(lsel[:], lsel[:], lme[:].rearrange("p (o t) -> p o t", o=1).to_broadcast([P, TOP, NT]),
                              ALU.subtract).then_inc(lme_ready, 1)
            dve.wait_ge(lexp_ready, 1)
            do(dve.tensor_tensor(lden[:], lsel[:, 0, :], lsel[:, 1, :], ALU.add))
            do(dve.reciprocal(lme[:], lden[:]))
            dve.tensor_tensor(rwf[:], lsel[:], lme[:].rearrange("p (o t) -> p o t", o=1).to_broadcast([P, TOP, NT]),
                              ALU.mult).then_inc(rwf_ready, 1)

            dve.sem_inc(y2_added, 1)
            with dve.Fori(0, B) as tb:
                dve.wait_ge(xs_loaded, tb * DMA + DMA)
                dve.wait_ge(up2_ready, tb * (TOP * FT) + 2)
                dve.tensor_copy(XSH[:], XS[:]).then_inc(xsh_ready, 1)
                dve.wait_ge(xsh_ready, tb + 1)
                dve.tensor_tensor(XSL[:], XS[:], XSH[:].bitcast(F32), ALU.subtract).then_inc(xs_split, 1)
                with dve.Fori(0, TOP) as e:
                    it = dve.snap(tb * (TOP * FT) + e * FT)
                    for f in range(FT):
                        dve.wait_ge(hf_ready, it + (f + 1))
                        dve.tensor_copy(HFH[f % 2][:], HF[f % 2][:]).then_inc(hfh_ready, 1)
                        dve.wait_ge(hfh_ready, it + (f + 1))
                        dve.tensor_tensor(HFL[f % 2][:], HF[f % 2][:], HFH[f % 2][:].bitcast(F32),
                                          ALU.subtract).then_inc(hfl_ready, 1)
                    dve.wait_ge(o_loaded, tb * DMA + DMA)
                    dve.wait_ge(b1_loaded, 2 * TOP * DMA)
                    for t in range(T):
                        w = rwf[:, ds(e, 1), ds(tb * T + t, 1)].rearrange("p e t -> p (e t)")
                        dve.scalar_tensor_tensor(O[:, t, :], b2b[:, ds(e, 1), :].rearrange("p e d -> p (e d)"), w,
                                                 O[:, t, :], ALU.mult, ALU.add).then_inc(ob_ready, 1)
                    dve.wait_ge(down2_done, it + (FT + 2))
                    for t in range(T):
                        w = rwf[:, ds(e, 1), ds(tb * T + t, 1)].rearrange("p e t -> p (e t)")
                        dve.wait_ge(ob_ready, tb * (TOP * T) + e * T + (t + 1))
                        ins = dve.scalar_tensor_tensor(O[:, t, :], PS[t][:], w, O[:, t, :], ALU.mult, ALU.add)
                    ins.then_inc(y2_added, 1)
                    dve.wait_ge(y2_added, tb * TOP + e + 2)

        @block.tensor
        def _(pe):
            pe.wait_ge(nat_loaded, NAT_LOADS * DMA)
            pe.wait_ge(const_ready, 2)
            for i, (srcs, parts_in, parts, dst) in enumerate(setup):
                if i >= 2:
                    pe.wait_ge(set_c, i - 1)
                if i == len(setup) - 2 * B:
                    pe.wait_ge(ctx_loaded, DMA)
                w = dst.shape[1] // len(srcs)
                for k, src in enumerate(srcs):
                    ins = pe.transpose(PS[4 + i % 2][0:parts, k * w:(k + 1) * w], src, ident[0:parts_in, 0:parts_in])
                ins.then_inc(set_t, 1)

            pe.wait_ge(set_c, len(setup))

            def in_proj(b):
                for c in range(DC):
                    for k in range(CK):
                        ins = pe.matmul(PS[c][:], inT[:, k, c * P:(c + 1) * P], ctxT[:, k, ds(b * L, L)],
                                        start=(k == 0), stop=(k == CK - 1))
                    ins.then_inc(xin_ready, 1)

            def four_transposes(src, i, count):
                for k in range(K):
                    ins = pe.transpose(PS[4 + i % 2][:, k * P:(k + 1) * P], src[:, k * P:(k + 1) * P], ident[:])
                ins.then_inc(count, 1)

            def sequence_pe(b, last):
                for w in range(2):
                    for k in range(CK):
                        ins = pe.matmul(PS[6 + w][:], wqkT[:, w, k, :], ctxT[:, k, ds(b * L, L)],
                                        start=(k == 0), stop=(k == CK - 1))
                ins.then_inc(qk_ready, 1)
                pe.wait_ge(qk_copied, b * 2 + 2)
                for t in range(T):
                    if t >= 2:
                        pe.wait_ge(exp_ready, b * T + (t - 1))
                    pe.matmul(PS[6 + t % 2][:], QKT[:, 0, t * P:(t + 1) * P], QKT[:, 1, :],
                              start=True, stop=True).then_inc(e_ready, 1)
                pe.wait_ge(xn_ready, b + 1)
                for t in range(T):
                    if t >= 2:
                        pe.wait_ge(t_copied, b * 12 + (t - 1))
                    four_transposes(XN[:, t, :], t, t_ready)
                for t in range(T):
                    pe.wait_ge(p_ready, b * T + (t + 1))
                    pe.wait_ge(t_copied, b * 12 + (T + t - 1))
                    four_transposes(PR[:, t, :], t, t_ready)
                pe.wait_ge(t_copied, b * 12 + 2 * T)
                for t in range(T):
                    if t >= 2:
                        pe.wait_ge(x1_ready, b * T + (t - 1))
                    for k in range(K):
                        ins = pe.matmul(PS[6 + t % 2][:], XNT[:, k, t * P:(t + 1) * P], ATT[:, k, :],
                                        start=(k == 0), stop=(k == K - 1))
                    ins.then_inc(o_ready, 1)
                pe.wait_ge(u_ready, b + 1)
                for c in range(DC):
                    ins = pe.matmul(PS[0][0:XD, :], xpT[:, c, :], U[:, c, :], start=(c == 0), stop=(c == DC - 1))
                ins.then_inc(xd_ready, 1)
                pe.wait_ge(xd_copied, b + 1)
                for c in range(DC):
                    pe.matmul(PS[c][:], dtpT[:, c * P:(c + 1) * P], xdb[0:R, :],
                              start=True, stop=True).then_inc(dtp_ready, 1)
                pe.wait_ge(xn1_ready, b + 1)
                for t in range(T):
                    pe.wait_ge(t_copied, b * 12 + (2 * T + t - 1))
                    four_transposes(XN1[:, t, :], t, t_ready)
                pe.wait_ge(t_copied, b * 12 + 3 * T)
                for t in range(T):
                    for k in range(K):
                        ins = pe.matmul(PS[6][:, t * E:(t + 1) * E], XNT[:, k, t * P:(t + 1) * P], routerW[:, k, :],
                                        start=(k == 0), stop=(k == K - 1))
                ins.then_inc(score_ready, 1)
                pe.wait_ge(abs_ready, b * DC + DC)
                if not last:
                    in_proj(b + 1)
                pe.wait_ge(score_copied, b + 1)

            in_proj(0)
            with pe.Fori(0, B - 1) as b:
                sequence_pe(b, False)
            sequence_pe(B - 1, True)

            pe.wait_ge(mask_ready, 1)
            pe.wait_ge(const_ready, 6)
            pe.matmul(PS[4][:, 0:NT * E], tri[:], MM[:].rearrange("p t e -> p (t e)"), start=True, stop=True)
            pe.matmul(PS[5][:, 0:NT * E], ones[:], MM[:].rearrange("p t e -> p (t e)"), start=True,
                      stop=True).then_inc(rank_ready, 1)

            pe.sem_inc(s_summed, 1)
            pe.sem_inc(xgt_ready, 2)
            pe.sem_inc(up_ready, 2)
            pe.sem_inc(down_ready, 2)

            def add_group(b, n):
                pe.wait_ge(added, (b * (NS // GROUP) + n // GROUP) * (GROUP - 1) + 2 * (GROUP - 1))
                if n == GROUP - 1 and not isinstance(b, int):
                    pe.wait_ge(y_ready, b * DC)
                for c in range(DC):
                    ins = pe.matmul(PS[c][:], ident[:], S[n % S_RING][:, c, :], start=(n == GROUP - 1), stop=(n == NS - 1))
                ins.then_inc(s_summed, 1)

            def turn_x(j0, n):
                xg = XG[n % 2][:].rearrange("p (q k) -> p k q", k=K)
                pe.wait_ge(xg_loaded[n % 2], block_of(j0, DMA) + (n // 2 + 1) * DMA)
                if not (isinstance(j0, int) and j0 + n == 0):
                    pe.wait_ge(xgt_copied, j0 + n)
                for k in range(K):
                    ins = pe.transpose(PS[4][:, k * P:(k + 1) * P], xg[:, k, :], ident[:])
                ins.then_inc(xgt_ready, 1)

            def up(j0, n):
                pe.wait_ge(xgt_copied, j0 + (n + 1))
                pe.wait_ge(gu_loaded[n % 2], block_of(j0, 2 * DMA) + (n // 2 + 1) * 2 * DMA)
                for k in range(K):
                    ins = pe.matmul(PS[5][:, 0:2 * F], XGT[n % 2][:, k, :],
                                    WGU[n % 2][:, k].rearrange("p g f -> p (g f)"), start=(k == 0), stop=(k == K - 1))
                ins.then_inc(up_ready, 1)

            def turn_h(j0, n):
                hh = HH[n % 2][:].rearrange("p (q k) -> p k q", k=2)
                pe.wait_ge(hh_ready, j0 + (n + 1))
                for k in range(2):
                    ins = pe.transpose(PS[6][0:FH, k * P:(k + 1) * P], hh[:, k, :], ident[:])
                ins.then_inc(ht_ready, 1)

            def down(j0, n):
                pe.wait_ge(ht_copied, j0 + (n + 1))
                pe.wait_ge(wd_loaded[n % 2], block_of(j0, DMA) + (n // 2 + 1) * DMA)
                pe.wait_ge(yt_ready, j0 + (n + 1))
                for k in range(2):
                    ins = pe.matmul(PS[7][:], HT[n % 2][:, k, :], WD[n % 2][:, k, :], start=(k == 0), stop=(k == 1))
                ins.then_inc(down_ready, 1)

            def block_of(j0, per):
                return j0 * (per // 2)

            def mixture_steps(b, last):
                j0 = b * NS - NS
                for n in range(NS):
                    turn_h(j0, n)
                    if n + 2 < NS:
                        turn_x(j0, n + 2)
                    elif not last:
                        turn_x(j0 + NS, n + 2 - NS)
                    if n + 1 < NS:
                        up(j0, n + 1)
                    elif not last:
                        up(j0 + NS, 0)
                    down(j0, n)
                    if n % GROUP == GROUP - 1:
                        add_group(b, n)

            for n in range(NS):
                if n % GROUP == GROUP - 1:
                    add_group(0, n)
                if n == NS - 5:
                    pe.wait_ge(slots_loaded, DMA)
                    pe.transpose(PS[6][:, 0:SLOT_TILES], slotf[:], ident[0:SLOT_TILES, 0:SLOT_TILES]).then_inc(slots_t, 1)
            pe.wait_ge(slots_ready, 1)
            turn_x(0, 0)
            up(0, 0)
            turn_x(0, 1)
            with pe.Fori(1, B - 1) as b:
                mixture_steps(b, False)
            mixture_steps(B - 1, True)

            def turn_gated(b):
                for c in range(DC):
                    pe.wait_ge(gate_ready, b * DC + (c + 1))
                    for t in range(T):
                        ins = pe.transpose(PS[t][:, c * P:(c + 1) * P], ZT[:, c, t * P:(t + 1) * P], ident[:])
                        if c == DC - 1:
                            ins.then_inc(gt_ready, 1)

            def combine_pe(b, ahead):
                if ahead:
                    pe.wait_ge(x3_ready, b * T + T)
                    turn_gated(b + 1)
                for t in range(T):
                    pe.wait_ge(xn3_ready, b * T + (t + 1))
                    if t >= 2:
                        pe.wait_ge(t3_copied, b * T + (t - 1))
                    four_transposes(ZN3[:, t, :], t, t3_ready)
                pe.wait_ge(t3_copied, b * T + T)
                for t in range(T):
                    for k in range(K):
                        ins = pe.matmul(PS[6][:, t * E2:(t + 1) * E2], XT3[:, k, t * P:(t + 1) * P], gate2T[:, k, :],
                                        start=(k == 0), stop=(k == K - 1))
                ins.then_inc(lg_ready, 1)
                pe.wait_ge(lg_copied, b + 1)

            pe.wait_ge(y_ready, B * DC)
            pe.sem_inc(t3_ready, T)
            turn_gated(0)
            with pe.Fori(0, B - 1) as b:
                combine_pe(b, 1)
            combine_pe(B - 1, 0)
            pe.wait_ge(lg_copied, B)
            for t in range(NT):
                ins = pe.matmul(PS[7][:, 0:E2], ones[:], logits[:, t, :], start=(t == 0), stop=(t == NT - 1))
            ins.then_inc(lsum_ready, 1)

            pe.wait_ge(b1_loaded, 2 * TOP * DMA)
            for k in range(TOP):
                ins = pe.transpose(PS[6][:, k * FT:(k + 1) * FT], b1n[:, k, :], ident[0:FT, 0:FT])
            ins.then_inc(b1_t, 1)
            pe.sem_inc(up2_ready, 2)
            pe.sem_inc(down2_done, 2)
            with pe.Fori(0, B) as tb:
                wait_apart(pe, xs_split, tb + 1)
                with pe.Fori(0, TOP) as e:
                    it = pe.snap(tb * (TOP * FT) + e * FT)

                    def up(f):
                        pe.wait_ge(w1l_ready, it + (f + 1))
                        for k in range(K):
                            for i, (w, v) in enumerate(((W1H, XSH), (W1H, XSL), (W1L, XSH))):
                                ins = pe.matmul(PS[4 + f % 2][:], w[f % 2][:, k, :], v[:, k, :],
                                                start=(k == 0 and i == 0), stop=(k == K - 1 and i == 2))
                        ins.then_inc(up2_ready, 1)

                    def down(f):
                        pe.wait_ge(hfl_ready, it + (f + 1))
                        pe.wait_ge(w2l_ready, it + (f + 1))
                        if f == 0:
                            pe.wait_ge(y2_added, tb * TOP + e + 1)
                        for t in range(T):
                            for i, (u_, w) in enumerate(((HFH, W2H), (HFH, W2L), (HFL, W2H))):
                                ins = pe.matmul(PS[t][:], u_[f % 2][:, t * P:(t + 1) * P], w[f % 2][:],
                                                start=(f == 0 and i == 0), stop=(f == FT - 1 and i == 2))
                        ins.then_inc(down2_done, 1)

                    up(0)
                    for f in range(FT):
                        if f + 1 < FT:
                            up(f + 1)
                        down(f)


_INS = ['x', 'ctx_1024', 'L0_xattn_Wq', 'L0_xattn_bq', 'L0_xattn_Wk', 'L0_xattn_bk', 'L0_ffn_router_w',
        'L0_ffn_gate_w', 'L0_ffn_up_w', 'L0_ffn_down_w', 'L1_xattn_in_proj_w', 'L1_xattn_conv_w',
        'L1_xattn_conv_b', 'L1_xattn_x_proj_w', 'L1_xattn_dt_proj_w', 'L1_xattn_dt_proj_b', 'L1_xattn_A_log',
        'L1_xattn_D', 'L1_ffn_gate_w', 'L1_ffn_w1', 'L1_ffn_b1', 'L1_ffn_w2', 'L1_ffn_b2']


def kernel(**inputs):
    import numpy as _np
    import concourse.bacc as _bacc
    from concourse import mybir as _mybir
    from concourse.bass_utils import run_bass_kernel_spmd as _run

    nc = _bacc.Bacc("TRN2", target_bir_lowering=False, num_devices=1)
    arrays, args = {}, []
    for name in _INS:
        a = _np.ascontiguousarray(inputs[name])
        arrays[f"in_{name}"] = a
        args.append(nc.dram_tensor(f"in_{name}", a.shape, _mybir.dt.from_np(a.dtype), kind="ExternalInput").ap())
    args.append(nc.dram_tensor("out_x", inputs["x"].shape, _mybir.dt.float32, kind="ExternalOutput").ap())
    build_program(nc, *args)
    r = _run(nc, [arrays], core_ids=[0])
    return r.results[0]["out_x"]
```

```python
from contextlib import ExitStack, contextmanager

import concourse.bass as bass
from concourse import mybir

ALU = mybir.AluOpType
ACT = mybir.ActivationFunctionType
AX = mybir.AxisListType.X
F32 = mybir.dt.float32
F32R = mybir.dt.float32r
I32 = mybir.dt.int32
U32 = mybir.dt.uint32
ds = bass.ds

P = 128
EPS = 1e-5
TOP = 2
DMA = 16
A_RING = 2
S_RING = 8
BC_RING = 4
GROUP = 2
AHEAD = 2
WQ = 4


class Steps:

    def __init__(self, eng, sem):
        self.eng, self.sem, self.n, self.base = eng, sem, 0, 0

    def mark(self, ins):
        ins.then_inc(self.sem, 1)
        self.n += 1

    def wait(self, apart=None):
        if apart:
            apart(self.eng, self.sem, self.base + self.n)
        else:
            self.eng.wait_ge(self.sem, self.base + self.n)

    @contextmanager
    def loop(self, trips, per):
        before = self.n
        with self.eng.Fori(0, trips) as i:
            self.base = i * per
            yield i
        assert self.n - before == per, f"{self.n - before} steps in the body, not {per}"
        self.base, self.n = 0, before + trips * per


def build_program(nc, x, ctx, Wq, bq, Wk, bk, router_w, gate_w, up_w, down_w, in_w, conv_w, conv_b,
                  xp_w, dtp_w, dtp_b, A_log, D_skip, gate2_w, w1, b1, w2, b2, out):
    B, L, DM = x.shape
    C = ctx.shape[2]
    CK = C // P
    T = L // P
    NT = B * T
    K = DM // P
    E, _, F = gate_w.shape
    FH = F // 2
    NS = A_log.shape[1]
    DI = in_w.shape[0]
    DC = DI // P
    R = dtp_w.shape[1]
    TAPS = conv_w.shape[2]
    XD = R + 2 * NS
    E2, _, FF = w1.shape
    FT = FF // P
    SLOT_TILES = B * L * TOP // P + E
    SLOTS = SLOT_TILES * P
    LONE = NS - GROUP
    OWN = range(3, LONE - BC_RING + 2, 2)
    SUMMED = NS // GROUP
    assert DC % GROUP == 0
    assert DI == DM == L and SLOT_TILES == (B - 1) * NS and F == 2 * FH and TAPS == 4 and E == NS

    def dram(name, shape):
        return nc.dram_tensor(name, shape, F32, kind="Internal").ap()

    u_dram = dram("u_spill", [B, P, DC * L])
    bc_dram = dram("bc_rows", [B, 2 * NS, L])
    x1_dram = dram("x1_spill", [NT, P, DM])
    xn_dram = dram("xn_rows", [B * L, DM])
    y_dram = dram("expert_rows", [SLOTS, DM])
    slot_dram = dram("slot_tokens", [SLOTS, 1])
    x3_dram = dram("x3_spill", [NT, P, DM])
    xt_dram = dram("xt_spill", [B, P, K * L])

    top = ExitStack()
    with top:
        def sem(name):
            return top.enter_context(nc.semaphore(name))

        def sb(stack, name, shape, dt=F32):
            return stack.enter_context(nc.sbuf_tensor(name, shape, dt))

        PS = [top.enter_context(nc.psum_tensor(f"bank{i}", [P, 512], F32)) for i in range(8)]


        ident = sb(top, "ident", [P, P])
        ones = sb(top, "ones", [P, P])
        gate2T = sb(top, "gate2T", [P, K, E2])
        minus_half = sb(top, "minus_half", [P, T])
        stats = sb(top, "stats", [P, T, 6])
        mv = sb(top, "mv", [P, T, 2])
        vare = sb(top, "vare", [P, T])
        rstd = sb(top, "rstd", [P, T])
        norm = (stats, mv, vare, rstd)
        iota_e = sb(top, "iota_e", [P, E])
        logits = sb(top, "logits", [P, NT, E2])
        rwf = sb(top, "rwf", [P, TOP, NT])
        lidx = sb(top, "lidx", [P, 8], U32)

        a = ExitStack()
        DT = sb(a, "DT", [P, B, DC, L])
        DTU = sb(a, "DTU", [P, B, DC, L])
        U = sb(a, "U", [P, DC, L])
        routerW = sb(a, "routerW", [P, K, E])
        qkb = sb(a, "qkb", [P, 2])
        convW = sb(a, "convW", [P, DC, TAPS])
        convB = sb(a, "convB", [P, DC])
        dtB = sb(a, "dtB", [P, DC])
        skip = sb(a, "skip", [P, DC])
        negA = sb(a, "negA", [P, DC, NS])
        SC = sb(a, "SC", [P, NT, E])
        rwt = sb(a, "rwt", [P, TOP, NT])
        pos = sb(a, "pos", [P, TOP, NT], I32)
        slot_tok = sb(a, "slot_tok", [P, SLOT_TILES], I32)
        tile_exp = sb(a, "tile_exp", [P, SLOT_TILES], I32)
        pcol = [sb(a, f"pcol{k}", [P, T], I32) for k in range(TOP)]

        s = ExitStack()
        zslots = sb(s, "zslots", [SLOT_TILES, P])
        XP = sb(s, "XP", [P, DC, L + TAPS - 1])
        XH = sb(s, "XH", [P, DC, L])
        ZZ = sb(s, "ZZ", [P, DC, L])
        ND = sb(s, "ND", [P, DC, L])
        RL = sb(s, "RL", [P, DC, L])
        xdb = sb(s, "xdb", [XD, L])
        ctxT = sb(s, "ctxT", [P, CK, B * L])
        wqkT = sb(s, "wqkT", [P, 2, CK, P])
        inT = sb(s, "inT", [P, CK, DI])
        xpT = sb(s, "xpT", [P, DC, XD])
        dtpT = sb(s, "dtpT", [R, DI])

        w = ExitStack()
        nat_qk = sb(w, "nat_qk", [P, 2, C])
        nat_in = sb(w, "nat_in", [P, DC, C])
        nat_xp = sb(w, "nat_xp", [XD, DI])
        nat_dtp = sb(w, "nat_dtp", [P, DC, R])
        nat_g2 = sb(w, "nat_g2", [E2, DM])
        nat_A = sb(w, "nat_A", [P, DC, NS])
        nat_ctx = sb(w, "nat_ctx", [P, NT, C])
        w.close()

        q = ExitStack()
        QKT = sb(q, "QKT", [P, 2, L])
        XNT = sb(q, "XNT", [P, K, L])
        ATT = sb(q, "ATT", [P, K, L])
        PR = sb(q, "PR", [P, T, L])
        X1A = sb(q, "X1A", [P, T, DM])
        XN1 = sb(q, "XN1", [P, T, DM])
        XN = sb(q, "XN", [P, T, DM])
        XB = sb(q, "XB", [P, T, DM])
        nmax = sb(q, "nmax", [P, T])
        nneg = sb(q, "nneg", [P, T])
        rsum = sb(q, "rsum", [P, T])
        rinv = sb(q, "rinv", [P, T])
        q.close()
        s.close()

        m = ExitStack()
        dA = [sb(m, f"dA{i}", [P, DC, L]) for i in range(A_RING)]
        S = [sb(m, f"S{i}", [P, DC, L]) for i in range(S_RING)]
        Bb = [sb(m, f"Bb{i}", [P, L]) for i in range(BC_RING)]
        Cb = [sb(m, f"Cb{i}", [P, L]) for i in range(BC_RING)]

        r = ExitStack()
        tri = sb(r, "tri", [P, P])
        M8 = sb(r, "M8", [P, NT, 8])
        I8 = sb(r, "I8", [P, NT, 8], U32)
        IF = sb(r, "IF", [P, TOP, NT])
        OH = sb(r, "OH", [P, TOP, NT, E])
        MM = sb(r, "MM", [P, NT, E])
        PX = sb(r, "PX", [P, NT + 1, E])
        PO = sb(r, "PO", [P, NT, E])
        PSEL = sb(r, "PSEL", [P, TOP, NT, E])
        posf = sb(r, "posf", [P, TOP, NT])
        cnt = sb(r, "cnt", [P, E])
        cnti = sb(r, "cnti", [P, E], I32)
        tiles = sb(r, "tiles", [P, E])
        incl = sb(r, "incl", [P, E])
        off = sb(r, "off", [P, E])
        iota_j = sb(r, "iota_j", [P, SLOT_TILES])
        cmpj = sb(r, "cmpj", [P, SLOT_TILES, E])
        texf = sb(r, "texf", [P, SLOT_TILES])
        tokid = sb(r, "tokid", [P, NT])
        diff = sb(r, "diff", [P, NT])
        ex = sb(r, "ex", [P, NT])
        den = sb(r, "den", [P, NT])
        slotf = sb(r, "slotf", [SLOT_TILES, P])
        r.close()

        f = ExitStack()
        WGU = [sb(f, f"WGU{i}", [P, K, 2, F]) for i in range(2)]
        WD = [sb(f, f"WD{i}", [FH, 2, DM]) for i in range(2)]
        XG = [sb(f, f"XG{i}", [P, DM]) for i in range(2)]
        XGT = [sb(f, f"XGT{i}", [P, K, P]) for i in range(2)]
        gcol = [sb(f, f"gcol{i}", [P, 1], I32) for i in range(2)]
        TG = [sb(f, f"TG{i}", [P, F]) for i in range(2)]
        HH = [sb(f, f"HH{i}", [P, F]) for i in range(2)]
        HT = [sb(f, f"HT{i}", [FH, 2, P]) for i in range(2)]
        YT = sb(f, "YT", [P, DM])
        f.close()
        m.close()

        g = ExitStack()
        X1 = sb(g, "X1", [P, T, DM])
        X2 = sb(g, "X2", [P, T, DM])
        X3 = sb(g, "X3", [P, T, DM])
        Y1 = sb(g, "Y1", [P, T, DM])
        Y2 = sb(g, "Y2", [P, T, DM])
        ZN = sb(g, "ZN", [P, T, DM])
        ZT = sb(g, "ZT", [P, T, DM])
        ZN3 = sb(g, "ZN3", [P, T, DM])
        XT3 = sb(g, "XT3", [P, K, L])
        norm3 = (sb(g, "stats3", [P, T, 6]), sb(g, "mv3", [P, T, 2]), sb(g, "vare3", [P, T]), sb(g, "rstd3", [P, T]))
        tsum = sb(g, "tsum", [P, E2])
        lsum = sb(g, "lsum", [P, E2])
        lmax = sb(g, "lmax", [P, 8])
        lidf = sb(g, "lidf", [P, TOP])
        lsel = sb(g, "lsel", [P, TOP, NT])
        loh = sb(g, "loh", [P, TOP, E2])
        ltmp = sb(g, "ltmp", [P, TOP, NT, E2])
        lme = sb(g, "lme", [P, NT])
        lden = sb(g, "lden", [P, NT])
        g.close()
        a.close()

        h = ExitStack()
        W1R = sb(h, "W1R", [P, TOP, K, FF])
        W2R = sb(h, "W2R", [P, TOP, FT, DM])
        W1H = [sb(h, f"W1H{i}", [P, K, P], F32R) for i in range(2)]
        W1L = [sb(h, f"W1L{i}", [P, K, P], F32R) for i in range(2)]
        W2H = [sb(h, f"W2H{i}", [P, DM], F32R) for i in range(2)]
        W2L = [sb(h, f"W2L{i}", [P, DM], F32R) for i in range(2)]
        HF = [sb(h, f"HF{i}", [P, L]) for i in range(2)]
        HFH = [sb(h, f"HFH{i}", [P, L], F32R) for i in range(2)]
        HFL = [sb(h, f"HFL{i}", [P, L], F32R) for i in range(2)]
        O = sb(h, "O", [P, T, DM])
        b1n = sb(h, "b1n", [FT, TOP, P])
        b1T = sb(h, "b1T", [P, TOP, FT])
        b2b = sb(h, "b2b", [P, TOP, DM])
        XS = sb(h, "XS", [P, K // 2, L])
        XSH = [sb(h, f"XSH{i}", [P, K, L], F32R) for i in range(2)]
        XSL = [sb(h, f"XSL{i}", [P, K, L], F32R) for i in range(2)]
        h.close()

        nat_loaded = sem("nat_loaded")
        small_loaded = sem("small_loaded")
        ctx_loaded = sem("ctx_loaded")
        slots_zeroed = sem("slots_zeroed")
        const_ready = sem("const_ready")
        pool_step = sem("pool_step")
        dve_step = sem("dve_step")
        small_ready = sem("small_ready")
        set_t = sem("set_t")
        set_c = sem("set_c")
        xin_ready = sem("xin_ready")
        xp_ready = sem("xp_ready")
        xh_ready = sem("xh_ready")
        u_ready = sem("u_ready")
        u_spilled = sem("u_spilled")
        xd_ready = sem("xd_ready")
        xd_copied = sem("xd_copied")
        bc_stored = sem("bc_stored")
        dtp_ready = sem("dtp_ready")
        abs_ready = sem("abs_ready")
        z_ready = sem("z_ready")
        r_ready = sem("r_ready")
        w_ready = sem("w_ready")
        ln_ready = sem("ln_ready")
        dt_ready = sem("dt_ready")

        xb_loaded = sem("xb_loaded")
        var_ready = sem("var_ready")
        rstd_ready = sem("rstd_ready")
        xn_ready = sem("xn_ready")
        qk_ready = sem("qk_ready")
        qk_copied = sem("qk_copied")
        t_ready = sem("t_ready")
        t_copied = sem("t_copied")
        e_ready = sem("e_ready")
        nneg_ready = sem("nneg_ready")
        exp_ready = sem("exp_ready")
        p_ready = sem("p_ready")
        o_ready = sem("o_ready")
        x1_ready = sem("x1_ready")
        x1_stored = sem("x1_stored")
        xn1_ready = sem("xn1_ready")
        xn1_stored = sem("xn1_stored")
        score_ready = sem("score_ready")
        score_copied = sem("score_copied")

        mask_ready = sem("mask_ready")
        rank_ready = sem("rank_ready")
        diff_ready = sem("diff_ready")
        ex_ready = sem("ex_ready")
        pos_ready = sem("pos_ready")
        tex_ready = sem("tex_ready")
        slots_set = sem("slots_set")
        slots_loaded = sem("slots_loaded")
        slots_t = sem("slots_t")
        slots_ready = sem("slots_ready")

        bb_loaded = [sem(f"bb_loaded{i}") for i in range(BC_RING)]
        cb_loaded = [sem(f"cb_loaded{i}") for i in range(BC_RING)]
        ul_loaded = sem("ul_loaded")
        da_ready = sem("da_ready")
        dbu_ready = sem("dbu_ready")
        own_ready = sem("own_ready")
        scan_done = sem("scan_done")
        hc_ready = sem("hc_ready")
        one_summed = sem("one_summed")
        added = sem("added")
        s_summed = sem("s_summed")
        y_ready = sem("y_ready")

        gu_loaded = [sem(f"gu_loaded{i}") for i in range(2)]
        wd_loaded = [sem(f"wd_loaded{i}") for i in range(2)]
        gcol_ready = sem("gcol_ready")
        xg_loaded = [sem(f"xg_loaded{i}") for i in range(2)]
        xgt_ready = sem("xgt_ready")
        xgt_copied = sem("xgt_copied")
        up_ready = sem("up_ready")
        tg_ready = sem("tg_ready")
        gg_ready = sem("gg_ready")
        hh_ready = sem("hh_ready")
        ht_ready = sem("ht_ready")
        ht_copied = sem("ht_copied")
        down_ready = sem("down_ready")
        yt_ready = sem("yt_ready")
        yt_stored = sem("yt_stored")

        x1_loaded = sem("x1_loaded")
        pcol_ready = sem("pcol_ready")
        y_loaded = [sem(f"y{k}_loaded") for k in range(TOP)]
        part_ready = sem("part_ready")
        x2_ready = sem("x2_ready")
        var2_ready = sem("var2_ready")
        rstd2_ready = sem("rstd2_ready")
        var3_ready = sem("var3_ready")
        rstd3_ready = sem("rstd3_ready")
        zn_ready = sem("zn_ready")
        zt_ready = sem("zt_ready")
        gate_ready = sem("gate_ready")
        gt_ready = sem("gt_ready")
        x3_ready = sem("x3_ready")
        x3_stored = sem("x3_stored")
        xn3_ready = sem("xn3_ready")
        t3_ready = sem("t3_ready")
        t3_copied = sem("t3_copied")
        xt3_stored = sem("xt3_stored")
        lg_ready = sem("lg_ready")
        lg_copied = sem("lg_copied")
        tsum_ready = sem("tsum_ready")
        lsum_ready = sem("lsum_ready")
        lidx_ready = sem("lidx_ready")
        lme_ready = sem("lme_ready")
        lexp_ready = sem("lexp_ready")
        rwf_ready = sem("rwf_ready")

        w1_loaded = [sem(f"w1_loaded{i}") for i in range(WQ)]
        w2_loaded = [sem(f"w2_loaded{i}") for i in range(WQ)]
        b1_loaded = sem("b1_loaded")
        b1_t = sem("b1_t")
        b1_ready = sem("b1_ready")
        xs_loaded = sem("xs_loaded")
        xs_split = sem("xs_split")
        w1h_ready = sem("w1h_ready")
        w1l_ready = sem("w1l_ready")
        w2h_ready = sem("w2h_ready")
        w2l_ready = sem("w2l_ready")
        xsh_ready = sem("xsh_ready")
        hfh_ready = sem("hfh_ready")
        ob_ready = sem("ob_ready")
        up2_ready = sem("up2_ready")
        hf_ready = sem("hf_ready")
        hfl_ready = sem("hfl_ready")
        down2_done = sem("down2_done")
        y2_added = sem("y2_added")
        o_loaded = sem("o_loaded")
        out_stored = sem("out_stored")

        def made(n):
            return BC_RING + len(OWN) + sum(i not in OWN for i in range(n + 1))

        wait_regs = {}

        def wait_apart(eng, sem_, value):
            if not isinstance(value, int):
                reg = wait_regs.setdefault(eng.engine, None) or eng.alloc_register(f"wait_value_{len(wait_regs)}")
                wait_regs[eng.engine] = reg
                eng.reg_mov(reg, value)
                eng.wait_ge(const_ready, 2)
                value = reg
            eng.wait_ge(sem_, value)

        def bank(i, parts, cols):
            return PS[i][0:parts, 0:cols]

        setup = [
            ([nat_qk[:, w, k * P:(k + 1) * P] for w in range(2) for k in range(CK)], P,
             P, wqkT[:].rearrange("p w k c -> p (w k c)")),
            *[([nat_in[:, c, k * P:(k + 1) * P] for c in range(DC)], P, P, inT[:, k, :]) for k in range(CK)],
            *[([nat_ctx[:, b * T + t, k * P:(k + 1) * P] for t in range(T)], P, P,
               ctxT[:, k, b * L:(b + 1) * L]) for b in range(B) for k in range(CK)],
            ([nat_xp[:, c * P:(c + 1) * P] for c in range(DC)], XD, P, xpT[:].rearrange("p c x -> p (c x)")),
            ([nat_dtp[:, c, :] for c in range(DC)], P, R, dtpT[:]),
            ([nat_g2[:, k * P:(k + 1) * P] for k in range(K)], E2, P, gate2T[:].rearrange("p k e -> p (k e)")),
        ]
        NAT_LOADS, SMALL_LOADS = 3, 11

        block = top.enter_context(nc.Block())

        @block.sync
        def _(sp):
            with nc.allow_non_contiguous_dma(reason="a few hundred words of weights"):
                sp.dma_start(nat_qk[:, 0, :], Wq).then_inc(nat_loaded, DMA)
                sp.dma_start(nat_qk[:, 1, :], Wk).then_inc(nat_loaded, DMA)
                sp.dma_start(nat_in[:], in_w.rearrange("(c p) k -> p c k", p=P)).then_inc(nat_loaded, DMA)
                sp.dma_start(nat_ctx[:], ctx.rearrange("b (t p) c -> p (b t) c", p=P)).then_inc(ctx_loaded, DMA)
                sp.dma_start(nat_xp[:], xp_w).then_inc(small_loaded, DMA)
                sp.dma_start(nat_dtp[:], dtp_w.rearrange("(c p) r -> p c r", p=P)).then_inc(small_loaded, DMA)
                sp.dma_start(nat_g2[:], gate2_w).then_inc(small_loaded, DMA)
                sp.dma_start(nat_A[:], A_log.rearrange("(c p) n -> p c n", p=P)).then_inc(small_loaded, DMA)
                sp.dma_start(convW[:], conv_w.rearrange("(c p) o t -> p c (o t)", p=P)).then_inc(small_loaded, DMA)
                sp.dma_start(convB[:], conv_b.rearrange("(c p) -> p c", p=P)).then_inc(small_loaded, DMA)
                sp.dma_start(dtB[:], dtp_b.rearrange("(c p) -> p c", p=P)).then_inc(small_loaded, DMA)
                sp.dma_start(skip[:], D_skip.rearrange("(c p) -> p c", p=P)).then_inc(small_loaded, DMA)
                sp.dma_start(qkb[:, 0:1], bq.rearrange("(p o) -> p o", o=1)).then_inc(small_loaded, DMA)
                sp.dma_start(qkb[:, 1:2], bk.rearrange("(p o) -> p o", o=1)).then_inc(small_loaded, DMA)
                sp.dma_start(routerW[:], router_w.rearrange("(k p) e -> p k e", p=P)).then_inc(small_loaded, DMA)
                sp.wait_ge(const_ready, 1)
                sp.dma_start(slot_dram.rearrange("(j p) o -> j (p o)", p=P), zslots[:]).then_inc(slots_zeroed, DMA)

            def load_x(b):
                sp.dma_start(XB[:], x[ds(b, 1)].rearrange("b (t p) d -> p (b t) d", p=P)).then_inc(xb_loaded, DMA)

            def sequence_transfers(b, last):
                sp.wait_ge(u_ready, b + 1)
                sp.dma_start(u_dram[ds(b, 1)].rearrange("b p f -> (b p) f"),
                             U[:].rearrange("p c l -> p (c l)")).then_inc(u_spilled, DMA)
                sp.wait_ge(x1_ready, (b + 1) * T)
                if not last:
                    load_x(b + 1)
                sp.dma_start(x1_dram[ds(b * T, T)].rearrange("t p d -> p t d"), X1A[:]).then_inc(x1_stored, DMA)
                sp.wait_ge(xd_copied, b + 1)
                sp.dma_start(bc_dram[ds(b, 1)].rearrange("b n l -> (b n) l"), xdb[R:XD, :]).then_inc(bc_stored, DMA)
                sp.wait_ge(xn1_ready, b + 1)
                sp.dma_start(xn_dram[ds(b * L, L), :].rearrange("(t p) d -> p t d", p=P),
                             XN1[:]).then_inc(xn1_stored, DMA)

            load_x(0)
            for stored in (u_spilled, bc_stored, x1_stored, xn1_stored):
                sp.sem_inc(stored, DMA)
            with sp.Fori(0, B - 1) as b:
                sequence_transfers(b, False)
            sequence_transfers(B - 1, True)

            def load_bc(b, n):
                if not isinstance(b, int) or b:
                    sp.wait_ge(dbu_ready, b * NS + (n + 1))
                elif n >= BC_RING and n - BC_RING in OWN:
                    sp.wait_ge(own_ready, OWN.index(n - BC_RING) + 1)
                elif n >= BC_RING:
                    sp.wait_ge(dbu_ready, made(n - BC_RING))
                sp.dma_start(Bb[n % BC_RING][:], bc_dram[ds(b, 1), n, :].to_broadcast([P, L])
                             ).then_inc(bb_loaded[n % BC_RING], DMA)
                sp.wait_ge(hc_ready, b * NS + (n + 1))
                sp.dma_start(Cb[n % BC_RING][:], bc_dram[ds(b, 1), NS + n, :].to_broadcast([P, L])
                             ).then_inc(cb_loaded[n % BC_RING], DMA)

            def load_u(b):
                sp.dma_start(U[:].rearrange("p c l -> p (c l)"),
                             u_dram[ds(b, 1)].rearrange("b p f -> (b p) f")).then_inc(ul_loaded, DMA)

            def load_expert(j0, n):
                j = j0 + n
                e = sp.value_load(tile_exp[0:1, ds(j, 1)], min_val=0, max_val=E - 1)
                sp.wait_ge(up_ready, j + 1)
                w = WGU[n % 2]
                for i, part in enumerate((gate_w, up_w)):
                    sp.dma_start(w[:, :, i, :], part[ds(e, 1)].rearrange("e (p k) f -> (e p) k f", p=P)
                                 ).then_inc(gu_loaded[n % 2], DMA)
                sp.wait_ge(down_ready, j + 1)
                sp.dma_start(WD[n % 2][:], down_w[ds(e, 1)].rearrange("e (p k) d -> (e p) k d", p=FH)
                             ).then_inc(wd_loaded[n % 2], DMA)

            sp.wait_ge(bc_stored, B * DMA + DMA)
            sp.wait_ge(u_spilled, B * DMA + DMA)
            sp.wait_ge(x1_stored, B * DMA + DMA)
            sp.wait_ge(xn1_stored, B * DMA + DMA)
            sp.wait_ge(dt_ready, B)
            sp.wait_ge(score_copied, B)
            load_u(0)
            for n in range(NS):
                load_bc(0, n)
                if n == NS - 3:
                    sp.wait_ge(slots_set, TOP * NT * DMA)
                    sp.dma_start(slotf[:], slot_dram.rearrange("(j p) o -> j (p o)", p=P)).then_inc(slots_loaded, DMA)
            sp.wait_ge(tex_ready, 1)
            sp.wait_ge(slots_ready, 1)

            def mixture_steps(b, last):
                for n in range(NS):
                    if n + 3 < NS:
                        load_bc(b, n + 3)
                    elif not last:
                        load_bc(b + 1, n + 3 - NS)
                    if n == NS // 2:
                        sp.wait_ge(y_ready, b * DC)
                        load_u(b)
                    if n + 1 < NS:
                        load_expert(b * NS - NS, n + 1)
                    elif not last:
                        load_expert(b * NS, 0)

            load_expert(0, 0)
            for n in range(3):
                load_bc(1, n)
            with sp.Fori(1, B - 1) as b:
                mixture_steps(b, False)
            mixture_steps(B - 1, True)

            def load_x1(b):
                sp.dma_start(X1[:], x1_dram[ds(b * T, T)].rearrange("t p d -> p t d")).then_inc(x1_loaded, DMA)

            def combine_transfers(b, ahead):
                sp.wait_ge(x3_ready, (b + 1) * T)
                sp.dma_start(x3_dram[ds(b * T, T)].rearrange("t p d -> p t d"), X3[:]).then_inc(x3_stored, DMA)
                if ahead > 1:
                    sp.wait_ge(x2_ready, (b + 2) * T)
                    load_x1(b + 2)
                sp.wait_ge(t3_copied, (b + 1) * T)
                sp.dma_start(xt_dram[ds(b, 1)].rearrange("b p f -> (b p) f"),
                             XT3[:].rearrange("p k l -> p (k l)")).then_inc(xt3_stored, DMA)

            sp.wait_ge(yt_stored, SLOT_TILES * DMA + DMA)
            sp.wait_ge(y_ready, B * DC)
            sp.sem_inc(x3_stored, DMA)
            sp.sem_inc(xt3_stored, DMA)
            load_x1(0)
            sp.wait_ge(x2_ready, T)
            load_x1(1)
            with sp.Fori(0, B - 2) as b:
                combine_transfers(b, 2)
            combine_transfers(B - 2, 1)
            combine_transfers(B - 1, 0)

            def load_xs(tb, i):
                if tb + i:
                    sp.wait_ge(xs_split, 2 * tb + i)
                sp.dma_start(XS[:].rearrange("p k l -> p (k l)"), xt_dram[tb, :, i * K // 2 * L:(i + 1) * K // 2 * L]
                             ).then_inc(xs_loaded, DMA)

            sp.wait_ge(xt3_stored, B * DMA + DMA)
            load_xs(0, 0)
            sp.wait_ge(x3_stored, B * DMA + DMA)
            sp.wait_ge(lidx_ready, 1)
            ev = [sp.value_load(lidx[0:1, k:k + 1], min_val=0, max_val=E2 - 1) for k in range(TOP)]
            FQ = FF // WQ

            def load_w1(k, i):
                sp.dma_start(W1R[:, k, :, i * FQ:(i + 1) * FQ], w1[ds(ev[k], 1), :, i * FQ:(i + 1) * FQ].rearrange(
                    "e (k p) f -> p (e k) f", p=P)).then_inc(w1_loaded[i], DMA)

            load_w1(0, 0)
            load_xs(0, 1)
            sp.wait_ge(rwf_ready, 1)
            for k in range(TOP):
                sp.dma_start(b1n[:, k, :], b1[ds(ev[k], 1)].rearrange("e (c p) -> (e c) p", p=P)).then_inc(b1_loaded, DMA)
                sp.dma_start(b2b[:, k, :], b2[ds(ev[k], 1), :].to_broadcast([P, DM])).then_inc(b1_loaded, DMA)
            for k in range(TOP):
                for i in range(WQ):
                    if k:
                        sp.wait_ge(w1_loaded[i], k * DMA)
                        sp.wait_ge(w2_loaded[i], k * DMA)
                    if k or i:
                        load_w1(k, i)
                    sp.dma_start(W2R[:, k, i * FT // WQ:(i + 1) * FT // WQ, :],
                                 w2[ds(ev[k], 1), i * FQ:(i + 1) * FQ, :].rearrange(
                                     "e (f p) d -> p (e f) d", p=P)).then_inc(w2_loaded[i], DMA)
            for tb in range(B):
                if tb + 1 < B:
                    load_xs(tb + 1, 0)
                if tb:
                    sp.wait_ge(out_stored, tb * DMA)
                sp.dma_start(O[:], x3_dram[tb * T:(tb + 1) * T].rearrange("t p d -> p t d")).then_inc(o_loaded, DMA)
                if tb + 1 < B:
                    load_xs(tb + 1, 1)
                sp.wait_ge(y2_added, (tb + 1) * TOP + 1)
                sp.dma_start(out[tb].rearrange("(t p) d -> p t d", p=P), O[:]).then_inc(out_stored, DMA)
            sp.wait_ge(out_stored, B * DMA)

        @block.gpsimd
        def _(pool):
            step = Steps(pool, pool_step)
            pool.memset(zslots[:], 0.0).then_inc(const_ready, 1)
            step.mark(pool.memset(ident[:], 0.0))
            step.mark(pool.memset(ones[:], 1.0))
            step.wait()
            pool.affine_select(out=ident[:], in_=ident[:], compare_op=ALU.not_equal, fill=1.0, base=0,
                               pattern=[[-1, P]], channel_multiplier=1).then_inc(const_ready, 1)
            pool.memset(minus_half[:], -0.5).then_inc(const_ready, 1)
            pool.iota(iota_e[:], pattern=[[1, E]], base=0, channel_multiplier=0,
                      allow_small_or_imprecise_dtypes=True).then_inc(const_ready, 1)
            pool.memset(XP[:], 0.0).then_inc(const_ready, 1)

            def rstd_of(count, ready, done):
                pool.wait_ge(ready, count)
                pool.tensor_tensor(rstd[:], vare[:], minus_half[:], ALU.pow).then_inc(done, 1)

            pool.wait_ge(const_ready, 5)
            rstd_of(1, var_ready, rstd_ready)
            with pool.Fori(0, B - 1) as b:
                rstd_of(b * 2 + 2, var_ready, rstd_ready)
                rstd_of(b * 2 + 3, var_ready, rstd_ready)
            rstd_of(2 * B, var_ready, rstd_ready)

            pool.wait_ge(score_copied, B)
            pool.wait_ge(x1_stored, B * DMA + DMA)
            pool.wait_ge(xn1_stored, B * DMA + DMA)
            pool.wait_ge(bc_stored, B * DMA + DMA)
            pool.wait_ge(dt_ready, B)
            pool.affine_select(out=tri[:], in_=ones[:], compare_op=ALU.is_gt, fill=0.0, base=0,
                               pattern=[[1, P]], channel_multiplier=-1).then_inc(const_ready, 1)
            pool.iota(iota_j[:], pattern=[[1, SLOT_TILES]], base=0, channel_multiplier=0,
                      allow_small_or_imprecise_dtypes=True).then_inc(const_ready, 1)
            pool.iota(tokid[:], pattern=[[P, NT]], base=0, channel_multiplier=1,
                      allow_small_or_imprecise_dtypes=True).then_inc(const_ready, 1)

            def scatter(k, t):
                pool.indirect_dma_start(
                    out=slot_dram, out_offset=bass.IndirectOffsetOnAxis(ap=pos[:, k, t:t + 1], axis=0),
                    in_=tokid[:, t:t + 1], in_offset=None).then_inc(slots_set, DMA)

            pool.sem_inc(dbu_ready, BC_RING + len(OWN))

            def dbu(b, n):
                group = b * (NS // GROUP) + n // GROUP
                pool.wait_ge(bb_loaded[n % BC_RING], b * (NS // BC_RING * DMA) + (n // BC_RING + 1) * DMA)
                if isinstance(b, int) and b == 0:
                    if n >= S_RING:
                        pool.wait_ge(one_summed, n - S_RING + 1)
                elif n % GROUP < GROUP - 1:
                    wait_apart(pool, added, group * (GROUP - 1) + (n % GROUP + 1))
                else:
                    wait_apart(pool, s_summed, group + (SUMMED + 1))
                pool.tensor_tensor(S[n % S_RING][:], DTU[:, ds(b, 1), :, :].rearrange("p b c l -> p (b c) l"),
                                   Bb[n % BC_RING][:].rearrange("p (o l) -> p o l", o=1).to_broadcast([P, DC, L]),
                                   ALU.mult).then_inc(dbu_ready, 1)

            def gather(j0, n):
                j = j0 + n
                pool.wait_ge(xgt_ready, j + 1)
                pool.tensor_copy(gcol[n % 2][:], slot_tok[:, ds(j, 1)]).then_inc(gcol_ready, 1)
                wait_apart(pool, gcol_ready, j + 1)
                pool.indirect_dma_start(out=XG[n % 2][:], out_offset=None, in_=xn_dram,
                                        in_offset=bass.IndirectOffsetOnAxis(ap=gcol[n % 2][:, 0:1], axis=0)
                                        ).then_inc(xg_loaded[n % 2], DMA)

            pool.wait_ge(dt_ready, B)
            per = TOP * NT // (NS // 2)
            BEFORE = 3
            for n in range(NS):
                if n not in OWN:
                    dbu(0, n)
                if n == BEFORE - 1:
                    pool.wait_ge(const_ready, 8)
                    pool.wait_ge(slots_zeroed, DMA)
                    pool.wait_ge(pos_ready, 1)
                if BEFORE <= n + 1 < BEFORE + NS // 2:
                    for i in range((n + 1 - BEFORE) * per, (n + 2 - BEFORE) * per):
                        scatter(i // NT, i % NT)
            pool.wait_ge(slots_ready, 1)

            def mixture_steps(b, last):
                for n in range(NS):
                    dbu(b, n)
                    if n + 2 < NS:
                        gather(b * NS - NS, n + 2)
                    elif not last:
                        gather(b * NS, n + 2 - NS)

            gather(0, 0)
            gather(0, 1)
            pool.wait_ge(one_summed, LONE)
            with pool.Fori(1, B - 1) as b:
                mixture_steps(b, False)
            mixture_steps(B - 1, True)

            def gather_y(b, k, y, count):
                pool.tensor_copy(pcol[k][:], pos[:, k, ds(b * T, T)]).then_inc(pcol_ready, 1)
                wait_apart(pool, pcol_ready, count)
                for t in range(T):
                    pool.indirect_dma_start(
                        out=y[:, t, :], out_offset=None, in_=y_dram,
                        in_offset=bass.IndirectOffsetOnAxis(ap=pcol[k][:, t:t + 1], axis=0)).then_inc(y_loaded[k], DMA)

            def rstd_and_gate(b):
                pool.wait_ge(var2_ready, b + 1)
                pool.tensor_tensor(rstd[:], vare[:], minus_half[:], ALU.pow).then_inc(rstd2_ready, 1)
                for c in range(DC):
                    wait_apart(pool, zt_ready, b * DC + (c + 1))
                    pool.tensor_tensor(ZT[:, c, :], ZT[:, c, :], DTU[:, ds(b, 1), c, :].rearrange("p b l -> p (b l)"),
                                       ALU.mult).then_inc(gate_ready, 1)

            def combine_pool(b, ahead):
                if ahead > 1:
                    pool.wait_ge(part_ready, (b + 2) * T)
                    gather_y(b + 2, 0, Y1, b * TOP + (2 * TOP + 1))
                pool.wait_ge(var3_ready, b + 1)
                pool.tensor_tensor(norm3[3][:], norm3[2][:], minus_half[:], ALU.pow).then_inc(rstd3_ready, 1)
                if ahead > 0:
                    rstd_and_gate(b + 1)
                if ahead > 1:
                    pool.wait_ge(x2_ready, (b + 2) * T)
                    gather_y(b + 2, 1, Y2, b * TOP + (2 * TOP + 2))

            pool.wait_ge(yt_stored, SLOT_TILES * DMA + DMA)
            pool.wait_ge(y_ready, B * DC)
            gather_y(0, 0, Y1, 1)
            gather_y(0, 1, Y2, 2)
            pool.wait_ge(part_ready, T)
            gather_y(1, 0, Y1, 3)
            rstd_and_gate(0)
            pool.wait_ge(x2_ready, T)
            gather_y(1, 1, Y2, 4)
            with pool.Fori(0, B - 2) as b:
                combine_pool(b, 2)
            combine_pool(B - 2, 1)
            combine_pool(B - 1, 0)

            pool.wait_ge(rwf_ready, 1)
            with pool.Fori(0, B) as tb:
                with pool.Fori(0, TOP) as e:
                    it = pool.snap(tb * (TOP * FT) + e * FT)
                    for f in range(FT):
                        pool.wait_ge(w1h_ready, it + (f + 1))
                        pool.tensor_tensor(W1L[f % 2][:],
                                           W1R[:, ds(e, 1), :, f * P:(f + 1) * P].rearrange("p e k f -> p (e k) f"),
                                           W1H[f % 2][:].bitcast(F32), ALU.subtract).then_inc(w1l_ready, 1)
                        pool.wait_ge(w2h_ready, it + (f + 1))
                        pool.tensor_tensor(W2L[f % 2][:], W2R[:, ds(e, 1), f, :].rearrange("p e d -> p (e d)"),
                                           W2H[f % 2][:].bitcast(F32), ALU.subtract).then_inc(w2l_ready, 1)

        @block.scalar
        def _(act):
            for i, (_, _, parts, dst) in enumerate(setup):
                act.wait_ge(set_t, i + 1)
                act.copy(dst, bank(4 + i % 2, parts, dst.shape[1])).then_inc(set_c, 1)

            act.wait_ge(small_loaded, SMALL_LOADS * DMA)
            act.activation(negA[:], nat_A[:], ACT.Exp).then_inc(small_ready, 1)
            act.wait_ge(small_ready, 1)
            act.mul(negA[:], negA[:], -1.0).then_inc(small_ready, 1)

            def copy_xin(b):
                for c in range(DC):
                    act.wait_ge(xin_ready, b * DC + (c + 1))
                    act.copy(XP[:, c, TAPS - 1:], PS[c][:]).then_inc(xp_ready, 1)

            def copy_t(count, dst, i):
                act.wait_ge(t_ready, count)
                act.copy(dst, PS[4 + i % 2][:].rearrange("p (k c) -> p k c", k=K)).then_inc(t_copied, 1)

            def sequence_act(b, last):
                act.wait_ge(qk_ready, b + 1)
                for w in range(2):
                    act.activation(QKT[:, w, :], PS[6 + w][:], ACT.Identity, bias=qkb[:, w:w + 1]).then_inc(qk_copied, 1)
                for t in range(2):
                    copy_t(b * 12 + (t + 1), XNT[:, :, t * P:(t + 1) * P], t)
                for t in range(T):
                    act.wait_ge(nneg_ready, b * T + (t + 1))
                    act.activation(PR[:, t, :], PS[6 + t % 2][:], ACT.Exp, bias=nneg[:, t:t + 1],
                                   accum_out=rsum[:, t:t + 1]).then_inc(exp_ready, 1)
                for t in range(2, T):
                    copy_t(b * 12 + (t + 1), XNT[:, :, t * P:(t + 1) * P], t)
                for t in range(T):
                    copy_t(b * 12 + (T + t + 1), ATT[:, :, t * P:(t + 1) * P], t)
                act.wait_ge(xh_ready, b + 1)
                act.wait_ge(u_spilled, b * DMA + DMA)
                act.activation(U[:], XH[:], ACT.Silu).then_inc(u_ready, 1)
                act.wait_ge(xd_ready, b + 1)
                act.wait_ge(bc_stored, b * DMA + DMA)
                act.copy(xdb[:], PS[0][0:XD, :]).then_inc(xd_copied, 1)
                for t in range(T):
                    copy_t(b * 12 + (2 * T + t + 1), XNT[:, :, t * P:(t + 1) * P], t)
                for c in range(DC):
                    act.wait_ge(r_ready, b * DC + (c + 1))
                    act.activation(ZZ[:, c, :], PS[c][:], ACT.Abs, bias=dtB[:, c:c + 1]).then_inc(abs_ready, 1)
                act.wait_ge(abs_ready, b * DC + DC)
                act.activation(ZZ[:], ZZ[:], ACT.Exp, scale=-1.0).then_inc(z_ready, 1)
                wait_apart(act, score_ready, b + 1)
                act.copy(SC[:, ds(b * T, T), :], PS[6][:, 0:T * E].rearrange("p (t e) -> p t e", t=T)
                         ).then_inc(score_copied, 1)
                act.wait_ge(w_ready, b * 2 + 2)
                act.activation(ZZ[:], XH[:], ACT.Ln).then_inc(ln_ready, 1)
                if not last:
                    copy_xin(b + 1)

            act.wait_ge(const_ready, 5)
            copy_xin(0)
            with act.Fori(0, B - 1) as b:
                sequence_act(b, False)
            sequence_act(B - 1, True)

            act.wait_ge(diff_ready, 1)
            act.activation(ex[:], diff[:], ACT.Exp).then_inc(ex_ready, 1)

            def decay(b, n):
                u = b * NS + n
                wait_apart(act, scan_done, u + 1)
                for c in range(DC):
                    ins = act.activation(
                        dA[n % A_RING][:, c, 1:], DT[:, ds(b, 1), c, 1:].rearrange("p b l -> p (b l)"),
                        ACT.Exp, scale=negA[:, c, n:n + 1])
                ins.then_inc(da_ready, 1)

            def copy_xg(j0, n):
                j = j0 + n
                act.wait_ge(xgt_ready, j + 3)
                act.copy(XGT[n % 2][:], PS[4][:].rearrange("p (k t) -> p k t", k=K)).then_inc(xgt_copied, 1)

            def tanh_g(j0, n):
                act.wait_ge(up_ready, j0 + (n + 3))
                act.activation(TG[n % 2][:], PS[5][:, 0:F], ACT.Tanh, scale=0.5).then_inc(tg_ready, 1)

            def copy_ht(j0, n):
                act.wait_ge(ht_ready, j0 + (n + 1))
                act.copy(HT[n % 2][:], PS[6][0:FH, 0:2 * P].rearrange("p (k t) -> p k t", k=2)).then_inc(ht_copied, 1)

            def copy_y(j0, n):
                j = j0 + n
                act.wait_ge(down_ready, j + 3)
                act.wait_ge(yt_stored, j * DMA + DMA)
                act.copy(YT[:], PS[7][:]).then_inc(yt_ready, 1)

            def store_y(j0, n):
                j = j0 + n
                act.wait_ge(yt_ready, j + 2)
                act.dma_start(y_dram[ds(j * P, P), :], YT[:]).then_inc(yt_stored, DMA)

            act.wait_ge(dt_ready, B)
            act.wait_ge(scan_done, A_RING)
            for n in range(NS):
                decay(0, n)
            act.wait_ge(slots_ready, 1)
            act.sem_inc(yt_ready, 1)
            act.sem_inc(yt_stored, DMA)

            def mixture_steps(b, last):
                j0 = b * NS - NS
                for n in range(NS):
                    if n + AHEAD < NS:
                        decay(b, n + AHEAD)
                    elif not last:
                        decay(b + 1, n + AHEAD - NS)
                    copy_ht(j0, n)
                    if n + 2 < NS:
                        copy_xg(j0, n + 2)
                    elif not last:
                        copy_xg(j0 + NS, n + 2 - NS)
                    if n + 1 < NS:
                        tanh_g(j0, n + 1)
                    elif not last:
                        tanh_g(j0 + NS, 0)
                    copy_y(j0, n)
                    store_y(j0, n)

            copy_xg(0, 0)
            tanh_g(0, 0)
            copy_xg(0, 1)
            for n in range(AHEAD):
                decay(1, n)
            with act.Fori(1, B - 1) as b:
                mixture_steps(b, False)
            mixture_steps(B - 1, True)

            def silu_z(b):
                for c in range(DC):
                    act.wait_ge(zn_ready, b * DC + (c + 1))
                    act.activation(ZT[:, c, :], ZN[:, c, :], ACT.Silu).then_inc(zt_ready, 1)

            def combine_act(b, ahead):
                if ahead:
                    silu_z(b + 1)
                act.wait_ge(xt3_stored, b * DMA + DMA)
                for t in range(T):
                    act.wait_ge(t3_ready, b * T + (T + t + 1))
                    act.copy(XT3[:, :, t * P:(t + 1) * P],
                             PS[4 + t % 2][:].rearrange("p (k c) -> p k c", k=K)).then_inc(t3_copied, 1)
                wait_apart(act, lg_ready, b + 1)
                act.copy(logits[:, ds(b * T, T), :],
                         PS[6][:, 0:T * E2].rearrange("p (t e) -> p t e", t=T)).then_inc(lg_copied, 1)

            silu_z(0)
            with act.Fori(0, B - 1) as b:
                combine_act(b, 1)
            combine_act(B - 1, 0)
            act.wait_ge(lme_ready, 1)
            act.activation(lsel[:], lsel[:], ACT.Exp).then_inc(lexp_ready, 1)

            act.wait_ge(b1_t, 1)
            act.copy(b1T[:], PS[6][:, 0:TOP * FT].rearrange("p (k f) -> p k f", k=TOP)).then_inc(b1_ready, 1)
            act.wait_ge(b1_ready, 1)
            with act.Fori(0, B) as tb:
                with act.Fori(0, TOP) as e:
                    it = act.snap(tb * (TOP * FT) + e * FT)

                    def split_w1(f):
                        if f % (FT // WQ) == 0:
                            act.wait_ge(w1_loaded[f // (FT // WQ)], e * DMA + DMA)
                        act.wait_ge(up2_ready, it + (f + 1))
                        act.copy(W1H[f % 2][:], W1R[:, ds(e, 1), :, f * P:(f + 1) * P].rearrange(
                            "p e k f -> p (e k) f")).then_inc(w1h_ready, 1)

                    def split_w2(f):
                        if f % (FT // WQ) == 0:
                            act.wait_ge(w2_loaded[f // (FT // WQ)], e * DMA + DMA)
                        act.wait_ge(down2_done, it + (f + 1))
                        act.copy(W2H[f % 2][:], W2R[:, ds(e, 1), f, :].rearrange("p e d -> p (e d)")
                                 ).then_inc(w2h_ready, 1)

                    def gelu(f):
                        wait_apart(act, up2_ready, it + (f + 3))
                        act.activation(HF[f % 2][:], PS[4 + f % 2][:], ACT.Gelu_apprx_tanh,
                                       bias=b1T[:, ds(e, 1), f:f + 1].rearrange("p e f -> p (e f)")).then_inc(hf_ready, 1)

                    split_w1(0)
                    split_w2(0)
                    for f in range(FT):
                        if f + 1 < FT:
                            split_w1(f + 1)
                        gelu(f)
                        if f + 1 < FT:
                            split_w2(f + 1)

        @block.vector
        def _(dve):
            step = Steps(dve, dve_step)
            dve.wait_ge(small_loaded, SMALL_LOADS * DMA)
            def layernorm(src, dst, count, ready, got, done):
                for t in range(T):
                    ins = dve.bn_stats(stats[:, t, :], src[:, t, :])
                step.mark(ins)
                step.wait(apart=wait_apart)
                for t in range(T):
                    ins = dve.bn_aggr(mv[:, t, :], stats[:, t, :])
                step.mark(ins)
                step.wait()
                dve.tensor_scalar(vare[:].rearrange("p (t o) -> p t o", o=1), mv[:, :, 1:2], EPS, None,
                                  ALU.add).then_inc(ready, 1)
                dve.wait_ge(got, count)
                for t in range(T):
                    ins = dve.tensor_scalar(dst[:, t, :], src[:, t, :], mv[:, t, 0:1], rstd[:, t:t + 1],
                                            ALU.subtract, ALU.mult)
                ins.then_inc(done, 1)

            def layernorm_x(b):
                dve.wait_ge(xb_loaded, b * DMA + DMA)
                layernorm(XB, XN, b * 2 + 1, var_ready, rstd_ready, xn_ready)

            def softmax(b):
                def row_max(t):
                    dve.wait_ge(e_ready, b * T + (t + 1))
                    step.mark(dve.tensor_reduce(nmax[:, t:t + 1], PS[6 + t % 2][:], AX, ALU.max))
                    step.wait()
                    dve.tensor_scalar(nneg[:, t:t + 1], nmax[:, t:t + 1], -1.0, None, ALU.mult).then_inc(nneg_ready, 1)

                def normalize(t):
                    dve.wait_ge(exp_ready, b * T + (t + 1))
                    step.mark(dve.reciprocal(rinv[:, t:t + 1], rsum[:, t:t + 1]))
                    step.wait()
                    dve.tensor_scalar(PR[:, t, :], PR[:, t, :], rinv[:, t:t + 1], None, ALU.mult).then_inc(p_ready, 1)

                row_max(0)
                row_max(1)
                for t in range(T):
                    normalize(t)
                    if t + 2 < T:
                        row_max(t + 2)

            def convolve(b):
                for c in range(DC):
                    dve.wait_ge(xp_ready, b * DC + (c + 1))
                    step.mark(dve.tensor_scalar(XH[:, c, :], XP[:, c, TAPS - 1:], convW[:, c, TAPS - 1:TAPS],
                                                convB[:, c:c + 1], ALU.mult, ALU.add))
                for j in range(TAPS - 1):
                    for c in range(DC):
                        if c == 0:
                            step.wait()
                        ins = dve.scalar_tensor_tensor(XH[:, c, :], XP[:, c, j:j + L], convW[:, c, j:j + 1],
                                                       XH[:, c, :], ALU.mult, ALU.add)
                        if j < TAPS - 2:
                            step.mark(ins)
                ins.then_inc(xh_ready, 1)

            def positive_part(b):
                for c in range(DC):
                    dve.wait_ge(dtp_ready, b * DC + (c + 1))
                    dve.tensor_scalar(RL[:, c, :], PS[c][:], dtB[:, c:c + 1], 0.0, ALU.add, ALU.max).then_inc(r_ready, 1)

            def softplus(b):
                dt, dtu = (a_[:, ds(b, 1)].rearrange("p b c l -> p (b c) l") for a_ in (DT, DTU))
                dve.wait_ge(z_ready, b + 1)
                dve.tensor_scalar(XH[:], ZZ[:], 1.0, None, ALU.add).then_inc(w_ready, 1)
                dve.wait_ge(w_ready, b * 2 + 1)
                dve.scalar_tensor_tensor(ND[:], XH[:], 1.0, ZZ[:], ALU.subtract, ALU.subtract).then_inc(w_ready, 1)
                dve.wait_ge(w_ready, b * 2 + 2)
                step.mark(dve.tensor_tensor(RL[:], RL[:], ND[:], ALU.subtract))
                dve.wait_ge(ln_ready, b + 1)
                step.wait()
                step.mark(dve.tensor_tensor(dt, RL[:], ZZ[:], ALU.add))
                step.wait()
                dve.tensor_tensor(dtu, dt, U[:], ALU.mult).then_inc(dt_ready, 1)

            def sequence_dve(b, last):
                softmax(b)
                convolve(b)
                dve.wait_ge(x1_stored, b * DMA + DMA)
                for t in range(T):
                    dve.wait_ge(o_ready, b * T + (t + 1))
                    dve.tensor_tensor(X1A[:, t, :], PS[6 + t % 2][:], XB[:, t, :], ALU.add).then_inc(x1_ready, 1)
                dve.wait_ge(x1_ready, b * T + T)
                dve.wait_ge(xn1_stored, b * DMA + DMA)
                layernorm(X1A, XN1, b * 2 + 2, var_ready, rstd_ready, xn1_ready)
                positive_part(b)
                if not last:
                    layernorm_x(b + 1)
                softplus(b)

            layernorm_x(0)
            with step.loop(B - 1, 3 * DC + 2 + 4 + 2 * T) as b:
                sequence_dve(b, False)
            sequence_dve(B - 1, True)

            def do(ins):
                step.mark(ins)
                step.wait()

            dve.wait_ge(score_copied, B)
            dve.wait_ge(x1_stored, B * DMA + DMA)
            dve.wait_ge(xn1_stored, B * DMA + DMA)
            dve.wait_ge(bc_stored, B * DMA + DMA)
            dve.wait_ge(slots_zeroed, DMA)
            for t in range(NT):
                ins = dve.max(M8[:, t, :], SC[:, t, :])
            do(ins)
            for t in range(NT):
                ins = dve.max_index(I8[:, t, :], M8[:, t, :], SC[:, t, :])
            dve.tensor_tensor(diff[:].rearrange("p (t o) -> p t o", o=1), M8[:, :, 1:2], M8[:, :, 0:1],
                              ALU.subtract).then_inc(diff_ready, 1)
            do(ins)
            for k in range(TOP):
                ins = dve.tensor_copy(IF[:, k, :].rearrange("p (t o) -> p t o", o=1), I8[:, :, k:k + 1])
            do(ins)
            dve.wait_ge(const_ready, 4)
            for k in range(TOP):
                ins = dve.tensor_tensor(OH[:, k], iota_e[:].rearrange("p (o e) -> p o e", o=1).to_broadcast([P, NT, E]),
                                        IF[:, k, :].rearrange("p (t o) -> p t o", o=1).to_broadcast([P, NT, E]),
                                        ALU.is_equal)
            do(ins)
            dve.tensor_tensor(MM[:], OH[:, 0], OH[:, 1], ALU.add).then_inc(mask_ready, 1)
            dve.wait_ge(ex_ready, 1)
            do(dve.tensor_scalar(den[:], ex[:], 1.0, None, ALU.add))
            do(dve.reciprocal(rwt[:, 0, :], den[:]))
            do(dve.tensor_tensor(rwt[:, 1, :], ex[:], rwt[:, 0, :], ALU.mult))
            dve.wait_ge(rank_ready, 1)
            do(dve.memset(PX[:, 0, :], 0.0))
            totals = PS[5][:, 0:NT * E].rearrange("p (t e) -> p t e", t=NT)
            for t in range(NT):
                do(dve.tensor_tensor(PX[:, t + 1, :], PX[:, t, :], totals[:, t, :], ALU.add))
            do(dve.tensor_tensor(PO[:], PX[:, 0:NT, :], PS[4][:, 0:NT * E].rearrange("p (t e) -> p t e", t=NT), ALU.add))
            do(dve.tensor_scalar(cnt[:], PX[:, NT, :], (P - 1) / 2, 1 / P, ALU.add, ALU.mult))
            do(dve.tensor_copy(cnti[:], cnt[:]))
            do(dve.tensor_copy(tiles[:], cnti[:]))
            do(dve.tensor_tensor_scan(incl[:], ones[:, 0:E], tiles[:], 0.0, ALU.mult, ALU.add))
            do(dve.tensor_tensor(off[:], incl[:], tiles[:], ALU.subtract))
            do(dve.tensor_scalar(off[:], off[:], float(P), None, ALU.mult))
            do(dve.tensor_tensor(PO[:], PO[:], off[:].rearrange("p (o e) -> p o e", o=1).to_broadcast([P, NT, E]), ALU.add))
            for k in range(TOP):
                ins = dve.tensor_tensor(PSEL[:, k], OH[:, k], PO[:], ALU.mult)
            do(ins)
            for k in range(TOP):
                ins = dve.tensor_reduce(posf[:, k, :].rearrange("p (t o) -> p t o", o=1), PSEL[:, k], AX, ALU.add)
            do(ins)
            dve.tensor_copy(pos[:], posf[:]).then_inc(pos_ready, 1)
            dve.wait_ge(const_ready, 8)
            do(dve.tensor_tensor(cmpj[:], incl[:].rearrange("p (o e) -> p o e", o=1).to_broadcast([P, SLOT_TILES, E]),
                                 iota_j[:].rearrange("p (j o) -> p j o", o=1).to_broadcast([P, SLOT_TILES, E]),
                                 ALU.is_le))
            do(dve.tensor_reduce(texf[:].rearrange("p (j o) -> p j o", o=1), cmpj[:], AX, ALU.add))
            do(dve.tensor_scalar(texf[:], texf[:], float(E - 1), None, ALU.min))
            dve.tensor_copy(tile_exp[:], texf[:]).then_inc(tex_ready, 1)
            for i in range(A_RING):
                ins = dve.memset(dA[i][:, :, 0:1], 0.0)
                ins.then_inc(scan_done, 1)
            dve.sem_inc(hc_ready, BC_RING)
            dve.sem_inc(added, (GROUP - 1) * (LONE // GROUP + S_RING // GROUP))

            def own_dbu(n):
                if n >= S_RING:
                    dve.wait_ge(one_summed, n - S_RING + 1)
                dve.wait_ge(bb_loaded[n % BC_RING], (n // BC_RING + 1) * DMA)
                dve.tensor_tensor(S[n % S_RING][:], DTU[:, 0], Bb[n % BC_RING][:].rearrange(
                    "p (o l) -> p o l", o=1).to_broadcast([P, DC, L]), ALU.mult).then_inc(own_ready, 1)

            def scan(b, n):
                u = b * NS + n
                dve.wait_ge(da_ready, u + 1)
                if not isinstance(b, int) or b:
                    dve.wait_ge(dbu_ready, u + (BC_RING + 1))
                elif n in OWN:
                    own_dbu(n)
                    dve.wait_ge(own_ready, OWN.index(n) + 1)
                else:
                    dve.wait_ge(dbu_ready, made(n))
                s_ = S[n % S_RING]
                flat = s_[:].rearrange("p c l -> p (c l)")
                dve.tensor_tensor_scan(flat, dA[n % A_RING][:].rearrange("p c l -> p (c l)"), flat, 0.0,
                                       ALU.mult, ALU.add).then_inc(scan_done, 1)
                dve.wait_ge(cb_loaded[n % BC_RING], b * (NS // BC_RING * DMA) + (n // BC_RING + 1) * DMA)
                dve.wait_ge(scan_done, u + (A_RING + 1))
                dve.tensor_tensor(s_[:], s_[:], Cb[n % BC_RING][:].rearrange("p (o l) -> p o l", o=1).to_broadcast([P, DC, L]),
                                  ALU.mult).then_inc(hc_ready, 1)
                if n % GROUP and not (isinstance(b, int) and b == 0 and n < LONE):
                    dve.wait_ge(hc_ready, u + (BC_RING + 1))
                    if n % GROUP > 1:
                        dve.wait_ge(added, (b * (NS // GROUP) + n // GROUP + S_RING // GROUP) * (GROUP - 1) + (n % GROUP - 1))
                    dve.tensor_tensor(s_[:], s_[:], S[n % S_RING - 1][:], ALU.add).then_inc(added, 1)

            def take_y(b):
                dve.wait_ge(s_summed, b * (NS // GROUP) + (SUMMED + NS // GROUP + S_RING // GROUP))
                dve.wait_ge(ul_loaded, b * DMA + DMA)
                for c in range(DC):
                    dve.scalar_tensor_tensor(DTU[:, ds(b, 1), c, :].rearrange("p b l -> p (b l)"), U[:, c, :],
                                             skip[:, c:c + 1], PS[c][:], ALU.mult, ALU.add).then_inc(y_ready, 1)

            def silu_h(j0, n):
                dve.wait_ge(tg_ready, j0 + (n + 1))
                dve.scalar_tensor_tensor(TG[n % 2][:], TG[n % 2][:], 1.0, PS[5][:, 0:F], ALU.add,
                                         ALU.mult).then_inc(gg_ready, 1)
                dve.wait_ge(gg_ready, j0 + (n + 1))
                dve.scalar_tensor_tensor(HH[n % 2][:], TG[n % 2][:], 0.5, PS[5][:, F:2 * F], ALU.mult,
                                         ALU.mult).then_inc(hh_ready, 1)

            for n in range(NS):
                scan(0, n)
                if n == NS - 4:
                    dve.wait_ge(slots_t, 1)
                    dve.tensor_copy(slot_tok[:], PS[6][:, 0:SLOT_TILES]).then_inc(slots_ready, 1)

            def mixture_steps(b, last):
                j0 = b * NS - NS
                for n in range(NS):
                    if n + 1 < NS:
                        scan(b, n + 1)
                        silu_h(j0, n + 1)
                    elif not last:
                        scan(b + 1, 0)
                        silu_h(j0 + NS, 0)
                    if n == GROUP - 2:
                        take_y(b - 1)

            scan(1, 0)
            silu_h(0, 0)
            with dve.Fori(1, B - 1) as b:
                mixture_steps(b, False)
            mixture_steps(B - 1, True)
            take_y(B - 1)

            def statistics(src, norm, ready):
                stats, mv, vare, _ = norm
                for t in range(T):
                    ins = dve.bn_stats(stats[:, t, :], src[:, t, :])
                step.mark(ins)
                step.wait(apart=wait_apart)
                for t in range(T):
                    ins = dve.bn_aggr(mv[:, t, :], stats[:, t, :])
                step.mark(ins)
                step.wait()
                dve.tensor_scalar(vare[:].rearrange("p (t o) -> p t o", o=1), mv[:, :, 1:2], EPS, None,
                                  ALU.add).then_inc(ready, 1)

            def normalized(dst, src, norm, got, count, done):
                _, mv, _, rstd = norm
                dve.wait_ge(got, count)
                for t in range(T):
                    dve.tensor_scalar(dst[:, t, :], src[:, t, :], mv[:, t, 0:1], rstd[:, t:t + 1],
                                      ALU.subtract, ALU.mult).then_inc(done, 1)

            def add_first(b):
                dve.wait_ge(x1_loaded, b * DMA + DMA)
                dve.wait_ge(y_loaded[0], b * (T * DMA) + T * DMA)
                for t in range(T):
                    dve.scalar_tensor_tensor(X1[:, t, :], Y1[:, t, :], rwt[:, 0, ds(b * T + t, 1)], X1[:, t, :],
                                             ALU.mult, ALU.add).then_inc(part_ready, 1)

            def add_second(b):
                dve.wait_ge(y_loaded[1], b * (T * DMA) + T * DMA)
                for t in range(T):
                    dve.wait_ge(part_ready, b * T + (t + 1))
                    dve.scalar_tensor_tensor(X2[:, t, :], Y2[:, t, :], rwt[:, 1, ds(b * T + t, 1)], X1[:, t, :],
                                             ALU.mult, ALU.add).then_inc(x2_ready, 1)
                dve.wait_ge(x2_ready, b * T + T)
                statistics(X2, norm, var2_ready)

            def combine(b, ahead):
                dve.wait_ge(x3_stored, b * DMA + DMA)
                for t in range(T):
                    dve.wait_ge(gt_ready, b * T + (t + 1))
                    dve.tensor_tensor(X3[:, t, :], PS[t][:], X2[:, t, :], ALU.add).then_inc(x3_ready, 1)
                dve.wait_ge(x3_ready, b * T + T)
                statistics(X3, norm3, var3_ready)
                if ahead > 0:
                    add_second(b + 1)
                    normalized(ZN, X2, norm, rstd2_ready, b + 2, zn_ready)
                dve.wait_ge(t3_ready, b * T + T)
                normalized(ZN3, X3, norm3, rstd3_ready, b + 1, xn3_ready)
                if ahead > 1:
                    add_first(b + 2)
                dve.wait_ge(xn3_ready, b * T + T)

            add_first(0)
            add_second(0)
            normalized(ZN, X2, norm, rstd2_ready, 1, zn_ready)
            add_first(1)
            with step.loop(B - 2, 4) as b:
                combine(b, 2)
            combine(B - 2, 1)
            combine(B - 1, 0)
            dve.wait_ge(lg_copied, B)
            dve.tensor_reduce(tsum[:].rearrange("p (e o) -> p e o", o=1), logits[:].rearrange("p t e -> p e t"), AX,
                              ALU.add).then_inc(tsum_ready, 1)

            dve.wait_ge(lsum_ready, 1)
            do(dve.tensor_copy(lsum[:], PS[7][:, 0:E2]))
            do(dve.max(lmax[:], lsum[:]))
            dve.max_index(lidx[:], lmax[:], lsum[:]).then_inc(lidx_ready, 1)
            dve.wait_ge(lidx_ready, 1)
            do(dve.tensor_copy(lidf[:], lidx[:, 0:TOP]))
            for k in range(TOP):
                ins = dve.tensor_scalar(loh[:, k, :], iota_e[:, 0:E2], lidf[:, k:k + 1], None, ALU.is_equal)
            do(ins)
            for k in range(TOP):
                ins = dve.tensor_tensor(ltmp[:, k], logits[:], loh[:, k:k + 1, :].to_broadcast([P, NT, E2]), ALU.mult)
            do(ins)
            for k in range(TOP):
                ins = dve.tensor_reduce(lsel[:, k, :].rearrange("p (t o) -> p t o", o=1), ltmp[:, k], AX, ALU.add)
            do(ins)
            do(dve.tensor_tensor(lme[:], lsel[:, 0, :], lsel[:, 1, :], ALU.max))
            dve.tensor_tensor(lsel[:], lsel[:], lme[:].rearrange("p (o t) -> p o t", o=1).to_broadcast([P, TOP, NT]),
                              ALU.subtract).then_inc(lme_ready, 1)
            dve.wait_ge(lexp_ready, 1)
            do(dve.tensor_tensor(lden[:], lsel[:, 0, :], lsel[:, 1, :], ALU.add))
            do(dve.reciprocal(lme[:], lden[:]))
            dve.tensor_tensor(rwf[:], lsel[:], lme[:].rearrange("p (o t) -> p o t", o=1).to_broadcast([P, TOP, NT]),
                              ALU.mult).then_inc(rwf_ready, 1)

            dve.sem_inc(y2_added, 1)

            def split_x(tb, i):
                if tb >= 2:
                    dve.wait_ge(up2_ready, (tb - 1) * (TOP * FT) + 2)
                hi, lo = (w[tb % 2][:, ds(i * (K // 2), K // 2), :] for w in (XSH, XSL))
                dve.wait_ge(xs_loaded, i * DMA + (2 * tb + 1) * DMA)
                dve.tensor_copy(hi, XS[:]).then_inc(xsh_ready, 1)
                dve.wait_ge(xsh_ready, i + (2 * tb + 1))
                dve.tensor_tensor(lo, XS[:], hi.bitcast(F32), ALU.subtract).then_inc(xs_split, 1)

            for i in range(2):
                split_x(0, i)

            for tb in range(B):
                with dve.Fori(0, TOP) as e:
                    it = dve.snap(e * FT + tb * (TOP * FT))
                    for f in range(FT):
                        dve.wait_ge(hf_ready, it + (f + 1))
                        dve.tensor_copy(HFH[f % 2][:], HF[f % 2][:]).then_inc(hfh_ready, 1)
                        dve.wait_ge(hfh_ready, it + (f + 1))
                        dve.tensor_tensor(HFL[f % 2][:], HF[f % 2][:], HFH[f % 2][:].bitcast(F32),
                                          ALU.subtract).then_inc(hfl_ready, 1)
                        if f == FT - 4 and tb + 1 < B:
                            split_x(tb + 1, e)
                    dve.wait_ge(o_loaded, tb * DMA + DMA)
                    dve.wait_ge(b1_loaded, 2 * TOP * DMA)
                    for t in range(T):
                        w = rwf[:, ds(e, 1), tb * T + t:tb * T + t + 1].rearrange("p e t -> p (e t)")
                        dve.scalar_tensor_tensor(O[:, t, :], b2b[:, ds(e, 1), :].rearrange("p e d -> p (e d)"), w,
                                                 O[:, t, :], ALU.mult, ALU.add).then_inc(ob_ready, 1)
                    dve.wait_ge(down2_done, it + (FT + 2))
                    for t in range(T):
                        w = rwf[:, ds(e, 1), tb * T + t:tb * T + t + 1].rearrange("p e t -> p (e t)")
                        dve.wait_ge(ob_ready, e * T + (tb * (TOP * T) + t + 1))
                        ins = dve.scalar_tensor_tensor(O[:, t, :], PS[t][:], w, O[:, t, :], ALU.mult, ALU.add)
                    ins.then_inc(y2_added, 1)
                    dve.wait_ge(y2_added, e + (tb * TOP + 2))

        @block.tensor
        def _(pe):
            pe.wait_ge(nat_loaded, NAT_LOADS * DMA)
            pe.wait_ge(const_ready, 2)
            for i, (srcs, parts_in, parts, dst) in enumerate(setup):
                if i >= 2:
                    pe.wait_ge(set_c, i - 1)
                if i == 1 + CK:
                    pe.wait_ge(ctx_loaded, DMA)
                if i == 1 + CK + B * CK:
                    pe.wait_ge(small_loaded, SMALL_LOADS * DMA)
                w = dst.shape[1] // len(srcs)
                for k, src in enumerate(srcs):
                    ins = pe.transpose(PS[4 + i % 2][0:parts, k * w:(k + 1) * w], src, ident[0:parts_in, 0:parts_in])
                ins.then_inc(set_t, 1)

            pe.wait_ge(set_c, len(setup))

            def in_proj(b):
                for c in range(DC):
                    for k in range(CK):
                        ins = pe.matmul(PS[c][:], inT[:, k, c * P:(c + 1) * P], ctxT[:, k, ds(b * L, L)],
                                        start=(k == 0), stop=(k == CK - 1))
                    ins.then_inc(xin_ready, 1)

            def four_transposes(src, i, count):
                for k in range(K):
                    ins = pe.transpose(PS[4 + i % 2][:, k * P:(k + 1) * P], src[:, k * P:(k + 1) * P], ident[:])
                ins.then_inc(count, 1)

            def sequence_pe(b, last):
                for w in range(2):
                    for k in range(CK):
                        ins = pe.matmul(PS[6 + w][:], wqkT[:, w, k, :], ctxT[:, k, ds(b * L, L)],
                                        start=(k == 0), stop=(k == CK - 1))
                ins.then_inc(qk_ready, 1)

                def turn_values(t):
                    if t >= 2:
                        pe.wait_ge(t_copied, b * 12 + (t - 1))
                    four_transposes(XN[:, t, :], t, t_ready)

                pe.wait_ge(xn_ready, b + 1)
                turn_values(0)
                turn_values(1)
                pe.wait_ge(qk_copied, b * 2 + 2)
                for t in range(T):
                    if t >= 2:
                        pe.wait_ge(exp_ready, b * T + (t - 1))
                    pe.matmul(PS[6 + t % 2][:], QKT[:, 0, t * P:(t + 1) * P], QKT[:, 1, :],
                              start=True, stop=True).then_inc(e_ready, 1)
                for t in range(2, T):
                    turn_values(t)
                for t in range(T):
                    pe.wait_ge(p_ready, b * T + (t + 1))
                    pe.wait_ge(t_copied, b * 12 + (T + t - 1))
                    four_transposes(PR[:, t, :], t, t_ready)
                pe.wait_ge(t_copied, b * 12 + 2 * T)
                for t in range(T):
                    if t >= 2:
                        pe.wait_ge(x1_ready, b * T + (t - 1))
                    for k in range(K):
                        ins = pe.matmul(PS[6 + t % 2][:], XNT[:, k, t * P:(t + 1) * P], ATT[:, k, :],
                                        start=(k == 0), stop=(k == K - 1))
                    ins.then_inc(o_ready, 1)
                pe.wait_ge(u_ready, b + 1)
                for c in range(DC):
                    ins = pe.matmul(PS[0][0:XD, :], xpT[:, c, :], U[:, c, :], start=(c == 0), stop=(c == DC - 1))
                ins.then_inc(xd_ready, 1)
                pe.wait_ge(xd_copied, b + 1)
                for c in range(DC):
                    pe.matmul(PS[c][:], dtpT[:, c * P:(c + 1) * P], xdb[0:R, :],
                              start=True, stop=True).then_inc(dtp_ready, 1)
                pe.wait_ge(xn1_ready, b + 1)
                for t in range(T):
                    pe.wait_ge(t_copied, b * 12 + (2 * T + t - 1))
                    four_transposes(XN1[:, t, :], t, t_ready)
                pe.wait_ge(t_copied, b * 12 + 3 * T)
                for t in range(T):
                    for k in range(K):
                        ins = pe.matmul(PS[6][:, t * E:(t + 1) * E], XNT[:, k, t * P:(t + 1) * P], routerW[:, k, :],
                                        start=(k == 0), stop=(k == K - 1))
                ins.then_inc(score_ready, 1)
                pe.wait_ge(abs_ready, b * DC + DC)
                if not last:
                    in_proj(b + 1)
                pe.wait_ge(score_copied, b + 1)

            in_proj(0)
            with pe.Fori(0, B - 1) as b:
                sequence_pe(b, False)
            sequence_pe(B - 1, True)

            pe.wait_ge(mask_ready, 1)
            pe.wait_ge(const_ready, 6)
            pe.matmul(PS[4][:, 0:NT * E], tri[:], MM[:].rearrange("p t e -> p (t e)"), start=True, stop=True)
            pe.matmul(PS[5][:, 0:NT * E], ones[:], MM[:].rearrange("p t e -> p (t e)"), start=True,
                      stop=True).then_inc(rank_ready, 1)

            pe.sem_inc(s_summed, SUMMED + LONE // GROUP + S_RING // GROUP)
            pe.sem_inc(xgt_ready, 2)
            pe.sem_inc(up_ready, 2)
            pe.sem_inc(down_ready, 2)

            def add_banks(b, n):
                q, phase = (n - (GROUP - 1)) // GROUP, (n + 1) % GROUP
                if phase == 0:
                    pe.wait_ge(added, (b * (NS // GROUP) + q + S_RING // GROUP + 1) * (GROUP - 1))
                    if q == 0:
                        pe.wait_ge(y_ready, b * DC)
                for c in range(phase * DC // GROUP, (phase + 1) * DC // GROUP):
                    ins = pe.matmul(PS[c][:], ident[:], S[(q * GROUP + GROUP - 1) % S_RING][:, c, :],
                                    start=(q == 0), stop=(q in (-1, NS // GROUP - 1)))
                if phase == GROUP - 1:
                    ins.then_inc(s_summed, 1)

            def turn_x(j0, n):
                xg = XG[n % 2][:].rearrange("p (q k) -> p k q", k=K)
                pe.wait_ge(xg_loaded[n % 2], block_of(j0, DMA) + (n // 2 + 1) * DMA)
                if not (isinstance(j0, int) and j0 + n == 0):
                    pe.wait_ge(xgt_copied, j0 + n)
                for k in range(K):
                    ins = pe.transpose(PS[4][:, k * P:(k + 1) * P], xg[:, k, :], ident[:])
                ins.then_inc(xgt_ready, 1)

            def up(j0, n):
                pe.wait_ge(xgt_copied, j0 + (n + 1))
                pe.wait_ge(gu_loaded[n % 2], block_of(j0, 2 * DMA) + (n // 2 + 1) * 2 * DMA)
                for k in range(K):
                    ins = pe.matmul(PS[5][:, 0:2 * F], XGT[n % 2][:, k, :],
                                    WGU[n % 2][:, k].rearrange("p g f -> p (g f)"), start=(k == 0), stop=(k == K - 1))
                ins.then_inc(up_ready, 1)

            def turn_h(j0, n):
                hh = HH[n % 2][:].rearrange("p (q k) -> p k q", k=2)
                pe.wait_ge(hh_ready, j0 + (n + 1))
                for k in range(2):
                    ins = pe.transpose(PS[6][0:FH, k * P:(k + 1) * P], hh[:, k, :], ident[:])
                ins.then_inc(ht_ready, 1)

            def down(j0, n):
                pe.wait_ge(ht_copied, j0 + (n + 1))
                pe.wait_ge(wd_loaded[n % 2], block_of(j0, DMA) + (n // 2 + 1) * DMA)
                pe.wait_ge(yt_ready, j0 + (n + 1))
                for k in range(2):
                    ins = pe.matmul(PS[7][:], HT[n % 2][:, k, :], WD[n % 2][:, k, :], start=(k == 0), stop=(k == 1))
                ins.then_inc(down_ready, 1)

            def block_of(j0, per):
                return j0 * (per // 2)

            def mixture_steps(b, last):
                j0 = b * NS - NS
                for n in range(NS):
                    turn_h(j0, n)
                    if n + 2 < NS:
                        turn_x(j0, n + 2)
                    elif not last:
                        turn_x(j0 + NS, n + 2 - NS)
                    if n + 1 < NS:
                        up(j0, n + 1)
                    elif not last:
                        up(j0 + NS, 0)
                    down(j0, n)
                    add_banks(b, n)

            for n in range(NS):
                if n < LONE:
                    pe.wait_ge(hc_ready, BC_RING + n + 1)
                    for c in range(DC):
                        ins = pe.matmul(PS[c][:], ident[:], S[n % S_RING][:, c, :], start=(n == 0), stop=False)
                    ins.then_inc(one_summed, 1)
                if n == NS - 5:
                    pe.wait_ge(slots_loaded, DMA)
                    pe.transpose(PS[6][:, 0:SLOT_TILES], slotf[:], ident[0:SLOT_TILES, 0:SLOT_TILES]).then_inc(slots_t, 1)
            pe.wait_ge(slots_ready, 1)
            turn_x(0, 0)
            up(0, 0)
            turn_x(0, 1)
            add_banks(0, NS - 1)
            with pe.Fori(1, B - 1) as b:
                mixture_steps(b, False)
            mixture_steps(B - 1, True)
            for n in range(GROUP - 1):
                add_banks(B, n)

            def turn_gated(b):
                for c in range(DC):
                    pe.wait_ge(gate_ready, b * DC + (c + 1))
                    for t in range(T):
                        ins = pe.transpose(PS[t][:, c * P:(c + 1) * P], ZT[:, c, t * P:(t + 1) * P], ident[:])
                        if c == DC - 1:
                            ins.then_inc(gt_ready, 1)

            def combine_pe(b, ahead):
                if ahead:
                    pe.wait_ge(x3_ready, b * T + T)
                    turn_gated(b + 1)
                for t in range(T):
                    pe.wait_ge(xn3_ready, b * T + (t + 1))
                    if t >= 2:
                        pe.wait_ge(t3_copied, b * T + (t - 1))
                    four_transposes(ZN3[:, t, :], t, t3_ready)
                pe.wait_ge(t3_copied, b * T + T)
                for t in range(T):
                    for k in range(K):
                        ins = pe.matmul(PS[6][:, t * E2:(t + 1) * E2], XT3[:, k, t * P:(t + 1) * P], gate2T[:, k, :],
                                        start=(k == 0), stop=(k == K - 1))
                ins.then_inc(lg_ready, 1)
                pe.wait_ge(lg_copied, b + 1)

            pe.wait_ge(y_ready, B * DC)
            pe.sem_inc(t3_ready, T)
            turn_gated(0)
            with pe.Fori(0, B - 1) as b:
                combine_pe(b, 1)
            combine_pe(B - 1, 0)
            pe.wait_ge(tsum_ready, 1)
            pe.matmul(PS[7][:, 0:E2], ones[:], tsum[:], start=True, stop=True).then_inc(lsum_ready, 1)

            pe.wait_ge(b1_loaded, 2 * TOP * DMA)
            for k in range(TOP):
                ins = pe.transpose(PS[6][:, k * FT:(k + 1) * FT], b1n[:, k, :], ident[0:FT, 0:FT])
            ins.then_inc(b1_t, 1)
            pe.sem_inc(up2_ready, 2)
            pe.sem_inc(down2_done, 2)
            def expert_products(tb, half):
                wait_apart(pe, xs_split, tb * 2 + 2)
                with pe.Fori(0, TOP) as e:
                    it = pe.snap(tb * (TOP * FT) + e * FT)

                    def up(f):
                        pe.wait_ge(w1l_ready, it + (f + 1))
                        for k in range(K):
                            for i, (w, v) in enumerate(((W1H, XSH), (W1H, XSL), (W1L, XSH))):
                                ins = pe.matmul(PS[4 + f % 2][:], w[f % 2][:, k, :], v[half][:, k, :],
                                                start=(k == 0 and i == 0), stop=(k == K - 1 and i == 2))
                        ins.then_inc(up2_ready, 1)

                    def down(f):
                        pe.wait_ge(hfl_ready, it + (f + 1))
                        pe.wait_ge(w2l_ready, it + (f + 1))
                        if f == 0:
                            pe.wait_ge(y2_added, tb * TOP + e + 1)
                        for t in range(T):
                            for i, (u_, w) in enumerate(((HFH, W2H), (HFH, W2L), (HFL, W2H))):
                                ins = pe.matmul(PS[t][:], u_[f % 2][:, t * P:(t + 1) * P], w[f % 2][:],
                                                start=(f == 0 and i == 0), stop=(f == FT - 1 and i == 2))
                        ins.then_inc(down2_done, 1)

                    up(0)
                    for f in range(FT):
                        if f + 1 < FT:
                            up(f + 1)
                        down(f)

            with pe.Fori(0, B // 2) as pair:
                for half in range(2):
                    expert_products(pe.snap(pair * 2 + half), half)


_INS = ['x', 'ctx_1024', 'L0_xattn_Wq', 'L0_xattn_bq', 'L0_xattn_Wk', 'L0_xattn_bk', 'L0_ffn_router_w',
        'L0_ffn_gate_w', 'L0_ffn_up_w', 'L0_ffn_down_w', 'L1_xattn_in_proj_w', 'L1_xattn_conv_w',
        'L1_xattn_conv_b', 'L1_xattn_x_proj_w', 'L1_xattn_dt_proj_w', 'L1_xattn_dt_proj_b', 'L1_xattn_A_log',
        'L1_xattn_D', 'L1_ffn_gate_w', 'L1_ffn_w1', 'L1_ffn_b1', 'L1_ffn_w2', 'L1_ffn_b2']


def kernel(**inputs):
    import numpy as _np
    import concourse.bacc as _bacc
    from concourse import mybir as _mybir
    from concourse.bass_utils import run_bass_kernel_spmd as _run

    nc = _bacc.Bacc("TRN2", target_bir_lowering=False, num_devices=1)
    arrays, args = {}, []
    for name in _INS:
        a = _np.ascontiguousarray(inputs[name])
        arrays[f"in_{name}"] = a
        args.append(nc.dram_tensor(f"in_{name}", a.shape, _mybir.dt.from_np(a.dtype), kind="ExternalInput").ap())
    args.append(nc.dram_tensor("out_x", inputs["x"].shape, _mybir.dt.float32, kind="ExternalOutput").ap())
    build_program(nc, *args)
    r = _run(nc, [arrays], core_ids=[0])
    return r.results[0]["out_x"]
```
